# Optimizing a Trainium2 kernel written in Bass

```python
import numpy as np
import jax
import jax.numpy as jnp

def _softmax(x, axis=-1):
    return jax.nn.softmax(x, axis=axis)

def _gelu(x):
    return jax.nn.gelu(x, approximate=True)

def _silu(x):
    return jax.nn.silu(x)

def _sigmoid(x):
    return jax.nn.sigmoid(x)

def _layernorm(x, axis=-1, eps=1e-05):
    m = jnp.mean(x, axis=axis, keepdims=True)
    v = jnp.var(x, axis=axis, keepdims=True)
    return (x - m) / jnp.sqrt(v + eps)

def _scatter_add(tgt, idx, src, axis=0):
    return tgt.at[idx].add(src)

def _segment_sum(src, seg, n):
    return jax.ops.segment_sum(src, seg, n)
kernel_name = 'mk_adaln_d2_jaxref_r4_7a7f5b'

def setup_inputs(seed: int=0):
    np.random.seed(seed)
    _w = jnp.asarray

    def _L0_attn_setup():
        import jax, jax.numpy as jnp
        import numpy as np
        B, SQ, H = (2, 512, 512)
        NH = 16
        HN = H // NH
        key = jax.random.key(seed)
        ks = jax.random.split(key, 6)
        query = jax.random.normal(ks[0], (B, SQ, H), dtype=jnp.float32)
        k_in = jax.random.normal(ks[1], (B, SQ, H), dtype=jnp.float32)
        v_in = jax.random.normal(ks[2], (B, SQ, H), dtype=jnp.float32)
        Wqkv = jax.random.normal(ks[3], (3 * H, H), dtype=jnp.float32) * (1.0 / np.sqrt(H))
        Wproj = jax.random.normal(ks[4], (H, H), dtype=jnp.float32) * (1.0 / np.sqrt(H))
        bproj = jnp.zeros((H,), dtype=jnp.float32)
        return {'query': query, 'key': k_in, 'value': v_in, 'Wqkv': Wqkv, 'Wproj': Wproj, 'bproj': bproj}
    _L0_attn_in = _L0_attn_setup()

    def _L0_ffn_setup():
        import jax, jax.numpy as jnp
        import numpy as np
        from jax import lax
        DIM = 512
        E = 8
        K = 2
        RANK = 32
        CAP_FACTOR = 1.25

        def gelu(x):
            return jax.nn.gelu(x, approximate=False)

        def _moe_forward(x, gate_w, w1, b1, w2, b2, wd, wu, sw1, sb1, sw2, sb2, swd, swu):
            B, S, D = x.shape
            T = B * S
            cap = max(1, int(T * CAP_FACTOR / E))
            xt = x.reshape(T, D)
            logits = xt @ gate_w
            probs_full = jax.nn.softmax(logits, axis=-1)
            top_p, top_i = lax.top_k(probs_full, K)
            out = jnp.zeros_like(xt)
            for k in range(K):
                e = top_i[:, k]
                w = top_p[:, k]
                onehot = jax.nn.one_hot(e, E, dtype=jnp.int32)
                pos_all = jnp.cumsum(onehot, axis=0) - 1
                pos = jnp.take_along_axis(pos_all, e[:, None], axis=1)[:, 0]
                keep = pos < cap
                pos_c = jnp.where(keep, pos, cap)
                buf = jnp.zeros((E, cap, D), x.dtype).at[e, pos_c].set(xt * keep[:, None].astype(x.dtype), mode='drop')
                h = gelu(jnp.einsum('ecd,edf->ecf', buf, w1) + b1[:, None, :])
                y = jnp.einsum('ecf,efd->ecd', h, w2) + b2[:, None, :]
                a = jnp.einsum('ecr,erd->ecd', gelu(jnp.einsum('ecd,edr->ecr', buf, wd)), wu)
                y = y + a
                tok = y[e, jnp.minimum(pos_c, cap - 1)]
                out = out + tok * keep[:, None].astype(x.dtype) * w[:, None]
            sh = gelu(xt @ sw1 + sb1) @ sw2 + sb2
            sh = sh + gelu(xt @ swd) @ swu
            out = out + 0.2 * sh
            return out.reshape(B, S, D)
        key = jax.random.key(seed)
        ks = jax.random.split(key, 16)
        s = 0.02
        d, h = (DIM, 4 * DIM)
        inp = {'x': jax.random.normal(ks[0], (4, 512, d), dtype=jnp.float32), 'gate_w': jax.random.normal(ks[1], (d, E), dtype=jnp.float32) * s, 'w1': jax.random.normal(ks[2], (E, d, h), dtype=jnp.float32) * s, 'b1': jnp.zeros((E, h), dtype=jnp.float32), 'w2': jax.random.normal(ks[3], (E, h, d), dtype=jnp.float32) * s, 'b2': jnp.zeros((E, d), dtype=jnp.float32), 'wd': jax.random.normal(ks[4], (E, d, RANK), dtype=jnp.float32) * s, 'wu': jax.random.normal(ks[5], (E, RANK, d), dtype=jnp.float32) * s, 'sw1': jax.random.normal(ks[6], (d, h), dtype=jnp.float32) * s, 'sb1': jnp.zeros((h,), dtype=jnp.float32), 'sw2': jax.random.normal(ks[7], (h, d), dtype=jnp.float32) * s, 'sb2': jnp.zeros((d,), dtype=jnp.float32), 'swd': jax.random.normal(ks[8], (d, RANK), dtype=jnp.float32) * s, 'swu': jax.random.normal(ks[9], (RANK, d), dtype=jnp.float32) * s}
        return inp
    _L0_ffn_in = _L0_ffn_setup()
    _L0_c = _w((lambda *s: np.random.randn(*s).astype(np.float32) * 0.05)(4, 512))
    _L0_wmod = _w((lambda *s: np.random.randn(*s).astype(np.float32) * 0.05)(512, 6 * 512) * 512 ** (-0.5))

    def _L1_attn_setup():
        import jax, jax.numpy as jnp
        import numpy as np
        key = jax.random.key(seed)
        B, C, N = (8, 64, 512)
        x = jax.random.normal(key, (B, C, N), dtype=jnp.float32)
        return {'x': x}
    _L1_attn_in = _L1_attn_setup()

    def _L1_ffn_setup():
        import jax, jax.numpy as jnp
        import numpy as np
        H = 512
        I = 352
        E = 8
        K = 2
        B, S = (2, 512)
        key = jax.random.key(seed)
        k0, k1, k2, k3, k4 = jax.random.split(key, 5)
        scale = 1.0 / np.sqrt(H)
        x = jax.random.normal(k0, (B, S, H), dtype=jnp.float32)
        Wr = jax.random.normal(k1, (H, E), dtype=jnp.float32) * scale
        Wg = jax.random.normal(k2, (E, H, I), dtype=jnp.float32) * scale
        Wu = jax.random.normal(k3, (E, H, I), dtype=jnp.float32) * scale
        Wd = jax.random.normal(k4, (E, I, H), dtype=jnp.float32) * (1.0 / np.sqrt(I))
        return {'x': x, 'Wr': Wr, 'Wg': Wg, 'Wu': Wu, 'Wd': Wd}
    _L1_ffn_in = _L1_ffn_setup()
    _L1_c = _w((lambda *s: np.random.randn(*s).astype(np.float32) * 0.05)(4, 512))
    _L1_wmod = _w((lambda *s: np.random.randn(*s).astype(np.float32) * 0.05)(512, 6 * 512) * 512 ** (-0.5))
    _d = {'L0_attn_query': _L0_attn_in['query'], 'L0_attn_key': _L0_attn_in['key'], 'L0_attn_value': _L0_attn_in['value'], 'L0_attn_Wqkv': _L0_attn_in['Wqkv'], 'L0_attn_Wproj': _L0_attn_in['Wproj'], 'L0_attn_bproj': _L0_attn_in['bproj'], 'L0_ffn_gate_w': _L0_ffn_in['gate_w'], 'L0_ffn_w1': _L0_ffn_in['w1'], 'L0_ffn_b1': _L0_ffn_in['b1'], 'L0_ffn_w2': _L0_ffn_in['w2'], 'L0_ffn_b2': _L0_ffn_in['b2'], 'L0_ffn_wd': _L0_ffn_in['wd'], 'L0_ffn_wu': _L0_ffn_in['wu'], 'L0_ffn_sw1': _L0_ffn_in['sw1'], 'L0_ffn_sb1': _L0_ffn_in['sb1'], 'L0_ffn_sw2': _L0_ffn_in['sw2'], 'L0_ffn_sb2': _L0_ffn_in['sb2'], 'L0_ffn_swd': _L0_ffn_in['swd'], 'L0_ffn_swu': _L0_ffn_in['swu'], 'L0_c': _L0_c, 'L0_wmod': _L0_wmod, 'L1_ffn_Wr': _L1_ffn_in['Wr'], 'L1_ffn_Wg': _L1_ffn_in['Wg'], 'L1_ffn_Wu': _L1_ffn_in['Wu'], 'L1_ffn_Wd': _L1_ffn_in['Wd'], 'L1_c': _L1_c, 'L1_wmod': _L1_wmod}
    _x0 = _d['L0_attn_query']
    _d['L0_attn_query'] = jax.random.normal(jax.random.fold_in(jax.random.key(seed), 1), (4, 512, 512), dtype=_x0.dtype)
    del _x0
    return _d

def reference(L0_attn_query, L0_attn_key, L0_attn_value, L0_attn_Wqkv, L0_attn_Wproj, L0_attn_bproj, L0_ffn_gate_w, L0_ffn_w1, L0_ffn_b1, L0_ffn_w2, L0_ffn_b2, L0_ffn_wd, L0_ffn_wu, L0_ffn_sw1, L0_ffn_sb1, L0_ffn_sw2, L0_ffn_sb2, L0_ffn_swd, L0_ffn_swu, L0_c, L0_wmod, L1_ffn_Wr, L1_ffn_Wg, L1_ffn_Wu, L1_ffn_Wd, L1_c, L1_wmod):

    def _L0_attn_ref(query, key, value, Wqkv, Wproj, bproj):
        import jax, jax.numpy as jnp
        import numpy as np
        B, SQ, H = (2, 512, 512)
        NH = 16
        HN = H // NH
        b, sq, h = query.shape
        nh, hn = (NH, HN)
        norm = 1.0 / jnp.sqrt(jnp.asarray(hn, query.dtype))
        x = jnp.transpose(query, (1, 0, 2)).reshape(sq * b, h)
        mixed = x @ Wqkv.T
        mixed = mixed.reshape(sq, b, nh, 3, hn)
        q = mixed[..., 0, :]
        k = mixed[..., 1, :]
        v = mixed[..., 2, :]
        q = q.reshape(sq, b * nh, hn).transpose(1, 0, 2)
        k = k.reshape(sq, b * nh, hn).transpose(1, 0, 2)
        v = v.reshape(sq, b * nh, hn).transpose(1, 0, 2)
        attn = jnp.einsum('gqd,gkd->gqk', q, k) * norm
        attn = jax.nn.softmax(attn, axis=-1)
        ctx = jnp.einsum('gqk,gkd->gqd', attn, v)
        ctx = ctx.reshape(nh, b, sq, hn)
        ctx = jnp.transpose(ctx, (2, 1, 0, 3)).reshape(sq * b, h)
        out = ctx @ Wproj.T + bproj
        out = out.reshape(sq, b, h)
        return jnp.transpose(out, (1, 0, 2))

    def _L0_ffn_ref(x, gate_w, w1, b1, w2, b2, wd, wu, sw1, sb1, sw2, sb2, swd, swu):
        import jax, jax.numpy as jnp
        import numpy as np
        from jax import lax
        DIM = 512
        E = 8
        K = 2
        RANK = 32
        CAP_FACTOR = 1.25

        def gelu(x):
            return jax.nn.gelu(x, approximate=False)

        def _moe_forward(x, gate_w, w1, b1, w2, b2, wd, wu, sw1, sb1, sw2, sb2, swd, swu):
            B, S, D = x.shape
            T = B * S
            cap = max(1, int(T * CAP_FACTOR / E))
            xt = x.reshape(T, D)
            logits = xt @ gate_w
            probs_full = jax.nn.softmax(logits, axis=-1)
            top_p, top_i = lax.top_k(probs_full, K)
            out = jnp.zeros_like(xt)
            for k in range(K):
                e = top_i[:, k]
                w = top_p[:, k]
                onehot = jax.nn.one_hot(e, E, dtype=jnp.int32)
                pos_all = jnp.cumsum(onehot, axis=0) - 1
                pos = jnp.take_along_axis(pos_all, e[:, None], axis=1)[:, 0]
                keep = pos < cap
                pos_c = jnp.where(keep, pos, cap)
                buf = jnp.zeros((E, cap, D), x.dtype).at[e, pos_c].set(xt * keep[:, None].astype(x.dtype), mode='drop')
                h = gelu(jnp.einsum('ecd,edf->ecf', buf, w1) + b1[:, None, :])
                y = jnp.einsum('ecf,efd->ecd', h, w2) + b2[:, None, :]
                a = jnp.einsum('ecr,erd->ecd', gelu(jnp.einsum('ecd,edr->ecr', buf, wd)), wu)
                y = y + a
                tok = y[e, jnp.minimum(pos_c, cap - 1)]
                out = out + tok * keep[:, None].astype(x.dtype) * w[:, None]
            sh = gelu(xt @ sw1 + sb1) @ sw2 + sb2
            sh = sh + gelu(xt @ swd) @ swu
            out = out + 0.2 * sh
            return out.reshape(B, S, D)
        return _moe_forward(x, gate_w, w1, b1, w2, b2, wd, wu, sw1, sb1, sw2, sb2, swd, swu)

    def _L1_attn_ref(x):
        import jax, jax.numpy as jnp
        import numpy as np
        scores = jnp.einsum('bci,bcj->bij', x, x)
        weights = jax.nn.softmax(scores, axis=-1)
        context = jnp.einsum('bij,bcj->bci', weights, x)
        return context

    def _L1_ffn_ref(x, Wr, Wg, Wu, Wd):
        import jax, jax.numpy as jnp
        import numpy as np
        H = 512
        I = 352
        E = 8
        K = 2
        B, S = (2, 512)
        router_logits = jnp.einsum('bsh,he->bse', x, Wr)
        probs = jax.nn.softmax(router_logits.astype(jnp.float32), axis=-1)
        topk_w, topk_idx = jax.lax.top_k(probs, K)
        topk_w = topk_w / jnp.sum(topk_w, axis=-1, keepdims=True)
        onehot = jax.nn.one_hot(topk_idx, E, dtype=topk_w.dtype)
        combine = jnp.einsum('bsk,bske->bse', topk_w, onehot)
        g = jnp.einsum('bsh,ehi->besi', x, Wg)
        u = jnp.einsum('bsh,ehi->besi', x, Wu)
        h = jax.nn.silu(g) * u
        y = jnp.einsum('besi,eih->besh', h, Wd)
        out = jnp.einsum('bse,besh->bsh', combine.astype(x.dtype), y)
        return out
    x = L0_attn_query
    mod = (_silu(L0_c) @ L0_wmod).reshape(L0_c.shape[0], 6, 1, -1)
    sa, ca, ga, sb, cb, gb = (mod[:, 0], mod[:, 1], mod[:, 2], mod[:, 3], mod[:, 4], mod[:, 5])
    ga = (2 * (ga >= 0) - 1) * jnp.maximum(jnp.abs(ga), 0.25)
    gb = (2 * (gb >= 0) - 1) * jnp.maximum(jnp.abs(gb), 0.25)
    h = _layernorm(x, axis=-1) * (1 + ca) + sa
    x = x + ga * _L0_attn_ref(h, L0_attn_key, L0_attn_value, L0_attn_Wqkv, L0_attn_Wproj, L0_attn_bproj)
    h = _layernorm(x, axis=-1) * (1 + cb) + sb
    x = x + gb * _L0_ffn_ref(h, L0_ffn_gate_w, L0_ffn_w1, L0_ffn_b1, L0_ffn_w2, L0_ffn_b2, L0_ffn_wd, L0_ffn_wu, L0_ffn_sw1, L0_ffn_sb1, L0_ffn_sw2, L0_ffn_sb2, L0_ffn_swd, L0_ffn_swu)
    mod = (_silu(L1_c) @ L1_wmod).reshape(L1_c.shape[0], 6, 1, -1)
    sa, ca, ga, sb, cb, gb = (mod[:, 0], mod[:, 1], mod[:, 2], mod[:, 3], mod[:, 4], mod[:, 5])
    ga = (2 * (ga >= 0) - 1) * jnp.maximum(jnp.abs(ga), 0.25)
    gb = (2 * (gb >= 0) - 1) * jnp.maximum(jnp.abs(gb), 0.25)
    h = _layernorm(x, axis=-1) * (1 + ca) + sa
    x = x + ga * _L1_attn_ref(h)
    h = _layernorm(x, axis=-1) * (1 + cb) + sb
    x = x + gb * _L1_ffn_ref(h, L1_ffn_Wr, L1_ffn_Wg, L1_ffn_Wu, L1_ffn_Wd)
    return x

_drawn_inputs = setup_inputs


def setup_inputs(seed=0):
    import zlib

    import numpy as np

    out = dict(_drawn_inputs(seed))
    spreads = {'L0_attn_bproj': (0.0, 0.286),
     'L0_ffn_b1': (0.0, 0.8),
     'L0_ffn_b2': (0.0, 0.72),
     'L0_ffn_sb1': (0.0, 0.8),
     'L0_ffn_sb2': (0.0, 0.8)}
    factors = {'L0_ffn_gate_w': 3.134,
     'L0_ffn_w1': 3.09,
     'L0_ffn_w2': 2.91,
     'L0_ffn_wd': 8.0,
     'L0_ffn_wu': 8.0,
     'L0_ffn_sw1': 4.012,
     'L0_ffn_sw2': 3.821,
     'L0_ffn_swd': 8.0,
     'L0_ffn_swu': 8.0}
    for name, (base, spread) in spreads.items():
        noise = np.random.default_rng([zlib.crc32(name.encode()), seed]).standard_normal(out[name].shape)
        drawn = base * np.exp(spread * noise) if base else spread * noise
        out[name] = jnp.asarray(drawn.astype(out[name].dtype))
    for name, factor in factors.items():
        out[name] = (out[name] * factor).astype(out[name].dtype)
    return out
```

```python
from contextlib import ExitStack

import concourse.bass as bass
from concourse import mybir

F32 = mybir.dt.float32
F32R = mybir.dt.float32r
I32 = mybir.dt.int32
U32 = mybir.dt.uint32
ALU = mybir.AluOpType
ACT = mybir.ActivationFunctionType
AX = mybir.AxisListType

P = 128
B, S, D = 4, 512, 512
T = B * S
NT = T // P
TB = S // P
KC = D // P
HEADS, HN = 16, 32
QUADS = 4
E = 8
F = 2048
FC = F // P
RANK = 32
CAP = 320
REGION = 2 * CAP
ROWS = T + E * REGION
INNER = 352
TILES1 = 40
EPS = 1e-5
SA, CA, GA, SB_, CB, GB = range(6)


def flat(ap):
    return ap.rearrange("p a d -> p (a d)")


def tile_of(buf, index):
    if isinstance(index, int):
        return buf[:, index, :]
    return flat(buf[:, bass.ds(index, 1), :])


def batch_loop(eng, body):
    with eng.Fori(0, B - 1) as b:
        body(b, False)
    body(B - 1, True)


def wait_alone(eng, sem, value, passed):
    eng.wait_ge(sem, value)
    eng.sem_inc(passed, 1)


class Core:

    def __init__(self, nc, stack, ins, out):
        self.nc, self.stack, self.ins, self.out, self.sems = nc, stack, ins, out, {}
        self.x = self.sb("x_resid", [P, NT, D])
        self.ident = self.sb("ident", [P, P])
        self.passed = self.sem("waits_passed")
        self.eps = self.sb("eps", [P, 1])
        self.mod_rows = nc.dram_tensor("mod_rows", (2, 6, B, D), F32, kind="Internal").ap()
        self.dispatch = nc.dram_tensor("dispatch0", (ROWS, D), F32, kind="Internal").ap()
        self.expert_out = nc.dram_tensor("expert_out0", (ROWS, D), F32, kind="Internal").ap()
        self.dispatch1 = nc.dram_tensor("dispatch1", (TILES1 * P, D), F32, kind="Internal").ap()
        self.h_rows1 = nc.dram_tensor("h_rows1", (T, D), F32, kind="Internal").ap()
        self.expert_out1 = nc.dram_tensor("expert_out1", (TILES1 * P, D), F32, kind="Internal").ap()

    def sb(self, name, shape, dtype=F32, stack=None):
        return (stack or self.stack).enter_context(self.nc.sbuf_tensor(name, shape, dtype))

    def ps(self, name, shape, stack):
        return stack.enter_context(self.nc.psum_tensor(name, shape, F32))

    def sem(self, name):
        if name not in self.sems:
            self.sems[name] = self.stack.enter_context(self.nc.semaphore(name))
        return self.sems[name]

    def mod_tile(self, layer, which, batch):
        row = self.mod_rows[layer, which]
        row = row[batch:batch + 1, :] if isinstance(batch, int) else row[bass.ds(batch, 1), :]
        return row.broadcast_to([P, D])


def start_and_modulation(k, att):
    RING = 6
    nc, ins = k.nc, k.ins
    x_loaded, c_loaded, att_w_loaded = k.sem("x_loaded"), k.sem("c_loaded"), k.sem("att_w_loaded")
    wmod_loaded = [k.sem(f"wmod_loaded{n}") for n in range(RING)]
    silu_done, rows_ready, rows_done, rows_stored = (
        k.sem("silu_done"), k.sem("mod_psum_ready"), k.sem("mod_rows_done"), k.sem("mod_rows_stored"))
    half_step = k.sem("mod_half_step")
    zero_done, zero_stored = k.sem("zero_done"), k.sem("zero_stored")
    ident_zeroed, consts_done = k.sem("ident_zeroed"), k.sem("consts_done")
    stats_done, var_done, sd_done, rstd_done = k.sem("stats_done"), k.sem("var_done"), k.sem("sd_done"), k.sem("rstd_done")
    with ExitStack() as st:
        wm = k.sb("wmod_sb", [P, RING, KC * D], stack=st)
        ct = k.sb("c_t", [P, 2, KC, B], stack=st)
        ct_silu = k.sb("c_t_silu", [P, 2, KC, B], stack=st)
        rows = k.sb("mod_rows_sb", [P, 4, D], stack=st)
        sign = k.sb("gate_sign", [P, 4, D], stack=st)
        zeros = k.sb("zero_rows", [P, 4 * D], stack=st)
        stats = k.sb("ln1_stats", [P, NT, 6], stack=st)
        sd = k.sb("ln1_sd", [P, NT], stack=st)
        pm = k.ps("mod_psum", [P, 4, D], st)

        def place(n):
            layer, which = divmod(n, 6)
            return 32 * (which % 4), 2 * layer + which // 4

        with nc.Block() as block:
            @block.sync
            def _(sp):
                sp.dma_start(ct[:, :, :, :], ins["c_t"]).then_inc(c_loaded, 16)
                for t in range(0, NT, TB):
                    sp.dma_start(k.x[:, t:t + TB, :],
                                 ins["x"][t * P:(t + TB) * P, :].rearrange("(t p) d -> p t d", p=P)
                                 ).then_inc(x_loaded, 16)
                for n in range(12):
                    if n >= RING:
                        sp.wait_ge(rows_ready, n - RING + 1)
                    sp.dma_start(wm[:, n % RING, :], ins["wmod"][n]).then_inc(wmod_loaded[n % RING], 16)
                for n in range(12):
                    q, bank = place(n)
                    sp.wait_ge(rows_done, n + 1)
                    sp.dma_start(k.mod_rows[n // 6, n % 6], rows[q:q + B, bank, :]).then_inc(rows_stored, 16)
                sp.wait_ge(rows_stored, 16 * 12)

            @block.scalar
            def _(act):
                act.dma_start(att.wqk[:, :, :, :], ins["wqk"]).then_inc(att_w_loaded, 16)
                act.dma_start(att.wv[:, :, :], ins["wv"]).then_inc(att_w_loaded, 16)
                act.wait_ge(c_loaded, 16)
                act.activation(ct_silu[:, :, :, :], ct[:, :, :, :], ACT.Silu).then_inc(silu_done, 1)
                act.wait_ge(zero_done, 1)
                for buf in (k.dispatch[T:, :], k.dispatch1):
                    for r in range(0, buf.shape[0], 4 * P):
                        act.dma_start(buf[r:r + 4 * P, :].rearrange("(p a) d -> p (a d)", p=P),
                                      zeros[:, :]).then_inc(zero_stored, 16)
                act.wait_ge(var_done, NT)
                act.activation(sd[:, :], att.mean_var[:, :, 1], ACT.Sqrt, bias=k.eps[:, 0:1]).then_inc(sd_done, 1)
                act.wait_ge(zero_stored, 16 * (E * REGION + TILES1 * P) // (4 * P))
                act.wait_ge(att_w_loaded, 32)

            @block.gpsimd
            def _(pool):
                pool.memset(zeros[:, :], 0.0).then_inc(zero_done, 1)
                pool.memset(k.ident[:, :], 0.0).then_inc(ident_zeroed, 1)
                pool.wait_ge(ident_zeroed, 1)
                pool.affine_select(out=k.ident[:, :], in_=k.ident[:, :], compare_op=ALU.not_equal, fill=1.0,
                                   base=0, pattern=[[-1, P]], channel_multiplier=1).then_inc(consts_done, 1)

            @block.tensor
            def _(pe):
                pe.wait_ge(silu_done, 1)
                for n in range(12):
                    q, bank = place(n)
                    pe.wait_ge(wmod_loaded[n % RING], 16 * (n // RING + 1))
                    for c in range(KC):
                        mm = pe.matmul(pm[q:q + B, bank, :], ct_silu[:, n // 6, c, :],
                                       wm[:, n % RING, c * D:(c + 1) * D], start=(c == 0), stop=(c == KC - 1))
                    mm.then_inc(rows_ready, 1)

            @block.vector
            def _(dve):
                dve.memset(k.eps[:, :], EPS)
                for t in range(NT):
                    dve.wait_ge(x_loaded, 16 * B)
                    dve.bn_stats(stats[:, t, :], k.x[:, t, :]).then_inc(stats_done, 1)
                for t in range(NT):
                    dve.wait_ge(stats_done, t + 1)
                    dve.bn_aggr(att.mean_var[:, t, :], stats[:, t, :]).then_inc(var_done, 1)
                dve.wait_ge(sd_done, 1)
                dve.reciprocal(att.rstd[:, :], sd[:, :]).then_inc(rstd_done, 1)
                dve.wait_ge(rstd_done, 1)
                dve.scalar_tensor_tensor(out=att.shift[:, :], in0=att.mean_var[:, :, 0], scalar=-1.0,
                                         in1=att.rstd[:, :], op0=ALU.mult, op1=ALU.mult)
                halves = 0
                for n in range(12):
                    q, bank = place(n)
                    src, dst, sg = pm[q:q + B, bank, :], rows[q:q + B, bank, :], sign[q:q + B, bank, :]
                    dve.wait_ge(rows_ready, n + 1)
                    if n % 6 in (CA, CB):
                        dve.tensor_scalar(dst, src, 1.0, None, ALU.add).then_inc(rows_done, 1)
                    elif n % 6 in (SA, SB_):
                        dve.tensor_copy(dst, src).then_inc(rows_done, 1)
                    else:
                        dve.tensor_scalar(sg, src, 0.0, 2.0, ALU.is_ge, ALU.mult).then_inc(half_step, 1)
                        dve.wait_ge(half_step, halves + 1)
                        dve.tensor_scalar(sg, sg, -1.0, None, ALU.add).then_inc(half_step, 1)
                        dve.wait_ge(half_step, halves + 2)
                        dve.tensor_tensor(dst, src, sg, ALU.mult).then_inc(half_step, 1)
                        halves += 3
                        dve.wait_ge(half_step, halves)
                        dve.scalar_tensor_tensor(out=dst, in0=dst, scalar=0.25, in1=sg, op0=ALU.max,
                                                 op1=ALU.mult).then_inc(rows_done, 1)


class Attention0:

    def __init__(self, k, st):
        self.wqk = k.sb("wqk_sb", [P, 2, KC, D], stack=st)
        self.wv = k.sb("wv_sb", [P, KC, D], stack=st)
        self.mean_var = k.sb("ln1_mean_var", [P, NT, 2], stack=st)
        self.rstd = k.sb("ln1_rstd", [P, NT], stack=st)
        self.shift = k.sb("ln1_shift", [P, NT], stack=st)


def attention0(k, att, ctx_t):
    nc, ins = k.nc, k.ins
    NORM = float(HN) ** -0.5
    mod_loaded = k.sem("a0_mod_loaded")
    n_centered, n_scaled, h_ready = k.sem("a0_centered"), k.sem("a0_scaled"), k.sem("a0_h_ready")
    transposed = k.sem("a0_h_transposed")
    gen_full = [k.sem(f"a0_gen_full{i}") for i in range(2)]
    gen_free = [k.sem(f"a0_gen_free{i}") for i in range(2)]
    hi_done = k.sem("a0_hi_done")
    scores_full, max_done = k.sem("a0_scores_full"), k.sem("a0_max_done")
    row_full, row_taken = k.sem("a0_max_row_full"), k.sem("a0_max_row_taken")
    st_full, p_ready = k.sem("a0_st_full"), k.sem("a0_p_ready")
    pv_done, ctx_taken, recip_done, ctx_done = (
        k.sem("a0_pv_done"), k.sem("a0_ctx_taken"), k.sem("a0_recip_done"), k.sem("a0_ctx_done"))
    consts = k.sem("a0_consts")

    uses = [("hT", c) for c in range(KC)] + [("q", 0), ("k", 0)] + [("v", t) for t in range(TB)]
    for j in range(QUADS):
        if j + 1 < QUADS:
            uses += [("q", j + 1), ("k", j + 1)]
    G = {u: n for n, u in enumerate(uses)}
    GH = len(uses) // 2
    assert len(uses) % 2 == 0

    with ExitStack() as st:
        mod = k.sb("a0_mod", [P, 2, D], stack=st)
        h = k.sb("a0_h", [P, TB, D], stack=st)
        h_t = k.sb("a0_h_t", [P, KC, S], stack=st)
        v = k.sb("a0_v", [P, TB, D], stack=st)
        qs = k.sb("a0_q_stack", [P, 2, 4, S], F32R, stack=st)
        ks = k.sb("a0_k_stack", [P, 2, 4, S], F32R, stack=st)
        mx = k.sb("a0_max", [P, 16], stack=st)
        prob = k.sb("a0_prob", [P, 8, S], stack=st)
        ones = k.sb("a0_ones", [P, HN], stack=st)
        rec = k.sb("a0_rec", [P, S], stack=st)
        ctx_raw = k.sb("a0_ctx_raw", [P, S], stack=st)
        den_raw = k.sb("a0_den_raw", [P, S], stack=st)
        gen = k.ps("a0_gen", [P, 2, S], st)
        sc = k.ps("a0_scores", [P, 2, S], st)
        scT = k.ps("a0_scores_t", [P, 2, S], st)
        ctx = k.ps("a0_ctx", [P, S], st)
        den = k.ps("a0_den", [P, S], st)

        def wait_full(eng, b, use):
            eng.wait_ge(gen_full[G[use] % 2], b * GH + G[use] // 2 + 1)

        def wait_freed(pe, b, use):
            pe.wait_ge(gen_free[G[use] % 2], b * GH + G[use] // 2)

        def wait_taken(eng, b, use):
            eng.wait_ge(gen_free[G[use] % 2], b * GH + G[use] // 2 + 1)

        with nc.Block() as block:
            @block.sync
            def _(sp):
                with sp.Fori(0, B) as b:
                    sp.wait_ge(h_ready, TB * b)
                    sp.dma_start(mod[:, 0, :], k.mod_tile(0, CA, b)).then_inc(mod_loaded, 16)
                    sp.dma_start(mod[:, 1, :], k.mod_tile(0, SA, b)).then_inc(mod_loaded, 16)

            @block.gpsimd
            def _(pool):
                with pool.Fori(0, B) as b:
                    pool.wait_ge(mod_loaded, 32 * b + 32)
                    for i in range(TB):
                        pool.wait_ge(n_centered, TB * b + i + 1)
                        pool.tensor_tensor(h[:, i, :], h[:, i, :], mod[:, 0, :], ALU.mult).then_inc(n_scaled, 1)
                    for i in range(TB):
                        pool.wait_ge(n_scaled, TB * b + i + 1)
                        pool.tensor_tensor(h[:, i, :], h[:, i, :], mod[:, 1, :], ALU.add).then_inc(h_ready, 1)

            @block.tensor
            def _(pe):
                with pe.Fori(0, B) as b:
                    def project(which, j, chunks):
                        n, g = (0 if which == "q" else 1), G[(which, j)]
                        if 0 in chunks:
                            wait_freed(pe, b, (which, j))
                        for c in chunks:
                            mm = pe.matmul(gen[:, g % 2, :], att.wqk[:, n, c, j * P:(j + 1) * P], h_t[:, c, :],
                                           start=(c == 0), stop=(c == KC - 1))
                        if KC - 1 in chunks:
                            mm.then_inc(gen_full[g % 2], 1)

                    pe.wait_ge(h_ready, TB * b + TB)
                    for c in range(KC):
                        wait_freed(pe, b, ("hT", c))
                        for i in range(TB):
                            mm = pe.transpose(gen[:, G[("hT", c)] % 2, i * P:(i + 1) * P],
                                              h[:, i, c * P:(c + 1) * P], k.ident[:, :])
                        mm.then_inc(gen_full[G[("hT", c)] % 2], 1)
                    wait_taken(pe, b, ("hT", KC - 2))
                    wait_taken(pe, b, ("hT", KC - 1))
                    project("q", 0, range(KC))
                    project("k", 0, range(KC))
                    for t in range(TB):
                        g = G[("v", t)]
                        wait_freed(pe, b, ("v", t))
                        for c in range(KC):
                            mm = pe.matmul(gen[:, g % 2, :], h_t[:, c, t * P:(t + 1) * P], att.wv[:, c, :],
                                           start=(c == 0), stop=(c == KC - 1))
                        mm.then_inc(gen_full[g % 2], 1)
                    for j in range(QUADS):
                        par = j % 2
                        wait_taken(pe, b, ("q", j))
                        wait_taken(pe, b, ("k", j))
                        for a in range(4):
                            for t in range(TB):
                                s = 16 * j + 4 * a + t
                                pe.wait_ge(max_done, 64 * b + max(s - 1, 0))
                                if a == 0 and t < 2:
                                    pe.wait_ge(row_taken, 16 * b + 4 * j)
                                pe.matmul(sc[:, s % 2, :], qs[0:96, par, a, t * P:(t + 1) * P], ks[0:96, par, a, :],
                                          start=True, stop=True).then_inc(scores_full, 1)
                                if t % 2 and j + 1 < QUADS:
                                    project("q" if a < 2 else "k", j + 1, [2 * (a % 2) + t // 2])
                        for a in range(4):
                            pe.wait_ge(max_done, 64 * b + 16 * (j + 1))
                            pe.wait_ge(row_taken, 16 * b + 4 * j + max(a - 1, 0))
                            for t in range(TB):
                                mm = pe.transpose(sc[0:1, a % 2, t * P:(t + 1) * P],
                                                  mx[:, 4 * a + t:4 * a + t + 1], k.ident[:, :])
                            mm.then_inc(row_full, 1)

                        def score_t(t, a):
                            s = 16 * j + 4 * t + a
                            if t == 0:
                                pe.wait_ge(row_taken, 16 * b + 4 * j + a + 1)
                            pe.wait_ge(p_ready, 64 * b + max(s - 1, 0))
                            pe.matmul(scT[:, s % 2, :], ks[:, par, a, t * P:(t + 1) * P], qs[:, par, a, :],
                                      start=True, stop=True).then_inc(st_full, 1)

                        def weigh(t, to):
                            if to is ctx:
                                pe.wait_ge(p_ready, 64 * b + 16 * j + 4 * t + 4)
                                if t == 0:
                                    pe.wait_ge(ctx_taken, 8 * b + 2 * j)
                            for a in range(4):
                                w = v[:, t, j * P + HN * a:j * P + HN * (a + 1)] if to is ctx else ones[:, :]
                                mm = pe.matmul(to[HN * a:HN * (a + 1), :], w, prob[:, 4 * (t % 2) + a, :],
                                               start=(t == 0), stop=(t == TB - 1))
                            mm.then_inc(pv_done, 1)

                        for t in range(TB + 1):
                            for a, to in ((0, ctx), (2, den)):
                                if t < TB:
                                    score_t(t, a)
                                    score_t(t, a + 1)
                                if t > 0:
                                    weigh(t - 1, to)

            @block.scalar
            def _(act):
                def center(b):
                    wait_alone(act, transposed, b, k.passed)
                    for i in range(TB):
                        act.activation(h[:, i, :], tile_of(k.x, b * TB + i), ACT.Identity,
                                       scale=att.rstd[:, bass.ds(b * TB + i, 1)],
                                       bias=att.shift[:, bass.ds(b * TB + i, 1)]).then_inc(n_centered, 1)

                def body(b, last):
                    for c in (1, 3):
                        wait_full(act, b, ("hT", c))
                        act.copy(h_t[:, c, :], gen[:, G[("hT", c)] % 2, :]).then_inc(gen_free[G[("hT", c)] % 2], 1)
                    def split_hi(which, j):
                        stack = qs if which == "q" else ks
                        wait_full(act, b, (which, j))
                        act.wait_ge(st_full, 64 * b + 16 * max(j - 1, 0))
                        for a in range(4):
                            act.activation(stack[0:HN, j % 2, a, :],
                                           gen[HN * a:HN * (a + 1), G[(which, j)] % 2, :],
                                           ACT.Copy).then_inc(hi_done, 1)

                    split_hi("q", 0)
                    split_hi("k", 0)
                    act.wait_ge(pv_done, 32 * b)
                    for t in (1, 3):
                        wait_full(act, b, ("v", t))
                        act.copy(v[:, t, :], gen[:, G[("v", t)] % 2, :]).then_inc(gen_free[G[("v", t)] % 2], 1)

                    for j in range(QUADS):
                        if j + 1 < QUADS:
                            split_hi("q", j + 1)
                        if j == 1 and not last:
                            center(b + 1)
                        for a in range(4):
                            act.wait_ge(row_full, 16 * b + 4 * j + a + 1)
                            act.activation(qs[96:97, j % 2, a, :], sc[0:1, a % 2, :], ACT.Copy,
                                           scale=-1.0).then_inc(row_taken, 1)
                        for t in range(TB):
                            for a in range(4):
                                s = 16 * j + 4 * t + a
                                act.wait_ge(st_full, 64 * b + s + 1)
                                act.wait_ge(pv_done, 32 * b + 2 * max(4 * j + t - 1, 0))
                                act.activation(prob[:, 4 * (t % 2) + a, :], scT[:, s % 2, :], ACT.Exp,
                                               scale=NORM).then_inc(p_ready, 1)
                            if t == 0 and j + 1 < QUADS:
                                split_hi("k", j + 1)
                        act.wait_ge(pv_done, 32 * b + 8 * j + 8)
                        act.wait_ge(ctx_done, 4 * b + j)
                        act.copy(den_raw[:, :], den[:, :]).then_inc(ctx_taken, 1)
                        act.copy(ctx_raw[:, :], ctx[:, :]).then_inc(ctx_taken, 1)

                center(0)
                batch_loop(act, body)

            @block.vector
            def _(dve):
                dve.memset(ones[:, :], 1.0).then_inc(consts, 1)
                dve.memset(qs[96:128, :, :, :].bitcast(F32), 0.0).then_inc(consts, 1)
                dve.memset(ks[96:128, :, :, :].bitcast(F32), 0.0).then_inc(consts, 1)
                dve.wait_ge(consts, 3)
                dve.memset(ks[96:97, :, :, :].bitcast(F32), 1.0).then_inc(consts, 1)
                dve.wait_ge(consts, 4)
                with dve.Fori(0, B) as b:
                    for c in (0, 2):
                        wait_full(dve, b, ("hT", c))
                        dve.tensor_copy(h_t[:, c, :], gen[:, G[("hT", c)] % 2, :]
                                        ).then_inc(gen_free[G[("hT", c)] % 2], 1)
                    wait_full(dve, b, ("hT", 3))
                    dve.nop().then_inc(transposed, 1)
                    def split_lo(which, j):
                        stack, lo, dup = (qs, HN, 2 * HN) if which == "q" else (ks, 2 * HN, HN)
                        g = G[(which, j)]
                        dve.wait_ge(st_full, 64 * b + 16 * max(j - 1, 0))
                        for a in range(4):
                            dve.wait_ge(hi_done, 32 * b + 8 * j + 4 * (which == "k") + a + 1)
                            dve.tensor_copy(stack[dup:dup + HN, j % 2, a, :], stack[0:HN, j % 2, a, :].bitcast(F32))
                            last = dve.tensor_tensor(stack[lo:lo + HN, j % 2, a, :],
                                                     gen[HN * a:HN * (a + 1), g % 2, :],
                                                     stack[0:HN, j % 2, a, :].bitcast(F32), ALU.subtract)
                        last.then_inc(gen_free[g % 2], 1)

                    def normalize(j):
                        dve.wait_ge(ctx_taken, 8 * b + 2 * j + 2)
                        dve.reciprocal(rec[:, :], den_raw[:, :]).then_inc(recip_done, 1)
                        dve.wait_ge(recip_done, 4 * b + j + 1)
                        dve.tensor_tensor(flat(ctx_t[:, j, bass.ds(b, 1), :]), ctx_raw[:, :], rec[:, :],
                                          ALU.mult).then_inc(ctx_done, 1)

                    split_lo("q", 0)
                    split_lo("k", 0)
                    dve.wait_ge(pv_done, 32 * b)
                    for t in (0, 2):
                        wait_full(dve, b, ("v", t))
                        dve.tensor_copy(v[:, t, :], gen[:, G[("v", t)] % 2, :]).then_inc(gen_free[G[("v", t)] % 2], 1)

                    for j in range(QUADS):
                        for s in range(16):
                            dve.wait_ge(scores_full, 64 * b + 16 * j + s + 1)
                            dve.tensor_reduce(mx[:, s:s + 1], sc[:, s % 2, :], AX.X, ALU.max).then_inc(max_done, 1)
                        if j + 1 < QUADS:
                            split_lo("q", j + 1)
                            split_lo("k", j + 1)
                        if j > 0:
                            normalize(j - 1)
                    normalize(QUADS - 1)


class NormPass:

    def __init__(self, k, st, name, *which, sems, before=0):
        self.k, self.which, self.before = k, which, before
        self.mod_loaded = k.sem(f"{name}_mod_loaded")
        self.mod = k.sb(f"{name}_mod", [P, len(which), B, D], stack=st)
        self.delta = k.sb(f"{name}_delta", [P, TB, D], stack=st)
        self.delta_ready, self.gated, self.added = (k.sem(f"{sems}_{s}") for s in ("delta_ready", "gated", "added"))
        if len(which) == 1:
            return
        self.h = k.sb(f"{name}_h", [P, TB, D], stack=st)
        self.stats = k.sb(f"{name}_stats", [P, TB, 6], stack=st)
        self.mean_var = k.sb(f"{name}_mean_var", [P, TB, 2], stack=st)
        self.sd = k.sb(f"{name}_sd", [P, TB], stack=st)
        self.rstd = k.sb(f"{name}_rstd", [P, TB], stack=st)
        self.stats_done, self.var_done, self.sd_done, self.rstd_done, self.centered, self.scaled, self.h_ready = (
            k.sem(f"{sems}_{s}") for s in ("stats_done", "var_done", "sd_done", "rstd_done", "centered", "scaled", "h_ready"))

    def count(self, b, tiles=0):
        return TB * (self.before + b) + tiles

    def load(self, eng):
        for n, (layer, which) in enumerate(self.which):
            for b in range(B):
                eng.dma_start(self.mod[:, n, b, :], self.k.mod_tile(layer, which, b)).then_inc(self.mod_loaded, 16)

    def mod_of(self, n, b):
        return self.mod[:, n, b, :] if isinstance(b, int) else flat(self.mod[:, n, bass.ds(b, 1), :])

    def gate(self, pool, b):
        pool.wait_ge(self.mod_loaded, 16 * len(self.which) * B)
        for i in range(TB):
            wait_alone(pool, self.delta_ready, self.count(b, i + 1), self.k.passed)
            pool.tensor_tensor(self.delta[:, i, :], self.delta[:, i, :], self.mod_of(0, b),
                               ALU.mult).then_inc(self.gated, 1)

    def add(self, dve, b):
        for i in range(TB):
            x = tile_of(self.k.x, b * TB + i)
            dve.wait_ge(self.gated, self.count(b, i + 1))
            dve.tensor_tensor(x, x, self.delta[:, i, :], ALU.add).then_inc(self.added, 1)

    def statistics(self, dve, b):
        wait_alone(dve, self.added, self.count(b, TB), self.k.passed)
        for i in range(TB):
            dve.bn_stats(self.stats[:, i, :], tile_of(self.k.x, b * TB + i)).then_inc(self.stats_done, 1)
        wait_alone(dve, self.stats_done, self.count(b, TB), self.k.passed)
        for i in range(TB):
            dve.bn_aggr(self.mean_var[:, i, :], self.stats[:, i, :]).then_inc(self.var_done, 1)

    def root(self, act, b):
        act.wait_ge(self.var_done, self.count(b, TB))
        act.activation(self.sd[:, :], self.mean_var[:, :, 1], ACT.Sqrt, bias=self.k.eps[:, 0:1]).then_inc(self.sd_done, 1)

    def center(self, dve, b):
        dve.wait_ge(self.sd_done, self.before + b + 1)
        dve.reciprocal(self.rstd[:, :], self.sd[:, :]).then_inc(self.rstd_done, 1)
        dve.wait_ge(self.rstd_done, self.before + b + 1)
        for i in range(TB):
            dve.tensor_scalar(self.h[:, i, :], tile_of(self.k.x, b * TB + i), self.mean_var[:, i, 0:1],
                              self.rstd[:, i:i + 1], ALU.subtract, ALU.mult).then_inc(self.centered, 1)

    def scale(self, pool, b):
        for i in range(TB):
            wait_alone(pool, self.centered, self.count(b, i + 1), self.k.passed)
            pool.tensor_tensor(self.h[:, i, :], self.h[:, i, :], self.mod_of(1, b), ALU.mult).then_inc(self.scaled, 1)

    def shift(self, dve, b):
        for i in range(TB):
            dve.wait_ge(self.scaled, self.count(b, i + 1))
            dve.tensor_tensor(self.h[:, i, :], self.h[:, i, :], self.mod_of(2, b), ALU.add).then_inc(self.h_ready, 1)


class RouterPass:

    def __init__(self, k, st, name, w_name, norm, logits, before=0):
        self.k, self.norm, self.logits, self.w_name, self.before = k, norm, logits, w_name, before
        self.w_loaded = k.sem(f"{name}_w_loaded")
        self.w = k.sb(f"{name}_w", [P, KC, E], stack=st)
        self.h_t = k.sb(f"{name}_h_t", [P, 2, KC, P], stack=st)
        self.t_psum = k.ps(f"{name}_t_psum", [P, 2, KC, P], st)
        self.l_psum = k.ps(f"{name}_l_psum", [P, TB, E], st)
        self.t_full, self.t_taken, self.tile_routed, self.logits_taken = (
            k.sem("router_t_full"), k.sem("router_t_taken"), k.sem("router_tile_routed"), k.sem("router_logits_taken"))

    def count(self, b, tiles=0):
        return TB * (self.before + b) + tiles

    def load(self, eng):
        eng.dma_start(self.w[:, :, :], self.k.ins[self.w_name]).then_inc(self.w_loaded, 16)

    def tensor(self, pe, b):
        pe.wait_ge(self.w_loaded, 16)

        def logits_of(i):
            pe.wait_ge(self.t_taken, self.count(b, i + 1))
            for c in range(KC):
                mm = pe.matmul(self.l_psum[:, i, :], self.h_t[:, i % 2, c, :], self.w[:, c, :],
                               start=(c == 0), stop=(c == KC - 1))
            mm.then_inc(self.tile_routed, 1)

        for i in range(TB):
            pe.wait_ge(self.norm.h_ready, self.norm.count(b, i + 1))
            pe.wait_ge(self.t_taken, self.count(b, max(i - 1, 0)))
            for c in range(KC):
                mm = pe.transpose(self.t_psum[:, i % 2, c, :], self.norm.h[:, i, c * P:(c + 1) * P], self.k.ident[:, :])
            mm.then_inc(self.t_full, 1)
            if i == 0:
                pe.wait_ge(self.logits_taken, self.before + b)
            else:
                logits_of(i - 1)
        logits_of(TB - 1)

    def scalar(self, act, b):
        for i in range(TB):
            act.wait_ge(self.t_full, self.count(b, i + 1))
            act.wait_ge(self.tile_routed, self.count(b, max(i - 1, 0)))
            act.copy(self.h_t[:, i % 2, :, :], self.t_psum[:, i % 2, :, :]).then_inc(self.t_taken, 1)
        act.wait_ge(self.tile_routed, self.count(b, TB))
        act.copy(self.logits[:, bass.ds(b * TB, TB), :], self.l_psum[:, :, :]).then_inc(self.logits_taken, 1)

    def wait_h_free(self, dve, b):
        dve.wait_ge(self.t_full, self.count(b))


def project_and_norm0(k, ctx_t, logits, h_rows):
    nc, ins = k.nc, k.ins
    w_loaded, ctx_ready, proj_full, stored = (
        k.sem("p_w_loaded"), k.sem("p_ctx_ready"), k.sem("p_proj_full"), k.sem("p_h_stored"))
    with ExitStack() as st:
        w = k.sb("wproj_sb", [P, KC, D], stack=st)
        bias = k.sb("bproj_tile", [P, D], stack=st)
        cj = k.sb("ctx_batch", [P, KC, S], stack=st)
        pp = k.ps("proj_psum", [P, TB, D], st)
        norm = NormPass(k, st, "n0", (0, GA), (0, CB), (0, SB_), sems="norm_a")
        router = RouterPass(k, st, "r0", "gate_w", norm, logits)

        with nc.Block() as block:
            @block.sync
            def _(sp):
                sp.dma_start(w[:, :, :], ins["wproj"]).then_inc(w_loaded, 16)
                sp.dma_start(bias[:, :], ins["bproj"].broadcast_to([P, D])).then_inc(w_loaded, 16)
                norm.load(sp)
                router.load(sp)
                with sp.Fori(0, B) as b:
                    for i in range(TB):
                        sp.wait_ge(norm.h_ready, norm.count(b, i + 1))
                        sp.dma_start(h_rows(b, i), norm.h[:, i, :]).then_inc(stored, 16)
                sp.wait_ge(stored, 16 * NT)

            @block.gpsimd
            def _(pool):
                with pool.Fori(0, B) as b:
                    norm.gate(pool, b)
                    norm.scale(pool, b)

            @block.tensor
            def _(pe):
                def project(b, first):
                    pe.wait_ge(ctx_ready, b + 1)
                    for i in range(TB):
                        if not first:
                            pe.wait_ge(norm.delta_ready, norm.count(b - 1, i + 1))
                        for c in range(KC):
                            mm = pe.matmul(pp[:, i, :], cj[:, c, i * P:(i + 1) * P], w[:, c, :],
                                           start=(c == 0), stop=(c == KC - 1))
                        mm.then_inc(proj_full, 1)

                def body(b, last):
                    if not last:
                        project(b + 1, False)
                    router.tensor(pe, b)

                pe.wait_ge(w_loaded, 32)
                project(0, True)
                batch_loop(pe, body)

            @block.scalar
            def _(act):
                act.copy(cj[:, :, :], ctx_t[:, 0, :, :]).then_inc(ctx_ready, 1)

                def body(b, last):
                    if not last:
                        act.wait_ge(proj_full, TB * b + TB)
                        act.copy(cj[:, :, :], ctx_t[:, bass.ds(b + 1, 1), :, :].rearrange("p a c s -> p (a c) s")
                                 ).then_inc(ctx_ready, 1)
                    norm.root(act, b)
                    router.scalar(act, b)

                batch_loop(act, body)

            @block.vector
            def _(dve):
                dve.wait_ge(w_loaded, 32)
                dve.wait_ge(norm.mod_loaded, 16 * 3 * B)
                with dve.Fori(0, B) as b:
                    for i in range(TB):
                        dve.wait_ge(proj_full, TB * b + i + 1)
                        dve.tensor_tensor(norm.delta[:, i, :], pp[:, i, :], bias[:, :], ALU.add
                                          ).then_inc(norm.delta_ready, 1)
                    norm.add(dve, b)
                    norm.statistics(dve, b)
                    router.wait_h_free(dve, b)
                    dve.wait_ge(stored, 16 * TB * b)
                    norm.center(dve, b)
                    norm.shift(dve, b)


class Routing:

    def __init__(self, k, name, stack):
        self.weight = k.sb(f"{name}_weight", [P, 2, NT], stack=stack)
        self.steps = 0
        self.scatter_row = k.sb(f"{name}_scatter_row", [P, 2, NT], U32, stack=stack)
        self.gather_row = k.sb(f"{name}_gather_row", [P, 2, NT], U32, stack=stack)


def route(k, name, layer, logits, h_rows, routing, dispatch, tile_expert=None):
    nc = k.nc
    exp_in, exp_out, onehot_done, counted = (
        k.sem("route_exp_in"), k.sem("route_exp_out"), k.sem("route_onehot_done"), k.sem("route_counted"))
    step_done, rows_done, scattered, h_loaded = (
        k.sem("route_step"), k.sem("route_rows_done"), k.sem("route_scattered"), k.sem("route_h_loaded"))
    iota_done, consts = k.sem(f"{name}_iota_done"), k.sem(f"{name}_consts")
    HUGE = float(1 << 20)
    NK = 2 * E * NT
    with ExitStack() as st:
        def sb(n, shape, dtype=F32):
            return k.sb(f"{name}_{n}", shape, dtype, stack=st)

        h_all = sb("h_all", [P, NT, D])
        before = sb("before", [P, P])
        ones = sb("ones", [P, P])
        running = sb("running", [P, 2 * E, NT])
        iotas = sb("iotas", [P, 2 * E + TILES1], I32)
        iotas_f = sb("iotas_f", [P, 2 * E + TILES1])
        stat = sb("stat", [P, 4, NT])
        best = sb("best", [P, NT, 8])
        index = sb("index", [P, NT, 8], U32)
        index_f = sb("index_f", [P, NT, 8])
        onehot = sb("onehot", [P, 2, E, NT])
        total = sb("total", [P, 2, E, NT])
        incl = sb("incl", [P, 2, E, NT])
        place = sb("place", [P, 2, E, NT])
        prod = sb("prod", [P, 2, E, NT])
        pos = sb("pos", [P, 2, NT])
        base = sb("base", [P, 2, E])
        row = sb("row", [P, 2, NT])
        keep = sb("keep", [P, 2, NT])
        counts = sb("counts", [P, 4, E])
        counts_i = sb("counts_i", [P, E], I32)
        cmp = sb("cmp", [P, TILES1, E])
        te = sb("te", [P, TILES1])
        cp = k.ps(f"{name}_count_psum", [P, 2, NK], st)

        def over_e(ap):
            return ap.rearrange("p (t a) -> p t a", a=1).broadcast_to([P, NT, E])

        def ket(ap):
            return ap.rearrange("p k e t -> p (k e) t")

        with nc.Block() as block:
            @block.sync
            def _(sp):
                for t in range(NT):
                    sp.dma_start(h_all[:, t, :], h_rows(t // TB, t % TB)).then_inc(h_loaded, 16)

            @block.gpsimd
            def _(pool):
                pool.iota(iotas[:, 0:E], [[1, E]], base=0, channel_multiplier=0).then_inc(iota_done, 1)
                pool.wait_ge(iota_done, 1)
                pool.iota(iotas[:, E:2 * E], [[REGION, E]], base=T, channel_multiplier=0).then_inc(iota_done, 1)
                pool.wait_ge(iota_done, 2)
                pool.iota(iotas[:, 2 * E:], [[P, TILES1]], base=0, channel_multiplier=0).then_inc(iota_done, 1)
                pool.memset(ones[:, :], 1.0).then_inc(consts, 1)
                pool.memset(before[:, :], 1.0).then_inc(consts, 1)
                pool.memset(running[:, :, :], 1.0).then_inc(consts, 1)
                pool.wait_ge(consts, 3)
                pool.memset(running[:, :, 0:1], 0.0).then_inc(consts, 1)
                pool.affine_select(out=before[:, :], in_=before[:, :], compare_op=ALU.is_gt, fill=0.0,
                                   base=0, pattern=[[1, P]], channel_multiplier=-1).then_inc(consts, 1)
                pool.wait_ge(rows_done, layer + 1)
                pool.wait_ge(h_loaded, 16 * NT * (layer + 1))
                for t in range(NT):
                    for c in range(2):
                        pool.indirect_dma_start(
                            out=dispatch, out_offset=bass.IndirectOffsetOnAxis(ap=routing.scatter_row[:, c, t:t + 1], axis=0),
                            in_=h_all[:, t, :], in_offset=None, bounds_check=dispatch.shape[0] - 1, oob_is_err=False,
                        ).then_inc(scattered, 16)
                pool.wait_ge(scattered, 16 * 2 * NT * (layer + 1))

            @block.scalar
            def _(act):
                act.wait_ge(exp_in, layer + 1)
                act.activation(logits[:, :, :], logits[:, :, :], ACT.Exp).then_inc(exp_out, 1)

            @block.tensor
            def _(pe):
                pe.wait_ge(consts, 5)
                pe.wait_ge(onehot_done, 2 * (layer + 1))
                pe.matmul(cp[:, 0, :], before[:, :], onehot.rearrange("p k e t -> p (k e t)"), start=True, stop=True)
                pe.matmul(cp[:, 1, :], ones[:, :], onehot.rearrange("p k e t -> p (k e t)"), start=True,
                          stop=True).then_inc(counted, 1)

            @block.vector
            def _(dve):
                def step(ins):
                    routing.steps += 1
                    ins.then_inc(step_done, 1)
                    dve.wait_ge(step_done, routing.steps)

                dve.wait_ge(iota_done, 3)
                step(dve.tensor_copy(iotas_f[:, :], iotas[:, :]))
                top, total_p, inv, both = (stat[:, n, :] for n in range(4))
                step(dve.tensor_reduce(top, logits[:, :, :], AX.X, ALU.max))
                dve.tensor_tensor(logits[:, :, :], logits[:, :, :], over_e(top), ALU.subtract).then_inc(exp_in, 1)
                dve.wait_ge(exp_out, layer + 1)
                step(dve.tensor_reduce(total_p, logits[:, :, :], AX.X, ALU.add))
                step(dve.reciprocal(inv, total_p))
                step(dve.tensor_tensor(logits[:, :, :], logits[:, :, :], over_e(inv), ALU.mult))
                for t in range(NT):
                    step(dve.max(best[:, t, :], logits[:, t, :]))
                    step(dve.max_index(index[:, t, :], best[:, t, :], logits[:, t, :]))
                step(dve.tensor_copy(index_f[:, :, :], index[:, :, :]))
                for c in range(2):
                    ids = iotas_f[:, 0:E].rearrange("p (a e) -> p a e", a=1).broadcast_to([P, NT, E])
                    dve.tensor_tensor(onehot[:, c, :, :].rearrange("p e t -> p t e"), ids,
                                      over_e(index_f[:, :, c]), ALU.is_equal).then_inc(onehot_done, 1)
                dve.wait_ge(counted, layer + 1)
                dve.wait_ge(consts, 5)
                step(dve.tensor_copy(total.rearrange("p k e t -> p (k e t)"), cp[:, 1, :]))
                step(dve.tensor_tensor_scan(incl.rearrange("p k e t -> p (k e t)"),
                                            running.rearrange("p a t -> p (a t)"),
                                            total.rearrange("p k e t -> p (k e t)"), 0.0, ALU.mult, ALU.add))
                step(dve.tensor_tensor(ket(place), ket(incl), ket(total), ALU.subtract))
                step(dve.tensor_tensor(place.rearrange("p k e t -> p (k e t)"),
                                       place.rearrange("p k e t -> p (k e t)"), cp[:, 0, :], ALU.add))
                step(dve.tensor_tensor(ket(prod), ket(onehot), ket(place), ALU.mult))
                for c in range(2):
                    step(dve.tensor_reduce(pos[:, c, :], prod[:, c, :, :].rearrange("p e t -> p t e"), AX.X, ALU.add))
                n_first, n_second = incl[:, 0, :, NT - 1], incl[:, 1, :, NT - 1]
                if layer == 0:
                    step(dve.tensor_copy(base[:, 0, :], iotas_f[:, E:2 * E]))
                    step(dve.tensor_scalar(counts[:, 0, :], n_first, float(CAP), None, ALU.min))
                    step(dve.tensor_tensor(base[:, 1, :], base[:, 0, :], counts[:, 0, :], ALU.add))
                else:
                    step(dve.tensor_tensor(counts[:, 0, :], n_first, n_second, ALU.add))
                    step(dve.tensor_scalar(counts_i[:, :], counts[:, 0, :], float(P - 1), None, ALU.add))
                    step(dve.tensor_scalar(counts_i[:, :], counts_i[:, :], P.bit_length() - 1, None,
                                           ALU.logical_shift_right))
                    step(dve.tensor_copy(counts[:, 1, :], counts_i[:, :]))
                    step(dve.tensor_tensor_scan(counts[:, 2, :], ones[:, 0:E], counts[:, 1, :], 0.0, ALU.mult, ALU.add))
                    step(dve.tensor_tensor(counts[:, 3, :], counts[:, 2, :], counts[:, 1, :], ALU.subtract))
                    step(dve.tensor_scalar(base[:, 0, :], counts[:, 3, :], float(P), None, ALU.mult))
                    step(dve.tensor_tensor(base[:, 1, :], base[:, 0, :], n_first, ALU.add))
                    tiles = iotas_f[:, 2 * E:].rearrange("p (t a) -> p t a", a=1).broadcast_to([P, TILES1, E])
                    starts = base[:, 0, :].rearrange("p (a e) -> p a e", a=1).broadcast_to([P, TILES1, E])
                    step(dve.tensor_tensor(cmp[:, :, :], tiles, starts, ALU.is_ge))
                    step(dve.tensor_reduce(te[:, :], cmp[:, :, :], AX.X, ALU.add))
                    step(dve.tensor_scalar(tile_expert[:, :], te[:, :], -1.0, None, ALU.add))
                step(dve.tensor_tensor(ket(prod), ket(onehot),
                                       base.rearrange("p k (e a) -> p (k e) a", a=1).broadcast_to([P, 2 * E, NT]),
                                       ALU.mult))
                for c in range(2):
                    step(dve.tensor_reduce(row[:, c, :], prod[:, c, :, :].rearrange("p e t -> p t e"), AX.X, ALU.add))
                step(dve.tensor_tensor(row[:, :, :], row[:, :, :], pos[:, :, :], ALU.add))
                w = routing.weight
                if layer == 0:
                    step(dve.tensor_scalar(keep[:, :, :], pos[:, :, :], float(CAP), None, ALU.is_lt))
                    for c in range(2):
                        step(dve.tensor_tensor(w[:, c, :], best[:, :, c], keep[:, c, :], ALU.mult))
                    step(dve.tensor_tensor(pos[:, :, :], row[:, :, :], keep[:, :, :], ALU.mult))
                    step(dve.tensor_copy(routing.gather_row[:, :, :], pos[:, :, :]))
                    step(dve.tensor_scalar(keep[:, :, :], keep[:, :, :], -HUGE, HUGE, ALU.mult, ALU.add))
                    step(dve.tensor_tensor(row[:, :, :], row[:, :, :], keep[:, :, :], ALU.add))
                else:
                    step(dve.tensor_tensor(both, best[:, :, 0], best[:, :, 1], ALU.add))
                    step(dve.reciprocal(inv, both))
                    for c in range(2):
                        step(dve.tensor_tensor(w[:, c, :], best[:, :, c], inv, ALU.mult))
                    step(dve.tensor_copy(routing.gather_row[:, :, :], row[:, :, :]))
                dve.tensor_copy(routing.scatter_row[:, :, :], row[:, :, :]).then_inc(rows_done, 1)


def experts0(k):
    nc, ins = k.nc, k.ins
    STEPS = FC + 1
    GROUP = 4
    GROUPS = FC // GROUP
    BIG = 4 * P

    def sem(n):
        return k.sem(f"e0_{n}")

    small_loaded, x_loaded, branch_loaded = sem("small_loaded"), sem("x_loaded"), sem("branch_loaded")
    w_loaded = [sem(f"w_loaded{i}") for i in range(2)]
    xt_full, xt5_full, xt_hi, xt5_hi, xt_split = (
        sem("xt_full"), sem("xt5_full"), sem("xt_hi"), sem("xt5_hi"), sem("xt_split"))
    branch_hi, branch_split, w1_hi, w1_split, w2_hi, w2_split = (
        sem("branch_hi"), sem("branch_split"), sem("w1_hi"), sem("w1_split"), sem("w2_hi"), sem("w2_split"))
    h_full, gelu_done, g_hi, g_split = sem("h_full"), sem("gelu_done"), sem("g_hi"), sem("g_split")
    small_taken = sem("small_taken")
    y_done, y_taken, y_stored, consts = sem("y_done"), sem("y_taken"), sem("y_stored"), sem("consts")

    with ExitStack() as st:
        def sb(n, shape, dtype=F32):
            return k.sb(f"e0_{n}", shape, dtype, stack=st)

        x_raw = sb("x_raw", [P, 5, D])
        xh, xl = sb("x_hi", [P, KC, BIG], F32R), sb("x_lo", [P, KC, BIG], F32R)
        x5h, x5l = sb("x5_hi", [P, KC, P], F32R), sb("x5_lo", [P, KC, P], F32R)
        w1_raw, w2_raw = sb("w1_raw", [P, 2, GROUP, KC * P]), sb("w2_raw", [P, 2, GROUP, D])
        w1h, w1l = sb("w1_hi", [P, 2, KC, P], F32R), sb("w1_lo", [P, 2, KC, P], F32R)
        w2h, w2l = sb("w2_hi", [P, 2, D], F32R), sb("w2_lo", [P, 2, D], F32R)
        g_raw = sb("g_raw", [P, 2, REGION])
        gh, gl = sb("g_hi", [P, 2, REGION], F32R), sb("g_lo", [P, 2, REGION], F32R)
        a_raw = sb("branch_g_raw", [RANK, REGION])
        ah, al = sb("branch_g_hi", [P, REGION], F32R), sb("branch_g_lo", [P, REGION], F32R)
        wub_raw = sb("wu_b2_raw", [RANK + 1, D])
        wubh, wubl = sb("wu_b2_hi", [P, D], F32R), sb("wu_b2_lo", [P, D], F32R)
        wd_raw = sb("wd_raw", [P, E + 1, KC * RANK])
        wdh, wdl = sb("wd_hi", [P, KC, RANK], F32R), sb("wd_lo", [P, KC, RANK], F32R)
        b1 = sb("b1_sb", [P, (E + 1) * FC])
        y_sb = sb("y_sb", [P, 5, D])
        y = k.ps("e0_y", [P, 5, D], st)
        hb = k.ps("e0_h", [P, 2, BIG], st)
        hs = k.ps("e0_h_small", [P, 4, P], st)

        def region(rows, v, tiles):
            if tiles == 4:
                return rows[0:T, :].rearrange("(r t p) d -> r p t d", r=B, p=P)[bass.ds(v, 1)].rearrange("a p t d -> (a p) t d")
            return rows[T:, :].rearrange("(r t p) d -> r p t d", r=E, p=P)[bass.ds(v - B, 1)].rearrange("a p t d -> (a p) t d")

        def splits(v, tiles):
            return 4 * v if tiles == 4 else 5 * v - B

        def of_expert(ap, w):
            if isinstance(w, int):
                return ap[w]
            return ap[bass.ds(w, 1)].rearrange("a p n -> (a p) n")

        def loops(eng, body):
            with eng.Fori(0, B) as v:
                body(v, 0, 4)
            with eng.Fori(B, B + E) as v:
                body(v, v - (B - 1), 5)

        with nc.Block() as block:
            @block.sync
            def _(sp):
                sp.dma_start(wd_raw[:, :, :], ins["wd"]).then_inc(small_loaded, 16)
                sp.dma_start(b1[:, :], ins["b1"]).then_inc(small_loaded, 16)

                def body(v, w, tiles):
                    sp.wait_ge(xt_split, splits(v, tiles))
                    sp.dma_start(x_raw[:, 0:tiles, :], region(k.dispatch, v, tiles)).then_inc(x_loaded, 16)
                    sp.wait_ge(branch_split, 2 * v)
                    sp.dma_start(wub_raw[:, :], of_expert(ins["wu_b2"], w)).then_inc(branch_loaded, 16)
                    for g in range(GROUPS):
                        done = FC * v + (GROUP * (g - 1) if g >= 2 else 0)
                        sp.wait_ge(w1_split, done)
                        sp.wait_ge(w2_split, done)
                        for raw, name in ((w1_raw, "w1"), (w2_raw, "w2")):
                            sp.dma_start(raw[:, g % 2, :, :].rearrange("p c n -> p (c n)"),
                                         of_expert(ins[name][:, g], w)).then_inc(w_loaded[g % 2], 16)

                loops(sp, body)

            def wait_weights(eng, v, c):
                g = c // GROUP
                eng.wait_ge(w_loaded[g % 2], 32 * (GROUPS // 2 * v + g // 2 + 1))

            @block.gpsimd
            def _(pool):
                def body(v, w, tiles):
                    for c in range(FC):
                        pool.wait_ge(w2_hi, FC * v + c + 1)
                        pool.tensor_tensor(w2l[:, c % 2, :], w2_raw[:, c // GROUP % 2, c % GROUP, :],
                                           w2h[:, c % 2, :].bitcast(F32), ALU.subtract).then_inc(w2_split, 1)

                loops(pool, body)

            @block.tensor
            def _(pe):
                def body(v, w, tiles):
                    pe.wait_ge(x_loaded, 16 * v + 16)
                    for c in range(KC):
                        if c < 2:
                            pe.wait_ge(gelu_done, STEPS * v)
                        else:
                            pe.wait_ge(xt_split, splits(v, tiles) + c - 1)
                        for t in range(4):
                            mm = pe.transpose(hb[:, c % 2, t * P:(t + 1) * P], x_raw[:, t, c * P:(c + 1) * P],
                                              k.ident[:, :])
                        mm.then_inc(xt_full, 1)
                    if tiles == 5:
                        for c in range(KC):
                            mm = pe.transpose(hs[:, c, :], x_raw[:, 4, c * P:(c + 1) * P], k.ident[:, :])
                        mm.then_inc(xt5_full, 1)

                    def hidden(a):
                        width = RANK if a == 0 else P
                        if a == 0:
                            pe.wait_ge(xt_split, splits(v, tiles) + tiles)
                            pe.wait_ge(branch_split, 2 * v + 2)
                            wh, wl = wdh, wdl
                        else:
                            pe.wait_ge(w1_split, FC * v + a)
                            wh, wl = w1h[:, (a - 1) % 2, :, :], w1l[:, (a - 1) % 2, :, :]
                        pe.wait_ge(gelu_done, STEPS * v + max(a - 1, 0))
                        parts = [(hb[0:width, a % 2, :], xh, xl)]
                        if tiles == 5:
                            parts.append((hs[0:width, 0, :], x5h, x5l))
                        for out, high, low in parts:
                            if high is x5h:
                                pe.wait_ge(small_taken, STEPS * (v - B) + a)
                            for c in range(KC):
                                pe.matmul(out, wh[:, c, :], high[:, c, :], start=(c == 0), stop=False)
                                pe.matmul(out, wh[:, c, :], low[:, c, :], start=False, stop=False)
                                mm = pe.matmul(out, wl[:, c, :], high[:, c, :], start=False, stop=(c == KC - 1))
                        mm.then_inc(h_full, 1)

                    def output(a):
                        if a == 0:
                            pe.wait_ge(y_taken, v)
                            sh, sl, wh, wl = ah, al, wubh[:, :], wubl[:, :]
                        else:
                            pe.wait_ge(w2_split, FC * v + a)
                            i = (a - 1) % 2
                            sh, sl, wh, wl = gh[:, a % 2, :], gl[:, a % 2, :], w2h[:, i, :], w2l[:, i, :]
                        pe.wait_ge(g_split, STEPS * v + a + 1)
                        for t in range(tiles):
                            tile = slice(t * P, (t + 1) * P)
                            pe.matmul(y[:, t, :], sh[:, tile], wh, start=(a == 0), stop=False)
                            pe.matmul(y[:, t, :], sh[:, tile], wl, start=False, stop=False)
                            mm = pe.matmul(y[:, t, :], sl[:, tile], wh, start=False, stop=(a == STEPS - 1))
                        mm.then_inc(y_done, 1)

                    hidden(0)
                    for a in range(1, STEPS):
                        hidden(a)
                        output(a - 1)
                    output(STEPS - 1)

                loops(pe, body)

            @block.scalar
            def _(act):
                def body(v, w, tiles):
                    for c in range(KC):
                        act.wait_ge(xt_full, KC * v + c + 1)
                        act.activation(xh[:, c, :], hb[:, c % 2, :], ACT.Copy).then_inc(xt_hi, 1)
                    if tiles == 5:
                        act.wait_ge(xt5_full, v - (B - 1))
                        act.activation(x5h[:, :, :], hs[:, :, :], ACT.Copy).then_inc(xt5_hi, 1)
                    for a in range(STEPS):
                        if a > 0:
                            c = a - 1
                            wait_weights(act, v, c)
                            act.wait_ge(y_done, STEPS * v + (c if c >= 2 else 0))
                            act.activation(w2h[:, c % 2, :], w2_raw[:, c // GROUP % 2, c % GROUP, :],
                                           ACT.Copy).then_inc(w2_hi, 1)
                        act.wait_ge(h_full, STEPS * v + a + 1)
                        act.wait_ge(g_split, STEPS * v + max(a - 1, 0))
                        dst = a_raw[:, :] if a == 0 else g_raw[:, a % 2, :]
                        width = RANK if a == 0 else P
                        bias = 0.0 if a == 0 else (b1[:, w * FC + a - 1:w * FC + a] if isinstance(w, int)
                                                   else b1[:, bass.ds(w * FC + (a - 1), 1)])
                        if a == 1:
                            act.wait_ge(small_loaded, 32)
                        if tiles == 5:
                            act.activation(dst[:, BIG:REGION], hs[0:width, 0, :], ACT.Gelu,
                                           bias=bias).then_inc(small_taken, 1)
                        act.activation(dst[:, 0:BIG], hb[0:width, a % 2, :], ACT.Gelu, bias=bias).then_inc(gelu_done, 1)
                    act.wait_ge(y_done, STEPS * (v + 1))
                    act.wait_ge(y_stored, 16 * v)
                    for t in range(tiles):
                        last = act.copy(y_sb[:, t, :], y[:, t, :])
                    last.then_inc(y_taken, 1)
                    act.wait_ge(y_taken, v + 1)
                    act.dma_start(region(k.expert_out, v, tiles), y_sb[:, 0:tiles, :]).then_inc(y_stored, 16)

                loops(act, body)
                act.wait_ge(y_stored, 16 * (B + E))

            @block.vector
            def _(dve):
                for buf in (ah, al, wubh, wubl):
                    dve.memset(buf[32:64, :].bitcast(F32), 0.0).then_inc(consts, 1)
                    dve.memset(buf[64:128, :].bitcast(F32), 0.0).then_inc(consts, 1)
                dve.wait_ge(consts, 8)
                dve.memset(ah[32:33, :].bitcast(F32), 1.0).then_inc(consts, 1)
                dve.wait_ge(small_loaded, 32)

                def body(v, w, tiles):
                    dve.wait_ge(branch_loaded, 16 * v + 16)
                    dve.wait_ge(y_done, STEPS * v)
                    dve.wait_ge(consts, 9)
                    wd = flat(wd_raw[:, bass.ds(w, 1), :]) if not isinstance(w, int) else wd_raw[:, w, :]
                    wd_h, wd_l = (x.rearrange("p c n -> p (c n)") for x in (wdh, wdl))
                    dve.tensor_copy(wd_h, wd).then_inc(branch_hi, 1)
                    dve.tensor_copy(wubh[0:RANK + 1, :], wub_raw[:, :]).then_inc(branch_hi, 1)
                    dve.wait_ge(branch_hi, 2 * v + 2)
                    dve.tensor_tensor(wd_l, wd, wd_h.bitcast(F32), ALU.subtract).then_inc(branch_split, 1)
                    dve.tensor_tensor(wubl[0:RANK + 1, :], wub_raw[:, :], wubh[0:RANK + 1, :].bitcast(F32),
                                      ALU.subtract).then_inc(branch_split, 1)
                    for c in range(KC):
                        dve.wait_ge(xt_hi, KC * v + c + 1)
                        dve.tensor_tensor(xl[:, c, :], hb[:, c % 2, :], xh[:, c, :].bitcast(F32),
                                          ALU.subtract).then_inc(xt_split, 1)
                    if tiles == 5:
                        dve.wait_ge(xt5_hi, v - (B - 1))
                        dve.tensor_tensor(x5l[:, :, :], hs[:, :, :], x5h[:, :, :].bitcast(F32),
                                          ALU.subtract).then_inc(xt_split, 1)
                    for a in range(STEPS):
                        if a < FC:
                            c = a
                            wait_weights(dve, v, c)
                            dve.wait_ge(h_full, STEPS * v + (c if c >= 2 else 0))
                            raw = w1_raw[:, c // GROUP % 2, c % GROUP, :]
                            hi, lo = (x[:, c % 2, :, :].rearrange("p c n -> p (c n)") for x in (w1h, w1l))
                            dve.tensor_copy(hi, raw).then_inc(w1_hi, 1)
                            dve.wait_ge(w1_hi, FC * v + c + 1)
                            dve.tensor_tensor(lo, raw, hi.bitcast(F32), ALU.subtract).then_inc(w1_split, 1)
                        n = tiles * P
                        dve.wait_ge(gelu_done, STEPS * v + a + 1)
                        if a == 0:
                            raw, hi, lo = a_raw[:, 0:n], ah[0:RANK, 0:n], al[0:RANK, 0:n]
                        else:
                            raw, hi, lo = g_raw[:, a % 2, 0:n], gh[:, a % 2, 0:n], gl[:, a % 2, 0:n]
                            dve.wait_ge(y_done, STEPS * v + max(a - 1, 0))
                        dve.tensor_copy(hi, raw).then_inc(g_hi, 1)
                        dve.wait_ge(g_hi, STEPS * v + a + 1)
                        dve.tensor_tensor(lo, raw, hi.bitcast(F32), ALU.subtract).then_inc(g_split, 1)

                loops(dve, body)


class Combine:

    def __init__(self, k, st, name, routing, source, norm, shared=None, before=0):
        self.k, self.routing, self.source, self.norm, self.shared, self.before = k, routing, source, norm, shared, before
        self.rows = k.sb(f"{name}_rows", [P, 2, TB, D], stack=st)
        self.index = k.sb(f"{name}_index", [P, 2, TB], U32, stack=st)
        if shared is not None:
            self.shared_rows = k.sb(f"{name}_shared_rows", [P, TB, D], stack=st)
        self.gathered = [k.sem(f"combine_gathered{i}") for i in range(2)]
        self.index_ready, self.shared_loaded, self.first, self.second = (
            k.sem("combine_index_ready"), k.sem("combine_shared_loaded"), k.sem("combine_first"), k.sem("combine_second"))

    def load_shared(self, eng, b):
        eng.wait_ge(self.norm.delta_ready, self.norm.count(b))
        eng.dma_start(self.shared_rows[:, :, :],
                      self.shared[bass.ds(b, 1), 0:S, :].rearrange("a (t p) d -> p (a t) d", p=P)
                      ).then_inc(self.shared_loaded, 16)

    def gather(self, pool, b):
        pool.wait_ge(self.norm.delta_ready, self.norm.count(b))
        pool.tensor_copy(self.index[:, :, :], self.routing.gather_row[:, :, bass.ds(b * TB, TB)]
                         ).then_inc(self.index_ready, 1)
        wait_alone(pool, self.index_ready, self.before + b + 1, self.k.passed)
        for c in range(2):
            for i in range(TB):
                pool.indirect_dma_start(
                    out=self.rows[:, c, i, :], out_offset=None, in_=self.source,
                    in_offset=bass.IndirectOffsetOnAxis(ap=self.index[:, c, i:i + 1], axis=0),
                ).then_inc(self.gathered[c], 16)

    def weight(self, c, b, i):
        return self.routing.weight[:, c, bass.ds(b * TB + i, 1)]

    def sum(self, dve, b):
        delta = self.norm.delta
        dve.wait_ge(self.gathered[0], 16 * TB * (self.before + b + 1))
        dve.wait_ge(self.norm.added, self.norm.count(b))
        for i in range(TB):
            dve.tensor_scalar(delta[:, i, :], self.rows[:, 0, i, :], self.weight(0, b, i), None,
                              ALU.mult).then_inc(self.first, 1)
        dve.wait_ge(self.gathered[1], 16 * TB * (self.before + b + 1))
        for i in range(TB):
            dve.wait_ge(self.first, TB * (self.before + b) + i + 1)
            last = dve.scalar_tensor_tensor(out=delta[:, i, :], in0=self.rows[:, 1, i, :],
                                            scalar=self.weight(1, b, i), in1=delta[:, i, :], op0=ALU.mult, op1=ALU.add)
            last.then_inc(self.norm.delta_ready if self.shared is None else self.second, 1)
        if self.shared is not None:
            dve.wait_ge(self.shared_loaded, 16 * (b + 1))
            for i in range(TB):
                dve.wait_ge(self.second, TB * b + i + 1)
                dve.scalar_tensor_tensor(out=delta[:, i, :], in0=self.shared_rows[:, i, :], scalar=0.2,
                                         in1=delta[:, i, :], op0=ALU.mult, op1=ALU.add
                                         ).then_inc(self.norm.delta_ready, 1)


def combine_and_attention1(k, routing, logits, h_rows):
    nc = k.nc

    def sem(n):
        return k.sem(f"a1_{n}")

    BANKS = 4
    full = [sem(f"full{i}") for i in range(BANKS)]
    free = [sem(f"free{i}") for i in range(BANKS)]
    max_done, negated, inv_done, prob_done, stored = (
        sem("max_done"), sem("negated"), sem("inv_done"), sem("prob_done"), sem("stored"))
    KINDS = ("hT", "scores", "probT", "ctx")

    with ExitStack() as st:
        norm1 = NormPass(k, st, "n1", (0, GB), (1, CA), (1, SA), sems="norm_a", before=B)
        norm2 = NormPass(k, st, "n2", (1, GA), (1, CB), (1, SB_), sems="norm_b")
        combine = Combine(k, st, "c0", routing, k.expert_out, norm1,
                          shared=k.expert_out[0:T, :].rearrange("(r q) d -> r q d", q=S))
        router = RouterPass(k, st, "r1", "wr", norm2, logits, before=B)
        h_t = k.sb("a1_h_t", [P, KC, S], stack=st)
        prob = k.sb("a1_prob", [P, KC, D], stack=st)
        prob_t = k.sb("a1_prob_t", [P, KC, D], stack=st)
        mx = k.sb("a1_max", [P, KC], stack=st)
        neg = k.sb("a1_neg_max", [P, KC], stack=st)
        total = k.sb("a1_total", [P, KC], stack=st)
        inv = k.sb("a1_inv", [P, KC], stack=st)
        ps = k.ps("a1_psum", [P, BANKS, D], st)
        h = norm1.h

        def turn(kind, b):
            return 4 * b + KINDS.index(kind)

        def wait_full(eng, kind, n, b):
            eng.wait_ge(full[n], turn(kind, b) + 1)

        def wait_free(pe, kind, n, b):
            pe.wait_ge(free[n], turn(kind, b))

        def wait_taken(pe, kind, b):
            for n in range(4):
                pe.wait_ge(free[n], turn(kind, b) + 1)

        with nc.Block() as block:
            @block.sync
            def _(sp):
                norm1.load(sp)
                norm2.load(sp)
                router.load(sp)
                combine.load_shared(sp, 0)

                def body(b, last):
                    if not last:
                        combine.load_shared(sp, b + 1)
                    for i in range(TB):
                        sp.wait_ge(norm2.h_ready, norm2.count(b, i + 1))
                        sp.dma_start(h_rows(b, i), norm2.h[:, i, :]).then_inc(stored, 16)

                batch_loop(sp, body)
                sp.wait_ge(stored, 16 * NT)

            @block.gpsimd
            def _(pool):
                combine.gather(pool, 0)
                norm1.gate(pool, 0)
                norm1.scale(pool, 0)

                def body(b, last):
                    if not last:
                        combine.gather(pool, b + 1)
                        norm1.gate(pool, b + 1)
                        norm1.scale(pool, b + 1)
                    norm2.gate(pool, b)
                    norm2.scale(pool, b)

                batch_loop(pool, body)

            @block.tensor
            def _(pe):
                def body(b, last):
                    pe.wait_ge(norm1.h_ready, norm1.count(b, TB))
                    for c in range(KC):
                        wait_free(pe, "hT", c, b)
                        for i in range(TB):
                            mm = pe.transpose(ps[:, c, i * P:(i + 1) * P], h[:, i, c * P:(c + 1) * P], k.ident[:, :])
                        mm.then_inc(full[c], 1)
                    for n in range(KC):
                        wait_free(pe, "scores", n, b)
                        for i in range(TB):
                            mm = pe.matmul(ps[:, n, :], h[:, i, n * P:(n + 1) * P], h[:, i, :],
                                           start=(i == 0), stop=(i == TB - 1))
                        mm.then_inc(full[n], 1)
                    pe.wait_ge(prob_done, KC * b + KC)
                    for c in range(KC):
                        wait_free(pe, "probT", c, b)
                        for n in range(KC):
                            mm = pe.transpose(ps[:, c, n * P:(n + 1) * P], prob[:, n, c * P:(c + 1) * P], k.ident[:, :])
                        mm.then_inc(full[c], 1)
                    wait_taken(pe, "probT", b)
                    for i in range(TB):
                        for c in range(KC):
                            mm = pe.matmul(ps[:, i, :], h_t[:, c, i * P:(i + 1) * P], prob_t[:, c, :],
                                           start=(c == 0), stop=(c == KC - 1))
                        mm.then_inc(full[i], 1)
                    router.tensor(pe, b)

                with pe.Fori(0, B) as b:
                    body(b, False)

            @block.scalar
            def _(act):
                norm1.root(act, 0)

                def body(b, last):
                    for c in range(KC):
                        wait_full(act, "hT", c, b)
                        act.copy(h_t[:, c, :], ps[:, c, :]).then_inc(free[c], 1)
                    act.wait_ge(negated, b + 1)
                    for n in range(KC):
                        act.activation(prob[:, n, :], ps[:, n, :], ACT.Exp, bias=neg[:, n:n + 1],
                                       accum_out=total[:, n:n + 1]).then_inc(free[n], 1)
                    for c in range(KC):
                        wait_full(act, "probT", c, b)
                        act.copy(prob_t[:, c, :], ps[:, c, :]).then_inc(free[c], 1)
                    if not last:
                        norm1.root(act, b + 1)
                    norm2.root(act, b)
                    router.scalar(act, b)

                batch_loop(act, body)

            @block.vector
            def _(dve):
                def front(b):
                    combine.sum(dve, b)
                    norm1.add(dve, b)
                    norm1.statistics(dve, b)
                    norm1.center(dve, b)
                    norm1.shift(dve, b)

                dve.wait_ge(norm1.mod_loaded, 16 * 3 * B)
                dve.wait_ge(norm2.mod_loaded, 16 * 3 * B)
                front(0)

                def body(b, last):
                    for n in range(KC):
                        wait_full(dve, "scores", n, b)
                        dve.tensor_reduce(mx[:, n:n + 1], ps[:, n, :], AX.X, ALU.max).then_inc(max_done, 1)
                    dve.wait_ge(max_done, KC * b + KC)
                    dve.tensor_scalar(neg[:, :], mx[:, :], -1.0, None, ALU.mult).then_inc(negated, 1)
                    for n in range(KC):
                        dve.wait_ge(free[n], turn("scores", b) + 1)
                    dve.reciprocal(inv[:, :], total[:, :]).then_inc(inv_done, 1)
                    dve.wait_ge(inv_done, b + 1)
                    for n in range(KC):
                        dve.tensor_scalar(prob[:, n, :], prob[:, n, :], inv[:, n:n + 1], None,
                                          ALU.mult).then_inc(prob_done, 1)
                    if not last:
                        front(b + 1)
                    dve.wait_ge(norm2.added, norm2.count(b))
                    for i in range(TB):
                        wait_full(dve, "ctx", i, b)
                        dve.tensor_copy(norm2.delta[:, i, :], ps[:, i, :]).then_inc(free[i], 1)
                    for i in range(TB):
                        dve.wait_ge(free[i], turn("ctx", b) + 1)
                    dve.sem_inc(norm2.delta_ready, TB)
                    norm2.add(dve, b)
                    norm2.statistics(dve, b)
                    router.wait_h_free(dve, b)
                    dve.wait_ge(stored, 16 * TB * b)
                    norm2.center(dve, b)
                    norm2.shift(dve, b)

                batch_loop(dve, body)


def experts1(k, tile_expert):
    nc, ins = k.nc, k.ins
    U = 4
    FULL, REST = INNER // P, INNER % P
    NCH = FULL + 1

    def sem(n):
        return k.sem(f"e1_{n}")

    w_loaded, x_in, x_out = sem("w_loaded"), [sem(f"x_loaded{i}") for i in range(2)], [sem(f"y_stored{i}") for i in range(2)]
    xt_full, xt_taken, gu_full, silu_done, h_ready = (
        sem("xt_full"), sem("xt_taken"), sem("gu_full"), sem("silu_done"), sem("h_ready"))
    ht_full, ht_taken, y_full, y_taken = sem("ht_full"), sem("ht_taken"), sem("y_full"), sem("y_taken")
    with ExitStack() as st:
        def sb(n, shape, dtype=F32):
            return k.sb(f"e1_{n}", shape, dtype, stack=st)

        wgu = sb("wgu", [P, E * KC * 2, INNER])
        wd = sb("wd", [P, E * FULL, D])
        wd_rest = sb("wd_rest", [REST, E, D])
        x = sb("x", [P, 2, D])
        xt = sb("xt", [P, 2, KC, P])
        g = sb("silu", [P, 2, INNER])
        h = sb("h", [P, 2, INNER])
        ht = sb("ht", [P, 2, NCH, P])
        y_sb = sb("y", [P, 2, D])
        pt = k.ps("e1_xt_psum", [P, KC, P], st)
        pgu = k.ps("e1_gu_psum", [P, 4, D], st)
        ph = k.ps("e1_ht_psum", [P, 4, P], st)
        py = k.ps("e1_y_psum", [P, D], st)
        src = k.dispatch1.rearrange("(t p) d -> t p d", p=P)
        dst = k.expert_out1.rearrange("(t p) d -> t p d", p=P)

        def loop(eng, body):
            with eng.Fori(0, TILES1 // U) as r:
                body(r, r * U)

        def half(r, i):
            return r * (U // 2) + i // 2

        with nc.Block() as block:
            @block.sync
            def _(sp):
                def body(r, t0):
                    for i in range(U):
                        sp.wait_ge(xt_full, t0 + max(i - 1, 0))
                        sp.dma_start(x[:, i % 2, :], src[bass.ds(t0 + i, 1)].rearrange("a p d -> (a p) d")
                                     ).then_inc(x_in[i % 2], 16)

                for name, buf in (("wgu", wgu), ("wd1", wd), ("wd1_rest", wd_rest)):
                    sp.dma_start(buf[:, :, :], ins[name]).then_inc(w_loaded, 16)
                loop(sp, body)

            @block.gpsimd
            def _(pool):
                def body(r, t0):
                    for i in range(U):
                        pool.wait_ge(y_taken, t0 + i + 1)
                        pool.dma_start(dst[bass.ds(t0 + i, 1)].rearrange("a p d -> (a p) d"), y_sb[:, i % 2, :]
                                       ).then_inc(x_out[i % 2], 16)

                loop(pool, body)
                for s in x_out:
                    pool.wait_ge(s, 16 * (TILES1 // 2))

            @block.tensor
            def _(pe):
                pe.wait_ge(w_loaded, 48)

                def body(r, t0):
                    experts = [pe.value_load(tile_expert[0:1, bass.ds(t0 + i, 1)], min_val=0, max_val=E - 1)
                               for i in range(U)]

                    def turn_x(i):
                        pe.wait_ge(x_in[i % 2], 16 * (half(r, i) + 1))
                        pe.wait_ge(xt_taken, t0 + i)
                        for c in range(KC):
                            mm = pe.transpose(pt[:, c, :], x[:, i % 2, c * P:(c + 1) * P], k.ident[:, :])
                        mm.then_inc(xt_full, 1)

                    def gate_up(i):
                        pe.wait_ge(xt_taken, t0 + i + 1)
                        pe.wait_ge(h_ready, t0 + max(i - 1, 0))
                        for n in range(2):
                            for c in range(KC):
                                w = flat(wgu[:, bass.ds(experts[i] * (2 * KC) + (2 * c + n), 1), :])
                                mm = pe.matmul(pgu[:, 2 * (i % 2) + n, 0:INNER], xt[:, i % 2, c, :], w,
                                               start=(c == 0), stop=(c == KC - 1))
                        mm.then_inc(gu_full, 1)

                    def turn_h(i):
                        pe.wait_ge(h_ready, t0 + i + 1)
                        pe.wait_ge(ht_taken, t0 + i)
                        for c in range(NCH):
                            n = P if c < FULL else REST
                            mm = pe.transpose(ph[0:n, c, :], h[:, i % 2, c * P:c * P + n], k.ident[:, :])
                        mm.then_inc(ht_full, 1)

                    def down(i):
                        pe.wait_ge(ht_taken, t0 + i + 1)
                        pe.wait_ge(y_taken, t0 + i)
                        for c in range(NCH):
                            w = (flat(wd[:, bass.ds(experts[i] * FULL + c, 1), :]) if c < FULL
                                 else flat(wd_rest[:, bass.ds(experts[i], 1), :]))
                            n = P if c < FULL else REST
                            mm = pe.matmul(py[:, :], ht[0:n, i % 2, c, :], w, start=(c == 0), stop=(c == NCH - 1))
                        mm.then_inc(y_full, 1)

                    turn_x(0)
                    for i in range(U + 1):
                        if i + 1 < U:
                            turn_x(i + 1)
                        if i < U:
                            gate_up(i)
                        if i > 0:
                            turn_h(i - 1)
                            down(i - 1)

                loop(pe, body)

            @block.scalar
            def _(act):
                def body(r, t0):
                    def take_x(i):
                        act.wait_ge(xt_full, t0 + i + 1)
                        act.wait_ge(gu_full, t0 + max(i - 1, 0))
                        act.copy(xt[:, i % 2, :, :], pt[:, :, :]).then_inc(xt_taken, 1)

                    take_x(0)
                    for i in range(U + 1):
                        if i + 1 < U:
                            take_x(i + 1)
                        if i < U:
                            act.wait_ge(gu_full, t0 + i + 1)
                            act.wait_ge(h_ready, t0 + max(i - 1, 0))
                            act.activation(g[:, i % 2, :], pgu[:, 2 * (i % 2), 0:INNER], ACT.Silu).then_inc(silu_done, 1)
                        if i > 0:
                            act.wait_ge(y_full, t0 + i)
                            act.wait_ge(x_out[(i - 1) % 2], 16 * half(r, i - 1))
                            act.copy(y_sb[:, (i - 1) % 2, :], py[:, :]).then_inc(y_taken, 1)

                loop(act, body)

            @block.vector
            def _(dve):
                def body(r, t0):
                    def take_h(i):
                        dve.wait_ge(ht_full, t0 + i + 1)
                        dve.wait_ge(y_full, t0 + max(i - 1, 0))
                        dve.tensor_copy(ht[:, i % 2, 0:FULL, :], ph[:, 0:FULL, :])
                        dve.tensor_copy(ht[0:REST, i % 2, FULL, :], ph[0:REST, FULL, :]).then_inc(ht_taken, 1)

                    for i in range(U + 1):
                        if i < U:
                            dve.wait_ge(silu_done, t0 + i + 1)
                            dve.wait_ge(ht_full, t0 + max(i - 1, 0))
                            dve.tensor_tensor(h[:, i % 2, :], g[:, i % 2, :], pgu[:, 2 * (i % 2) + 1, 0:INNER],
                                              ALU.mult).then_inc(h_ready, 1)
                        if i > 0:
                            take_h(i - 1)

                loop(dve, body)


def combine_to_output(k, routing):
    nc = k.nc
    x_ready, stored = k.sem("out_x_ready"), k.sem("out_stored")
    with ExitStack() as st:
        norm = NormPass(k, st, "n3", (1, GB), sems="norm_b", before=B)
        combine = Combine(k, st, "c1", routing, k.expert_out1, norm, before=B)
        with nc.Block() as block:
            @block.sync
            def _(sp):
                norm.load(sp)
                with sp.Fori(0, B) as b:
                    sp.wait_ge(norm.added, norm.count(b, TB))
                    sp.dma_start(k.out[bass.ds(b, 1)].rearrange("a (t p) d -> p (a t) d", p=P),
                                 k.x[:, bass.ds(b * TB, TB), :]).then_inc(stored, 16)
                sp.wait_ge(stored, 16 * B)

            @block.gpsimd
            def _(pool):
                combine.gather(pool, 0)

                def body(b, last):
                    if not last:
                        combine.gather(pool, b + 1)
                    norm.gate(pool, b)

                batch_loop(pool, body)

            @block.vector
            def _(dve):
                with dve.Fori(0, B) as b:
                    combine.sum(dve, b)
                    norm.add(dve, b)


def program(nc, ins, out, phases=99):
    with ExitStack() as stack:
        k = Core(nc, stack, ins, out)
        routing = Routing(k, "route", stack)
        tile_expert = k.sb("tile_expert", [P, TILES1], I32)
        logits = k.sb("logits", [P, NT, E])
        batches = k.dispatch[0:T, :].rearrange("(b s) d -> b s d", b=B)

        def one(ap, b, rows):
            return (ap[b:b + 1, rows, :] if isinstance(b, int) else ap[bass.ds(b, 1), rows, :]
                    ).rearrange("a q d -> (a q) d")

        def shared_rows(b, i):
            return one(batches, b, slice(i * P, (i + 1) * P))

        def h_rows1(b, i):
            return one(k.h_rows1.rearrange("(b s) d -> b s d", b=B), b, slice(i * P, (i + 1) * P))

        with ExitStack() as ctx_stack:
            ctx_t = k.sb("ctx_t", [P, B, KC, S], stack=ctx_stack)
            with ExitStack() as att_stack:
                att = Attention0(k, att_stack)
                start_and_modulation(k, att)
                if phases >= 1:
                    attention0(k, att, ctx_t)
            if phases >= 2:
                project_and_norm0(k, ctx_t, logits, shared_rows)
        if phases >= 2:
            route(k, "rt0", 0, logits, shared_rows, routing, k.dispatch)
        if phases >= 3:
            experts0(k)
        if phases >= 4:
            combine_and_attention1(k, routing, logits, h_rows1)
        if phases >= 5:
            route(k, "rt1", 1, logits, h_rows1, routing, k.dispatch1, tile_expert)
        if phases >= 6:
            experts1(k, tile_expert)
        if phases >= 7:
            combine_to_output(k, routing)


def lay_out(inputs):
    import numpy as np

    g = {n: np.asarray(a) for n, a in inputs.items()}
    con = np.ascontiguousarray

    def chunks(w):
        return con(w.reshape(-1, P, w.shape[1]).transpose(1, 0, 2))

    lay = {"x": con(g["L0_attn_query"].reshape(T, D))}
    lay["c_t"] = con(np.stack([chunks(g["L0_c"].T), chunks(g["L1_c"].T)], 1))
    lay["wmod"] = con(np.stack([g["L0_wmod"], g["L1_wmod"]]).reshape(2, KC, P, 6, D)
                      .transpose(0, 3, 2, 1, 4).reshape(12, P, KC * D))
    w = g["L0_attn_Wqkv"].reshape(4, 4, 3, HN, D).transpose(2, 1, 0, 3, 4).reshape(3, D, D)
    lay["wqk"] = con(np.stack([chunks(w[0].T), chunks(w[1].T)], 1))
    lay["wv"] = chunks(w[2].T)
    lay["wproj"] = chunks(g["L0_attn_Wproj"].T)
    lay["bproj"] = con(g["L0_attn_bproj"].reshape(1, D))
    w1 = np.concatenate([g["L0_ffn_sw1"][None], g["L0_ffn_w1"]])
    lay["w1"] = con(w1.reshape(E + 1, KC, P, 4, 4, P).transpose(0, 3, 2, 4, 1, 5).reshape(E + 1, 4, P, 4 * KC * P))
    w2 = np.concatenate([g["L0_ffn_sw2"][None], g["L0_ffn_w2"]])
    lay["w2"] = con(w2.reshape(E + 1, 4, 4, P, D).transpose(0, 1, 3, 2, 4).reshape(E + 1, 4, P, 4 * D))
    wd = np.concatenate([g["L0_ffn_swd"][None], g["L0_ffn_wd"]])
    lay["wd"] = con(wd.reshape(E + 1, KC, P, RANK).transpose(2, 0, 1, 3).reshape(P, E + 1, KC * RANK))
    wu = np.concatenate([g["L0_ffn_swu"][None], g["L0_ffn_wu"]])
    b2 = np.concatenate([g["L0_ffn_sb2"][None], g["L0_ffn_b2"]])
    lay["wu_b2"] = con(np.concatenate([wu, b2[:, None, :]], 1))
    b1 = np.concatenate([g["L0_ffn_sb1"][None], g["L0_ffn_b1"]])
    lay["b1"] = con(b1.reshape(E + 1, FC, P).transpose(2, 0, 1).reshape(P, (E + 1) * FC))
    lay["wr"] = chunks(g["L1_ffn_Wr"])
    wgu = np.stack([g["L1_ffn_Wg"], g["L1_ffn_Wu"]], 2).reshape(E, KC, P, 2, INNER)
    lay["wgu"] = con(wgu.transpose(2, 0, 1, 3, 4).reshape(P, E * KC * 2, INNER))
    whole = INNER // P * P
    lay["wd1"] = con(g["L1_ffn_Wd"][:, :whole].reshape(E, INNER // P, P, D).transpose(2, 0, 1, 3)
                     .reshape(P, E * (INNER // P), D))
    lay["wd1_rest"] = con(g["L1_ffn_Wd"][:, whole:].transpose(1, 0, 2))
    lay["gate_w"] = chunks(g["L0_ffn_gate_w"])
    return lay


def kernel(**inputs):
    import concourse.bacc as bacc
    import numpy as np
    from concourse.bass_utils import run_bass_kernel_spmd

    nc = bacc.Bacc("TRN2", target_bir_lowering=False, num_devices=1)
    arrays = {f"in_{n}": a for n, a in lay_out(inputs).items()}
    ins = {n[3:]: nc.dram_tensor(n, a.shape, mybir.dt.from_np(a.dtype), kind="ExternalInput").ap()
           for n, a in arrays.items()}
    out = nc.dram_tensor("out_0", (B, S, D), F32, kind="ExternalOutput").ap()
    program(nc, ins, out)
    r = run_bass_kernel_spmd(nc, [arrays], core_ids=[0])
    return np.asarray(r.results[0]["out_0"])
```

```python
from contextlib import ExitStack

import concourse.bass as bass
from concourse import mybir

F32 = mybir.dt.float32
F32R = mybir.dt.float32r
I32 = mybir.dt.int32
U32 = mybir.dt.uint32
ALU = mybir.AluOpType
ACT = mybir.ActivationFunctionType
AX = mybir.AxisListType

P = 128
B, S, D = 4, 512, 512
T = B * S
NT = T // P
TB = S // P
KC = D // P
HEADS, HN = 16, 32
QUADS = 4
E = 8
F = 2048
FC = F // P
RANK = 32
CAP = 320
REGION = 2 * CAP
ROWS = T + E * REGION
INNER = 352
TILES1 = 2 * T // P + E - 1
EPS = 1e-5
SA, CA, GA, SB_, CB, GB = range(6)


def flat(ap):
    return ap.rearrange("p a d -> p (a d)")


def tile_of(buf, index):
    if isinstance(index, int):
        return buf[:, index, :]
    return flat(buf[:, bass.ds(index, 1), :])


def batch_loop(eng, body):
    with eng.Fori(0, B - 1) as b:
        body(b, False)
    body(B - 1, True)


def wait_alone(eng, sem, value, passed):
    eng.wait_ge(sem, value)
    eng.sem_inc(passed, 1)


class Core:

    def __init__(self, nc, stack, ins, out):
        self.nc, self.stack, self.ins, self.out, self.sems = nc, stack, ins, out, {}
        self.x = self.sb("x_resid", [P, NT, D])
        self.ident = self.sb("ident", [P, P])
        self.passed = self.sem("waits_passed")
        self.eps = self.sb("eps", [P, 1])
        self.mod_rows = nc.dram_tensor("mod_rows", (2, 6, B, D), F32, kind="Internal").ap()
        self.dispatch = nc.dram_tensor("dispatch0", (ROWS, D), F32, kind="Internal").ap()
        self.expert_out = nc.dram_tensor("expert_out0", (ROWS, D), F32, kind="Internal").ap()
        self.dispatch1 = nc.dram_tensor("dispatch1", (TILES1 * P, D), F32, kind="Internal").ap()
        self.h_rows1 = nc.dram_tensor("h_rows1", (T, D), F32, kind="Internal").ap()
        self.expert_out1 = nc.dram_tensor("expert_out1", (TILES1 * P, D), F32, kind="Internal").ap()

    def sb(self, name, shape, dtype=F32, stack=None):
        return (stack or self.stack).enter_context(self.nc.sbuf_tensor(name, shape, dtype))

    def ps(self, name, shape, stack):
        return stack.enter_context(self.nc.psum_tensor(name, shape, F32))

    def sem(self, name):
        if name not in self.sems:
            self.sems[name] = self.stack.enter_context(self.nc.semaphore(name))
        return self.sems[name]

    def mod_tile(self, layer, which, batch):
        row = self.mod_rows[layer, which]
        row = row[batch:batch + 1, :] if isinstance(batch, int) else row[bass.ds(batch, 1), :]
        return row.broadcast_to([P, D])


def start_and_modulation(k, att):
    RING = 6
    nc, ins = k.nc, k.ins
    x_loaded, c_loaded, att_w_loaded = k.sem("x_loaded"), k.sem("c_loaded"), k.sem("att_w_loaded")
    wmod_loaded = [k.sem(f"wmod_loaded{n}") for n in range(RING)]
    silu_done, rows_ready, rows_done, rows_stored = (
        k.sem("silu_done"), k.sem("mod_psum_ready"), k.sem("mod_rows_done"), k.sem("mod_rows_stored"))
    half_step = k.sem("mod_half_step")
    zero_done, zero_stored = k.sem("zero_done"), k.sem("zero_stored")
    ident_zeroed, consts_done = k.sem("ident_zeroed"), k.sem("consts_done")
    stats_done, var_done, sd_done, rstd_done = k.sem("stats_done"), k.sem("var_done"), k.sem("sd_done"), k.sem("rstd_done")
    with ExitStack() as st:
        wm = k.sb("wmod_sb", [P, RING, KC * D], stack=st)
        ct = k.sb("c_t", [P, 2, KC, B], stack=st)
        ct_silu = k.sb("c_t_silu", [P, 2, KC, B], stack=st)
        rows = k.sb("mod_rows_sb", [P, 4, D], stack=st)
        sign = k.sb("gate_sign", [P, 4, D], stack=st)
        zeros = k.sb("zero_rows", [P, 4 * D], stack=st)
        stats = k.sb("ln1_stats", [P, NT, 6], stack=st)
        sd = k.sb("ln1_sd", [P, NT], stack=st)
        pm = k.ps("mod_psum", [P, 4, D], st)

        def place(n):
            layer, which = divmod(n, 6)
            return 32 * (which % 4), 2 * layer + which // 4

        with nc.Block() as block:
            @block.sync
            def _(sp):
                sp.dma_start(ct[:, :, :, :], ins["c_t"]).then_inc(c_loaded, 16)
                for t in range(0, NT, TB):
                    sp.dma_start(k.x[:, t:t + TB, :],
                                 ins["x"][t * P:(t + TB) * P, :].rearrange("(t p) d -> p t d", p=P)
                                 ).then_inc(x_loaded, 16)
                for n in range(12):
                    if n >= RING:
                        sp.wait_ge(rows_ready, n - RING + 1)
                    sp.dma_start(wm[:, n % RING, :], ins["wmod"][n]).then_inc(wmod_loaded[n % RING], 16)
                for n in range(12):
                    q, bank = place(n)
                    sp.wait_ge(rows_done, n + 1)
                    sp.dma_start(k.mod_rows[n // 6, n % 6], rows[q:q + B, bank, :]).then_inc(rows_stored, 16)
                sp.wait_ge(rows_stored, 16 * 12)

            @block.scalar
            def _(act):
                act.dma_start(att.wqk[:, :, :, :], ins["wqk"]).then_inc(att_w_loaded, 16)
                act.dma_start(att.wv[:, :, :], ins["wv"]).then_inc(att_w_loaded, 16)
                act.wait_ge(c_loaded, 16)
                act.activation(ct_silu[:, :, :, :], ct[:, :, :, :], ACT.Silu).then_inc(silu_done, 1)
                act.wait_ge(zero_done, 1)
                for buf in (k.dispatch[T:, :], k.dispatch1):
                    for r in range(0, buf.shape[0], 4 * P):
                        n = min(4, (buf.shape[0] - r) // P)
                        act.dma_start(buf[r:r + n * P, :].rearrange("(p a) d -> p (a d)", p=P),
                                      zeros[:, 0:n * D]).then_inc(zero_stored, 16)
                act.wait_ge(var_done, NT)
                act.activation(sd[:, :], att.mean_var[:, :, 1], ACT.Sqrt, bias=k.eps[:, 0:1]).then_inc(sd_done, 1)
                act.wait_ge(zero_stored, 16 * (-(-E * REGION // (4 * P)) - (-TILES1 // 4)))
                act.wait_ge(att_w_loaded, 32)

            @block.gpsimd
            def _(pool):
                pool.memset(zeros[:, :], 0.0).then_inc(zero_done, 1)
                pool.memset(k.ident[:, :], 0.0).then_inc(ident_zeroed, 1)
                pool.wait_ge(ident_zeroed, 1)
                pool.affine_select(out=k.ident[:, :], in_=k.ident[:, :], compare_op=ALU.not_equal, fill=1.0,
                                   base=0, pattern=[[-1, P]], channel_multiplier=1).then_inc(consts_done, 1)

            @block.tensor
            def _(pe):
                pe.wait_ge(silu_done, 1)
                for n in range(12):
                    q, bank = place(n)
                    pe.wait_ge(wmod_loaded[n % RING], 16 * (n // RING + 1))
                    for c in range(KC):
                        mm = pe.matmul(pm[q:q + B, bank, :], ct_silu[:, n // 6, c, :],
                                       wm[:, n % RING, c * D:(c + 1) * D], start=(c == 0), stop=(c == KC - 1))
                    mm.then_inc(rows_ready, 1)

            @block.vector
            def _(dve):
                dve.memset(k.eps[:, :], EPS)
                for t in range(NT):
                    dve.wait_ge(x_loaded, 16 * B)
                    dve.bn_stats(stats[:, t, :], k.x[:, t, :]).then_inc(stats_done, 1)
                for t in range(NT):
                    dve.wait_ge(stats_done, t + 1)
                    dve.bn_aggr(att.mean_var[:, t, :], stats[:, t, :]).then_inc(var_done, 1)
                dve.wait_ge(sd_done, 1)
                dve.reciprocal(att.rstd[:, :], sd[:, :]).then_inc(rstd_done, 1)
                dve.wait_ge(rstd_done, 1)
                dve.scalar_tensor_tensor(out=att.shift[:, :], in0=att.mean_var[:, :, 0], scalar=-1.0,
                                         in1=att.rstd[:, :], op0=ALU.mult, op1=ALU.mult)
                halves = 0
                for n in range(12):
                    q, bank = place(n)
                    src, dst, sg = pm[q:q + B, bank, :], rows[q:q + B, bank, :], sign[q:q + B, bank, :]
                    dve.wait_ge(rows_ready, n + 1)
                    if n % 6 in (CA, CB):
                        dve.tensor_scalar(dst, src, 1.0, None, ALU.add).then_inc(rows_done, 1)
                    elif n % 6 in (SA, SB_):
                        dve.tensor_copy(dst, src).then_inc(rows_done, 1)
                    else:
                        dve.tensor_scalar(sg, src, 0.0, 2.0, ALU.is_ge, ALU.mult).then_inc(half_step, 1)
                        dve.wait_ge(half_step, halves + 1)
                        dve.tensor_scalar(sg, sg, -1.0, None, ALU.add).then_inc(half_step, 1)
                        dve.wait_ge(half_step, halves + 2)
                        dve.tensor_tensor(dst, src, sg, ALU.mult).then_inc(half_step, 1)
                        halves += 3
                        dve.wait_ge(half_step, halves)
                        dve.scalar_tensor_tensor(out=dst, in0=dst, scalar=0.25, in1=sg, op0=ALU.max,
                                                 op1=ALU.mult).then_inc(rows_done, 1)


class Attention0:

    def __init__(self, k, st):
        self.wqk = k.sb("wqk_sb", [P, 2, KC, D], stack=st)
        self.wv = k.sb("wv_sb", [P, KC, D], stack=st)
        self.mean_var = k.sb("ln1_mean_var", [P, NT, 2], stack=st)
        self.rstd = k.sb("ln1_rstd", [P, NT], stack=st)
        self.shift = k.sb("ln1_shift", [P, NT], stack=st)


def attention0(k, att, ctx_t):
    nc, ins = k.nc, k.ins
    NORM = float(HN) ** -0.5
    mod_loaded = k.sem("a0_mod_loaded")
    n_centered, n_scaled, h_ready = k.sem("a0_centered"), k.sem("a0_scaled"), k.sem("a0_h_ready")
    transposed = k.sem("a0_h_transposed")
    gen_full = [k.sem(f"a0_gen_full{i}") for i in range(2)]
    gen_free = [k.sem(f"a0_gen_free{i}") for i in range(2)]
    hi_done = k.sem("a0_hi_done")
    scores_full, max_done = k.sem("a0_scores_full"), k.sem("a0_max_done")
    row_full, row_taken = k.sem("a0_max_row_full"), k.sem("a0_max_row_taken")
    st_full, p_ready = k.sem("a0_st_full"), k.sem("a0_p_ready")
    pv_done, ctx_taken, recip_done, ctx_done = (
        k.sem("a0_pv_done"), k.sem("a0_ctx_taken"), k.sem("a0_recip_done"), k.sem("a0_ctx_done"))
    consts = k.sem("a0_consts")

    uses = [("hT", c) for c in range(KC)] + [("q", 0), ("k", 0)] + [("v", t) for t in range(TB)]
    for j in range(QUADS):
        if j + 1 < QUADS:
            uses += [("q", j + 1), ("k", j + 1)]
    G = {u: n for n, u in enumerate(uses)}
    GH = len(uses) // 2
    assert len(uses) % 2 == 0

    with ExitStack() as st:
        mod = k.sb("a0_mod", [P, 2, D], stack=st)
        h = k.sb("a0_h", [P, TB, D], stack=st)
        h_t = k.sb("a0_h_t", [P, KC, S], stack=st)
        v = k.sb("a0_v", [P, TB, D], stack=st)
        qs = k.sb("a0_q_stack", [P, 2, 4, S], F32R, stack=st)
        ks = k.sb("a0_k_stack", [P, 2, 4, S], F32R, stack=st)
        mx = k.sb("a0_max", [P, 16], stack=st)
        prob = k.sb("a0_prob", [P, 8, S], stack=st)
        ones = k.sb("a0_ones", [P, HN], stack=st)
        rec = k.sb("a0_rec", [P, S], stack=st)
        ctx_raw = k.sb("a0_ctx_raw", [P, S], stack=st)
        den_raw = k.sb("a0_den_raw", [P, S], stack=st)
        gen = k.ps("a0_gen", [P, 2, S], st)
        sc = k.ps("a0_scores", [P, 2, S], st)
        scT = k.ps("a0_scores_t", [P, 2, S], st)
        ctx = k.ps("a0_ctx", [P, S], st)
        den = k.ps("a0_den", [P, S], st)

        def wait_full(eng, b, use):
            eng.wait_ge(gen_full[G[use] % 2], b * GH + G[use] // 2 + 1)

        def wait_freed(pe, b, use):
            pe.wait_ge(gen_free[G[use] % 2], b * GH + G[use] // 2)

        def wait_taken(eng, b, use):
            eng.wait_ge(gen_free[G[use] % 2], b * GH + G[use] // 2 + 1)

        with nc.Block() as block:
            @block.sync
            def _(sp):
                with sp.Fori(0, B) as b:
                    sp.wait_ge(h_ready, TB * b)
                    sp.dma_start(mod[:, 0, :], k.mod_tile(0, CA, b)).then_inc(mod_loaded, 16)
                    sp.dma_start(mod[:, 1, :], k.mod_tile(0, SA, b)).then_inc(mod_loaded, 16)

            @block.gpsimd
            def _(pool):
                with pool.Fori(0, B) as b:
                    pool.wait_ge(mod_loaded, 32 * b + 32)
                    for i in range(TB):
                        pool.wait_ge(n_centered, TB * b + i + 1)
                        pool.tensor_tensor(h[:, i, :], h[:, i, :], mod[:, 0, :], ALU.mult).then_inc(n_scaled, 1)
                    for i in range(TB):
                        pool.wait_ge(n_scaled, TB * b + i + 1)
                        pool.tensor_tensor(h[:, i, :], h[:, i, :], mod[:, 1, :], ALU.add).then_inc(h_ready, 1)

            @block.tensor
            def _(pe):
                with pe.Fori(0, B) as b:
                    def project(which, j, chunks):
                        n, g = (0 if which == "q" else 1), G[(which, j)]
                        if 0 in chunks:
                            wait_freed(pe, b, (which, j))
                        for c in chunks:
                            mm = pe.matmul(gen[:, g % 2, :], att.wqk[:, n, c, j * P:(j + 1) * P], h_t[:, c, :],
                                           start=(c == 0), stop=(c == KC - 1))
                        if KC - 1 in chunks:
                            mm.then_inc(gen_full[g % 2], 1)

                    pe.wait_ge(h_ready, TB * b + TB)
                    for c in range(KC):
                        wait_freed(pe, b, ("hT", c))
                        for i in range(TB):
                            mm = pe.transpose(gen[:, G[("hT", c)] % 2, i * P:(i + 1) * P],
                                              h[:, i, c * P:(c + 1) * P], k.ident[:, :])
                        mm.then_inc(gen_full[G[("hT", c)] % 2], 1)
                    wait_taken(pe, b, ("hT", KC - 2))
                    wait_taken(pe, b, ("hT", KC - 1))
                    project("q", 0, range(KC))
                    project("k", 0, range(KC))
                    for t in range(TB):
                        g = G[("v", t)]
                        wait_freed(pe, b, ("v", t))
                        for c in range(KC):
                            mm = pe.matmul(gen[:, g % 2, :], h_t[:, c, t * P:(t + 1) * P], att.wv[:, c, :],
                                           start=(c == 0), stop=(c == KC - 1))
                        mm.then_inc(gen_full[g % 2], 1)
                    for j in range(QUADS):
                        par = j % 2
                        wait_taken(pe, b, ("q", j))
                        wait_taken(pe, b, ("k", j))
                        for a in range(4):
                            for t in range(TB):
                                s = 16 * j + 4 * a + t
                                pe.wait_ge(max_done, 64 * b + max(s - 1, 0))
                                if a == 0 and t < 2:
                                    pe.wait_ge(row_taken, 16 * b + 4 * j)
                                pe.matmul(sc[:, s % 2, :], qs[0:96, par, a, t * P:(t + 1) * P], ks[0:96, par, a, :],
                                          start=True, stop=True).then_inc(scores_full, 1)
                                if t % 2 and j + 1 < QUADS:
                                    project("q" if a < 2 else "k", j + 1, [2 * (a % 2) + t // 2])
                        for a in range(4):
                            pe.wait_ge(max_done, 64 * b + 16 * (j + 1))
                            pe.wait_ge(row_taken, 16 * b + 4 * j + max(a - 1, 0))
                            for t in range(TB):
                                mm = pe.transpose(sc[0:1, a % 2, t * P:(t + 1) * P],
                                                  mx[:, 4 * a + t:4 * a + t + 1], k.ident[:, :])
                            mm.then_inc(row_full, 1)

                        def score_t(t, a):
                            s = 16 * j + 4 * t + a
                            if t == 0:
                                pe.wait_ge(row_taken, 16 * b + 4 * j + a + 1)
                            pe.wait_ge(p_ready, 64 * b + max(s - 1, 0))
                            pe.matmul(scT[:, s % 2, :], ks[:, par, a, t * P:(t + 1) * P], qs[:, par, a, :],
                                      start=True, stop=True).then_inc(st_full, 1)

                        def weigh(t, to):
                            if to is ctx:
                                pe.wait_ge(p_ready, 64 * b + 16 * j + 4 * t + 4)
                                if t == 0:
                                    pe.wait_ge(ctx_taken, 8 * b + 2 * j)
                            for a in range(4):
                                w = v[:, t, j * P + HN * a:j * P + HN * (a + 1)] if to is ctx else ones[:, :]
                                mm = pe.matmul(to[HN * a:HN * (a + 1), :], w, prob[:, 4 * (t % 2) + a, :],
                                               start=(t == 0), stop=(t == TB - 1))
                            mm.then_inc(pv_done, 1)

                        for t in range(TB + 1):
                            for a, to in ((0, ctx), (2, den)):
                                if t < TB:
                                    score_t(t, a)
                                    score_t(t, a + 1)
                                if t > 0:
                                    weigh(t - 1, to)

            @block.scalar
            def _(act):
                def center(b):
                    wait_alone(act, transposed, b, k.passed)
                    for i in range(TB):
                        act.activation(h[:, i, :], tile_of(k.x, b * TB + i), ACT.Identity,
                                       scale=att.rstd[:, bass.ds(b * TB + i, 1)],
                                       bias=att.shift[:, bass.ds(b * TB + i, 1)]).then_inc(n_centered, 1)

                def body(b, last):
                    for c in (1, 3):
                        wait_full(act, b, ("hT", c))
                        act.copy(h_t[:, c, :], gen[:, G[("hT", c)] % 2, :]).then_inc(gen_free[G[("hT", c)] % 2], 1)
                    def split_hi(which, j):
                        stack = qs if which == "q" else ks
                        wait_full(act, b, (which, j))
                        act.wait_ge(st_full, 64 * b + 16 * max(j - 1, 0))
                        for a in range(4):
                            act.activation(stack[0:HN, j % 2, a, :],
                                           gen[HN * a:HN * (a + 1), G[(which, j)] % 2, :],
                                           ACT.Copy).then_inc(hi_done, 1)

                    split_hi("q", 0)
                    split_hi("k", 0)
                    act.wait_ge(pv_done, 32 * b)
                    for t in (1, 3):
                        wait_full(act, b, ("v", t))
                        act.copy(v[:, t, :], gen[:, G[("v", t)] % 2, :]).then_inc(gen_free[G[("v", t)] % 2], 1)

                    for j in range(QUADS):
                        if j + 1 < QUADS:
                            split_hi("q", j + 1)
                        if j == 1 and not last:
                            center(b + 1)
                        for a in range(4):
                            act.wait_ge(row_full, 16 * b + 4 * j + a + 1)
                            act.activation(qs[96:97, j % 2, a, :], sc[0:1, a % 2, :], ACT.Copy,
                                           scale=-1.0).then_inc(row_taken, 1)
                        for t in range(TB):
                            for a in range(4):
                                s = 16 * j + 4 * t + a
                                act.wait_ge(st_full, 64 * b + s + 1)
                                act.wait_ge(pv_done, 32 * b + 2 * max(4 * j + t - 1, 0))
                                act.activation(prob[:, 4 * (t % 2) + a, :], scT[:, s % 2, :], ACT.Exp,
                                               scale=NORM).then_inc(p_ready, 1)
                            if t == 0 and j + 1 < QUADS:
                                split_hi("k", j + 1)
                        act.wait_ge(pv_done, 32 * b + 8 * j + 8)
                        act.wait_ge(ctx_done, 4 * b + j)
                        act.copy(den_raw[:, :], den[:, :]).then_inc(ctx_taken, 1)
                        act.copy(ctx_raw[:, :], ctx[:, :]).then_inc(ctx_taken, 1)

                center(0)
                batch_loop(act, body)

            @block.vector
            def _(dve):
                dve.memset(ones[:, :], 1.0).then_inc(consts, 1)
                dve.memset(qs[96:128, :, :, :].bitcast(F32), 0.0).then_inc(consts, 1)
                dve.memset(ks[96:128, :, :, :].bitcast(F32), 0.0).then_inc(consts, 1)
                dve.wait_ge(consts, 3)
                dve.memset(ks[96:97, :, :, :].bitcast(F32), 1.0).then_inc(consts, 1)
                dve.wait_ge(consts, 4)
                with dve.Fori(0, B) as b:
                    for c in (0, 2):
                        wait_full(dve, b, ("hT", c))
                        dve.tensor_copy(h_t[:, c, :], gen[:, G[("hT", c)] % 2, :]
                                        ).then_inc(gen_free[G[("hT", c)] % 2], 1)
                    wait_full(dve, b, ("hT", 3))
                    dve.nop().then_inc(transposed, 1)
                    def split_lo(which, j):
                        stack, lo, dup = (qs, HN, 2 * HN) if which == "q" else (ks, 2 * HN, HN)
                        g = G[(which, j)]
                        dve.wait_ge(st_full, 64 * b + 16 * max(j - 1, 0))
                        for a in range(4):
                            dve.wait_ge(hi_done, 32 * b + 8 * j + 4 * (which == "k") + a + 1)
                            dve.tensor_copy(stack[dup:dup + HN, j % 2, a, :], stack[0:HN, j % 2, a, :].bitcast(F32))
                            last = dve.tensor_tensor(stack[lo:lo + HN, j % 2, a, :],
                                                     gen[HN * a:HN * (a + 1), g % 2, :],
                                                     stack[0:HN, j % 2, a, :].bitcast(F32), ALU.subtract)
                        last.then_inc(gen_free[g % 2], 1)

                    def normalize(j):
                        dve.wait_ge(ctx_taken, 8 * b + 2 * j + 2)
                        dve.reciprocal(rec[:, :], den_raw[:, :]).then_inc(recip_done, 1)
                        dve.wait_ge(recip_done, 4 * b + j + 1)
                        dve.tensor_tensor(flat(ctx_t[:, j, bass.ds(b, 1), :]), ctx_raw[:, :], rec[:, :],
                                          ALU.mult).then_inc(ctx_done, 1)

                    split_lo("q", 0)
                    split_lo("k", 0)
                    dve.wait_ge(pv_done, 32 * b)
                    for t in (0, 2):
                        wait_full(dve, b, ("v", t))
                        dve.tensor_copy(v[:, t, :], gen[:, G[("v", t)] % 2, :]).then_inc(gen_free[G[("v", t)] % 2], 1)

                    for j in range(QUADS):
                        for s in range(16):
                            dve.wait_ge(scores_full, 64 * b + 16 * j + s + 1)
                            dve.tensor_reduce(mx[:, s:s + 1], sc[:, s % 2, :], AX.X, ALU.max).then_inc(max_done, 1)
                        if j + 1 < QUADS:
                            split_lo("q", j + 1)
                            split_lo("k", j + 1)
                        if j > 0:
                            normalize(j - 1)
                    normalize(QUADS - 1)


class NormPass:

    def __init__(self, k, st, name, *which, sems, before=0):
        self.k, self.which, self.before = k, which, before
        self.mod_loaded = k.sem(f"{name}_mod_loaded")
        self.mod = k.sb(f"{name}_mod", [P, len(which), B, D], stack=st)
        self.delta = k.sb(f"{name}_delta", [P, TB, D], stack=st)
        self.delta_ready, self.gated, self.added = (k.sem(f"{sems}_{s}") for s in ("delta_ready", "gated", "added"))
        if len(which) == 1:
            return
        self.h = k.sb(f"{name}_h", [P, TB, D], stack=st)
        self.stats = k.sb(f"{name}_stats", [P, TB, 6], stack=st)
        self.mean_var = k.sb(f"{name}_mean_var", [P, TB, 2], stack=st)
        self.sd = k.sb(f"{name}_sd", [P, TB], stack=st)
        self.rstd = k.sb(f"{name}_rstd", [P, TB], stack=st)
        self.stats_done, self.var_done, self.sd_done, self.rstd_done, self.centered, self.scaled, self.h_ready = (
            k.sem(f"{sems}_{s}") for s in ("stats_done", "var_done", "sd_done", "rstd_done", "centered", "scaled", "h_ready"))

    def count(self, b, tiles=0):
        return TB * (self.before + b) + tiles

    def load(self, eng):
        for n, (layer, which) in enumerate(self.which):
            for b in range(B):
                eng.dma_start(self.mod[:, n, b, :], self.k.mod_tile(layer, which, b)).then_inc(self.mod_loaded, 16)

    def mod_of(self, n, b):
        return self.mod[:, n, b, :] if isinstance(b, int) else flat(self.mod[:, n, bass.ds(b, 1), :])

    def gate(self, pool, b):
        pool.wait_ge(self.mod_loaded, 16 * len(self.which) * B)
        for i in range(TB):
            wait_alone(pool, self.delta_ready, self.count(b, i + 1), self.k.passed)
            pool.tensor_tensor(self.delta[:, i, :], self.delta[:, i, :], self.mod_of(0, b),
                               ALU.mult).then_inc(self.gated, 1)

    def add(self, dve, b):
        for i in range(TB):
            x = tile_of(self.k.x, b * TB + i)
            dve.wait_ge(self.gated, self.count(b, i + 1))
            dve.tensor_tensor(x, x, self.delta[:, i, :], ALU.add).then_inc(self.added, 1)

    def statistics(self, dve, b):
        wait_alone(dve, self.added, self.count(b, TB), self.k.passed)
        for i in range(TB):
            dve.bn_stats(self.stats[:, i, :], tile_of(self.k.x, b * TB + i)).then_inc(self.stats_done, 1)
        wait_alone(dve, self.stats_done, self.count(b, TB), self.k.passed)
        for i in range(TB):
            dve.bn_aggr(self.mean_var[:, i, :], self.stats[:, i, :]).then_inc(self.var_done, 1)

    def root(self, act, b):
        act.wait_ge(self.var_done, self.count(b, TB))
        act.activation(self.sd[:, :], self.mean_var[:, :, 1], ACT.Sqrt, bias=self.k.eps[:, 0:1]).then_inc(self.sd_done, 1)

    def center(self, dve, b):
        dve.wait_ge(self.sd_done, self.before + b + 1)
        dve.reciprocal(self.rstd[:, :], self.sd[:, :]).then_inc(self.rstd_done, 1)
        dve.wait_ge(self.rstd_done, self.before + b + 1)
        for i in range(TB):
            dve.tensor_scalar(self.h[:, i, :], tile_of(self.k.x, b * TB + i), self.mean_var[:, i, 0:1],
                              self.rstd[:, i:i + 1], ALU.subtract, ALU.mult).then_inc(self.centered, 1)

    def scale(self, pool, b):
        for i in range(TB):
            wait_alone(pool, self.centered, self.count(b, i + 1), self.k.passed)
            pool.tensor_tensor(self.h[:, i, :], self.h[:, i, :], self.mod_of(1, b), ALU.mult).then_inc(self.scaled, 1)

    def shift(self, dve, b):
        for i in range(TB):
            dve.wait_ge(self.scaled, self.count(b, i + 1))
            dve.tensor_tensor(self.h[:, i, :], self.h[:, i, :], self.mod_of(2, b), ALU.add).then_inc(self.h_ready, 1)


class RouterPass:

    def __init__(self, k, st, name, w_name, norm, logits, before=0):
        self.k, self.norm, self.logits, self.w_name, self.before = k, norm, logits, w_name, before
        self.w_loaded = k.sem(f"{name}_w_loaded")
        self.w = k.sb(f"{name}_w", [P, KC, E], stack=st)
        self.h_t = k.sb(f"{name}_h_t", [P, 2, KC, P], stack=st)
        self.t_psum = k.ps(f"{name}_t_psum", [P, 2, KC, P], st)
        self.l_psum = k.ps(f"{name}_l_psum", [P, TB, E], st)
        self.t_full, self.t_taken, self.tile_routed, self.logits_taken = (
            k.sem("router_t_full"), k.sem("router_t_taken"), k.sem("router_tile_routed"), k.sem("router_logits_taken"))

    def count(self, b, tiles=0):
        return TB * (self.before + b) + tiles

    def load(self, eng):
        eng.dma_start(self.w[:, :, :], self.k.ins[self.w_name]).then_inc(self.w_loaded, 16)

    def tensor(self, pe, b):
        pe.wait_ge(self.w_loaded, 16)

        def logits_of(i):
            pe.wait_ge(self.t_taken, self.count(b, i + 1))
            for c in range(KC):
                mm = pe.matmul(self.l_psum[:, i, :], self.h_t[:, i % 2, c, :], self.w[:, c, :],
                               start=(c == 0), stop=(c == KC - 1))
            mm.then_inc(self.tile_routed, 1)

        for i in range(TB):
            pe.wait_ge(self.norm.h_ready, self.norm.count(b, i + 1))
            pe.wait_ge(self.t_taken, self.count(b, max(i - 1, 0)))
            for c in range(KC):
                mm = pe.transpose(self.t_psum[:, i % 2, c, :], self.norm.h[:, i, c * P:(c + 1) * P], self.k.ident[:, :])
            mm.then_inc(self.t_full, 1)
            if i == 0:
                pe.wait_ge(self.logits_taken, self.before + b)
            else:
                logits_of(i - 1)
        logits_of(TB - 1)

    def scalar(self, act, b):
        for i in range(TB):
            act.wait_ge(self.t_full, self.count(b, i + 1))
            act.wait_ge(self.tile_routed, self.count(b, max(i - 1, 0)))
            act.copy(self.h_t[:, i % 2, :, :], self.t_psum[:, i % 2, :, :]).then_inc(self.t_taken, 1)
        act.wait_ge(self.tile_routed, self.count(b, TB))
        act.copy(self.logits[:, bass.ds(b * TB, TB), :], self.l_psum[:, :, :]).then_inc(self.logits_taken, 1)

    def wait_h_free(self, dve, b):
        dve.wait_ge(self.t_full, self.count(b))


def project_and_norm0(k, ctx_t, logits, h_rows):
    nc, ins = k.nc, k.ins
    w_loaded, ctx_ready, proj_full, stored = (
        k.sem("p_w_loaded"), k.sem("p_ctx_ready"), k.sem("p_proj_full"), k.sem("p_h_stored"))
    with ExitStack() as st:
        w = k.sb("wproj_sb", [P, KC, D], stack=st)
        bias = k.sb("bproj_tile", [P, D], stack=st)
        cj = k.sb("ctx_batch", [P, KC, S], stack=st)
        pp = k.ps("proj_psum", [P, TB, D], st)
        norm = NormPass(k, st, "n0", (0, GA), (0, CB), (0, SB_), sems="norm_a")
        router = RouterPass(k, st, "r0", "gate_w", norm, logits)

        with nc.Block() as block:
            @block.sync
            def _(sp):
                sp.dma_start(w[:, :, :], ins["wproj"]).then_inc(w_loaded, 16)
                sp.dma_start(bias[:, :], ins["bproj"].broadcast_to([P, D])).then_inc(w_loaded, 16)
                norm.load(sp)
                router.load(sp)
                with sp.Fori(0, B) as b:
                    for i in range(TB):
                        sp.wait_ge(norm.h_ready, norm.count(b, i + 1))
                        sp.dma_start(h_rows(b, i), norm.h[:, i, :]).then_inc(stored, 16)
                sp.wait_ge(stored, 16 * NT)

            @block.gpsimd
            def _(pool):
                with pool.Fori(0, B) as b:
                    norm.gate(pool, b)
                    norm.scale(pool, b)

            @block.tensor
            def _(pe):
                def project(b, first):
                    pe.wait_ge(ctx_ready, b + 1)
                    for i in range(TB):
                        if not first:
                            pe.wait_ge(norm.delta_ready, norm.count(b - 1, i + 1))
                        for c in range(KC):
                            mm = pe.matmul(pp[:, i, :], cj[:, c, i * P:(i + 1) * P], w[:, c, :],
                                           start=(c == 0), stop=(c == KC - 1))
                        mm.then_inc(proj_full, 1)

                def body(b, last):
                    if not last:
                        project(b + 1, False)
                    router.tensor(pe, b)

                pe.wait_ge(w_loaded, 32)
                project(0, True)
                batch_loop(pe, body)

            @block.scalar
            def _(act):
                act.copy(cj[:, :, :], ctx_t[:, 0, :, :]).then_inc(ctx_ready, 1)

                def body(b, last):
                    if not last:
                        act.wait_ge(proj_full, TB * b + TB)
                        act.copy(cj[:, :, :], ctx_t[:, bass.ds(b + 1, 1), :, :].rearrange("p a c s -> p (a c) s")
                                 ).then_inc(ctx_ready, 1)
                    norm.root(act, b)
                    router.scalar(act, b)

                batch_loop(act, body)

            @block.vector
            def _(dve):
                dve.wait_ge(w_loaded, 32)
                dve.wait_ge(norm.mod_loaded, 16 * 3 * B)
                with dve.Fori(0, B) as b:
                    for i in range(TB):
                        dve.wait_ge(proj_full, TB * b + i + 1)
                        dve.tensor_tensor(norm.delta[:, i, :], pp[:, i, :], bias[:, :], ALU.add
                                          ).then_inc(norm.delta_ready, 1)
                    norm.add(dve, b)
                    norm.statistics(dve, b)
                    router.wait_h_free(dve, b)
                    dve.wait_ge(stored, 16 * TB * b)
                    norm.center(dve, b)
                    norm.shift(dve, b)


class Routing:

    def __init__(self, k, name, stack):
        self.weight = k.sb(f"{name}_weight", [P, 2, NT], stack=stack)
        self.steps = 0
        self.scatter_row = k.sb(f"{name}_scatter_row", [P, 2, NT], U32, stack=stack)
        self.gather_row = k.sb(f"{name}_gather_row", [P, 2, NT], U32, stack=stack)


def route(k, name, layer, logits, h_rows, routing, dispatch, tile_expert=None, weights=None):
    nc = k.nc
    RING = 4
    exp_in, exp_out, onehot_done, counted = (
        k.sem("route_exp_in"), k.sem("route_exp_out"), k.sem("route_onehot_done"), k.sem("route_counted"))
    step_done, rows_done = k.sem("route_step"), k.sem("route_rows_done")
    scattered = [k.sem(f"route_scattered{i}") for i in range(RING)]
    h_loaded = [k.sem(f"route_h_loaded{i}") for i in range(RING)]
    iota_done, consts = k.sem(f"{name}_iota_done"), k.sem(f"{name}_consts")
    HUGE = float(1 << 20)
    NK = 2 * E * NT
    with ExitStack() as st:
        def sb(n, shape, dtype=F32):
            return k.sb(f"{name}_{n}", shape, dtype, stack=st)

        h = sb("h_ring", [P, RING, D])
        before = sb("before", [P, P])
        ones = sb("ones", [P, P])
        running = sb("running", [P, 2 * E, NT])
        iotas = sb("iotas", [P, 2 * E + TILES1], I32)
        iotas_f = sb("iotas_f", [P, 2 * E + TILES1])
        stat = sb("stat", [P, 4, NT])
        best = sb("best", [P, NT, 8])
        index = sb("index", [P, NT, 8], U32)
        index_f = sb("index_f", [P, NT, 8])
        onehot = sb("onehot", [P, 2, E, NT])
        total = sb("total", [P, 2, E, NT])
        incl = sb("incl", [P, 2, E, NT])
        place = sb("place", [P, 2, E, NT])
        prod = sb("prod", [P, 2, E, NT])
        pos = sb("pos", [P, 2, NT])
        base = sb("base", [P, 2, E])
        row = sb("row", [P, 2, NT])
        keep = sb("keep", [P, 2, NT])
        counts = sb("counts", [P, 4, E])
        counts_i = sb("counts_i", [P, E], I32)
        cmp = sb("cmp", [P, TILES1, E])
        te = sb("te", [P, TILES1])
        cp = k.ps(f"{name}_count_psum", [P, 2, NK], st)

        def over_e(ap):
            return ap.rearrange("p (t a) -> p t a", a=1).broadcast_to([P, NT, E])

        def ket(ap):
            return ap.rearrange("p k e t -> p (k e) t")

        with nc.Block() as block:
            @block.sync
            def _(sp):
                for t in range(NT):
                    if t >= RING:
                        sp.wait_ge(scattered[t % RING], 16 * 2 * (NT // RING * layer + t // RING))
                    sp.dma_start(h[:, t % RING, :], h_rows(t // TB, t % TB)).then_inc(h_loaded[t % RING], 16)

            @block.gpsimd
            def _(pool):
                pool.iota(iotas[:, 0:E], [[1, E]], base=0, channel_multiplier=0).then_inc(iota_done, 1)
                pool.wait_ge(iota_done, 1)
                pool.iota(iotas[:, E:2 * E], [[REGION, E]], base=T, channel_multiplier=0).then_inc(iota_done, 1)
                pool.wait_ge(iota_done, 2)
                pool.iota(iotas[:, 2 * E:], [[P, TILES1]], base=0, channel_multiplier=0).then_inc(iota_done, 1)
                pool.memset(ones[:, :], 1.0).then_inc(consts, 1)
                pool.memset(before[:, :], 1.0).then_inc(consts, 1)
                pool.memset(running[:, :, :], 1.0).then_inc(consts, 1)
                pool.wait_ge(consts, 3)
                pool.memset(running[:, :, 0:1], 0.0).then_inc(consts, 1)
                pool.affine_select(out=before[:, :], in_=before[:, :], compare_op=ALU.is_gt, fill=0.0,
                                   base=0, pattern=[[1, P]], channel_multiplier=-1).then_inc(consts, 1)
                pool.wait_ge(rows_done, layer + 1)
                for t in range(NT):
                    pool.wait_ge(h_loaded[t % RING], 16 * (NT // RING * layer + t // RING + 1))
                    for c in range(2):
                        pool.indirect_dma_start(
                            out=dispatch, out_offset=bass.IndirectOffsetOnAxis(ap=routing.scatter_row[:, c, t:t + 1], axis=0),
                            in_=h[:, t % RING, :], in_offset=None, bounds_check=dispatch.shape[0] - 1, oob_is_err=False,
                        ).then_inc(scattered[t % RING], 16)
                for s in scattered:
                    pool.wait_ge(s, 16 * 2 * (NT // RING) * (layer + 1))

            @block.scalar
            def _(act):
                if weights:
                    weights.load(act)
                act.wait_ge(exp_in, layer + 1)
                act.activation(logits[:, :, :], logits[:, :, :], ACT.Exp).then_inc(exp_out, 1)

            @block.tensor
            def _(pe):
                pe.wait_ge(consts, 5)
                pe.wait_ge(onehot_done, 2 * (layer + 1))
                pe.matmul(cp[:, 0, :], before[:, :], onehot.rearrange("p k e t -> p (k e t)"), start=True, stop=True)
                pe.matmul(cp[:, 1, :], ones[:, :], onehot.rearrange("p k e t -> p (k e t)"), start=True,
                          stop=True).then_inc(counted, 1)

            @block.vector
            def _(dve):
                def step(ins):
                    routing.steps += 1
                    ins.then_inc(step_done, 1)
                    dve.wait_ge(step_done, routing.steps)

                dve.wait_ge(iota_done, 3)
                step(dve.tensor_copy(iotas_f[:, :], iotas[:, :]))
                top, total_p, inv, both = (stat[:, n, :] for n in range(4))
                step(dve.tensor_reduce(top, logits[:, :, :], AX.X, ALU.max))
                dve.tensor_tensor(logits[:, :, :], logits[:, :, :], over_e(top), ALU.subtract).then_inc(exp_in, 1)
                dve.wait_ge(exp_out, layer + 1)
                step(dve.tensor_reduce(total_p, logits[:, :, :], AX.X, ALU.add))
                step(dve.reciprocal(inv, total_p))
                step(dve.tensor_tensor(logits[:, :, :], logits[:, :, :], over_e(inv), ALU.mult))
                for t in range(NT):
                    last = dve.max(best[:, t, :], logits[:, t, :])
                step(last)
                for t in range(NT):
                    last = dve.max_index(index[:, t, :], best[:, t, :], logits[:, t, :])
                step(last)
                step(dve.tensor_copy(index_f[:, :, :], index[:, :, :]))
                for c in range(2):
                    ids = iotas_f[:, 0:E].rearrange("p (a e) -> p a e", a=1).broadcast_to([P, NT, E])
                    dve.tensor_tensor(onehot[:, c, :, :].rearrange("p e t -> p t e"), ids,
                                      over_e(index_f[:, :, c]), ALU.is_equal).then_inc(onehot_done, 1)
                dve.wait_ge(counted, layer + 1)
                dve.wait_ge(consts, 5)
                step(dve.tensor_copy(total.rearrange("p k e t -> p (k e t)"), cp[:, 1, :]))
                step(dve.tensor_tensor_scan(incl.rearrange("p k e t -> p (k e t)"),
                                            running.rearrange("p a t -> p (a t)"),
                                            total.rearrange("p k e t -> p (k e t)"), 0.0, ALU.mult, ALU.add))
                step(dve.tensor_tensor(ket(place), ket(incl), ket(total), ALU.subtract))
                step(dve.tensor_tensor(place.rearrange("p k e t -> p (k e t)"),
                                       place.rearrange("p k e t -> p (k e t)"), cp[:, 0, :], ALU.add))
                step(dve.tensor_tensor(ket(prod), ket(onehot), ket(place), ALU.mult))
                for c in range(2):
                    step(dve.tensor_reduce(pos[:, c, :], prod[:, c, :, :].rearrange("p e t -> p t e"), AX.X, ALU.add))
                n_first, n_second = incl[:, 0, :, NT - 1], incl[:, 1, :, NT - 1]
                if layer == 0:
                    step(dve.tensor_copy(base[:, 0, :], iotas_f[:, E:2 * E]))
                    step(dve.tensor_scalar(counts[:, 0, :], n_first, float(CAP), None, ALU.min))
                    step(dve.tensor_tensor(base[:, 1, :], base[:, 0, :], counts[:, 0, :], ALU.add))
                else:
                    step(dve.tensor_tensor(counts[:, 0, :], n_first, n_second, ALU.add))
                    step(dve.tensor_scalar(counts_i[:, :], counts[:, 0, :], float(P - 1), None, ALU.add))
                    step(dve.tensor_scalar(counts_i[:, :], counts_i[:, :], P.bit_length() - 1, None,
                                           ALU.logical_shift_right))
                    step(dve.tensor_copy(counts[:, 1, :], counts_i[:, :]))
                    step(dve.tensor_tensor_scan(counts[:, 2, :], ones[:, 0:E], counts[:, 1, :], 0.0, ALU.mult, ALU.add))
                    step(dve.tensor_tensor(counts[:, 3, :], counts[:, 2, :], counts[:, 1, :], ALU.subtract))
                    step(dve.tensor_scalar(base[:, 0, :], counts[:, 3, :], float(P), None, ALU.mult))
                    step(dve.tensor_tensor(base[:, 1, :], base[:, 0, :], n_first, ALU.add))
                    tiles = iotas_f[:, 2 * E:].rearrange("p (t a) -> p t a", a=1).broadcast_to([P, TILES1, E])
                    starts = base[:, 0, :].rearrange("p (a e) -> p a e", a=1).broadcast_to([P, TILES1, E])
                    step(dve.tensor_tensor(cmp[:, :, :], tiles, starts, ALU.is_ge))
                    step(dve.tensor_reduce(te[:, :], cmp[:, :, :], AX.X, ALU.add))
                    step(dve.tensor_scalar(tile_expert[:, :], te[:, :], -1.0, None, ALU.add))
                step(dve.tensor_tensor(ket(prod), ket(onehot),
                                       base.rearrange("p k (e a) -> p (k e) a", a=1).broadcast_to([P, 2 * E, NT]),
                                       ALU.mult))
                for c in range(2):
                    step(dve.tensor_reduce(row[:, c, :], prod[:, c, :, :].rearrange("p e t -> p t e"), AX.X, ALU.add))
                step(dve.tensor_tensor(row[:, :, :], row[:, :, :], pos[:, :, :], ALU.add))
                w = routing.weight
                if layer == 0:
                    step(dve.tensor_scalar(keep[:, :, :], pos[:, :, :], float(CAP), None, ALU.is_lt))
                    for c in range(2):
                        step(dve.tensor_tensor(w[:, c, :], best[:, :, c], keep[:, c, :], ALU.mult))
                    step(dve.tensor_tensor(pos[:, :, :], row[:, :, :], keep[:, :, :], ALU.mult))
                    step(dve.tensor_copy(routing.gather_row[:, :, :], pos[:, :, :]))
                    step(dve.tensor_scalar(keep[:, :, :], keep[:, :, :], -HUGE, HUGE, ALU.mult, ALU.add))
                    step(dve.tensor_tensor(row[:, :, :], row[:, :, :], keep[:, :, :], ALU.add))
                else:
                    step(dve.tensor_tensor(both, best[:, :, 0], best[:, :, 1], ALU.add))
                    step(dve.reciprocal(inv, both))
                    for c in range(2):
                        step(dve.tensor_tensor(w[:, c, :], best[:, :, c], inv, ALU.mult))
                    step(dve.tensor_copy(routing.gather_row[:, :, :], row[:, :, :]))
                dve.tensor_copy(routing.scatter_row[:, :, :], row[:, :, :]).then_inc(rows_done, 1)


def experts0(k):
    nc, ins = k.nc, k.ins
    STEPS = FC + 1
    GROUP = 4
    GROUPS = FC // GROUP
    HALF = REGION // 2

    def sem(n):
        return k.sem(f"e0_{n}")

    small_loaded, x_loaded, branch_loaded = sem("small_loaded"), sem("x_loaded"), sem("branch_loaded")
    w_loaded = [sem(f"w_loaded{i}") for i in range(2)]
    xt_full, xt5_full, xt_hi, xt5_hi, xt_split = (
        sem("xt_full"), sem("xt5_full"), sem("xt_hi"), sem("xt5_hi"), sem("xt_split"))
    branch_hi, branch_split, w1_hi, w1_split, w2_hi, w2_split = (
        sem("branch_hi"), sem("branch_split"), sem("w1_hi"), sem("w1_split"), sem("w2_hi"), sem("w2_split"))
    h_full, gelu_done, g_hi, g_split = sem("h_full"), sem("gelu_done"), sem("g_hi"), sem("g_split")
    y_done, y_taken, y_stored, consts = sem("y_done"), sem("y_taken"), sem("y_stored"), sem("consts")

    with ExitStack() as st:
        def sb(n, shape, dtype=F32):
            return k.sb(f"e0_{n}", shape, dtype, stack=st)

        x_raw = sb("x_raw", [P, 5, D])
        xh, xl = sb("x_hi", [P, KC, REGION], F32R), sb("x_lo", [P, KC, REGION], F32R)
        w1_raw, w2_raw = sb("w1_raw", [P, 2, GROUP, KC * P]), sb("w2_raw", [P, 2, GROUP, D])
        w1h, w1l = sb("w1_hi", [P, 2, KC, P], F32R), sb("w1_lo", [P, 2, KC, P], F32R)
        w2h, w2l = sb("w2_hi", [P, 2, D], F32R), sb("w2_lo", [P, 2, D], F32R)
        g_raw = sb("g_raw", [P, 2, REGION])
        gh, gl = sb("g_hi", [P, 2, REGION], F32R), sb("g_lo", [P, 2, REGION], F32R)
        a_raw = sb("branch_g_raw", [RANK, REGION])
        ah, al = sb("branch_g_hi", [P, REGION], F32R), sb("branch_g_lo", [P, REGION], F32R)
        wub_raw = sb("wu_b2_raw", [RANK + 1, D])
        wubh, wubl = sb("wu_b2_hi", [P, D], F32R), sb("wu_b2_lo", [P, D], F32R)
        wd_raw = sb("wd_raw", [P, E + 1, KC * RANK])
        wdh, wdl = sb("wd_hi", [P, KC, RANK], F32R), sb("wd_lo", [P, KC, RANK], F32R)
        b1 = sb("b1_sb", [P, (E + 1) * FC])
        y_sb = sb("y_sb", [P, 5, D])
        y = k.ps("e0_y", [P, 5, D], st)
        hb = k.ps("e0_h", [P, 3, S], st)

        def region(rows, v, tiles):
            if tiles == 4:
                return rows[0:T, :].rearrange("(r t p) d -> r p t d", r=B, p=P)[bass.ds(v, 1)].rearrange("a p t d -> (a p) t d")
            return rows[T:, :].rearrange("(r t p) d -> r p t d", r=E, p=P)[bass.ds(v - B, 1)].rearrange("a p t d -> (a p) t d")

        def splits(v, tiles):
            return 4 * v if tiles == 4 else 5 * v - B

        def of_expert(ap, w):
            if isinstance(w, int):
                return ap[w]
            return ap[bass.ds(w, 1)].rearrange("a p n -> (a p) n")

        def loops(eng, body):
            with eng.Fori(0, B - 1) as v:
                body(v, 0, 4, (0, 4))
            body(B - 1, 0, 4, (1, 5))
            with eng.Fori(B, B + E - 1) as v:
                body(v, v - (B - 1), 5, (v - (B - 2), 5))
            body(B + E - 1, E, 5, None)

        def half_of(tiles, half):
            n = tiles * P // 2
            return n, slice(half * n, (half + 1) * n)

        def order(tiles):
            return (0, 1, 2, 3) if tiles == 4 else (0, 1, None, 2, 3)

        with nc.Block() as block:
            @block.sync
            def _(sp):
                sp.dma_start(wd_raw[:, :, :], ins["wd"]).then_inc(small_loaded, 16)
                sp.dma_start(b1[:, :], ins["b1"]).then_inc(small_loaded, 16)

                def load_x(v, w, tiles):
                    sp.dma_start(x_raw[:, 0:tiles, :], region(k.dispatch, v, tiles)).then_inc(x_loaded, 16)
                    sp.dma_start(wub_raw[:, :], of_expert(ins["wu_b2"], w)).then_inc(branch_loaded, 16)

                def body(v, w, tiles, after):
                    for g in range(GROUPS):
                        done = FC * v + (GROUP * (g - 1) if g >= 2 else 0)
                        sp.wait_ge(w1_split, done)
                        sp.wait_ge(w2_split, done)
                        for raw, name in ((w1_raw, "w1"), (w2_raw, "w2")):
                            sp.dma_start(raw[:, g % 2, :, :].rearrange("p c n -> p (c n)"),
                                         of_expert(ins[name][:, g], w)).then_inc(w_loaded[g % 2], 16)
                        if g == 1 and after:
                            sp.wait_ge(xt_split, splits(v, tiles) + tiles)
                            sp.wait_ge(branch_split, 2 * v + 2)
                            load_x(v + 1, *after)

                load_x(0, 0, 4)
                loops(sp, body)

            def wait_weights(eng, v, c):
                g = c // GROUP
                eng.wait_ge(w_loaded[g % 2], 32 * (GROUPS // 2 * v + g // 2 + 1))

            @block.gpsimd
            def _(pool):
                def body(v, w, tiles, after):
                    for c in range(FC):
                        pool.wait_ge(w2_hi, FC * v + c + 1)
                        pool.tensor_tensor(w2l[:, c % 2, :], w2_raw[:, c // GROUP % 2, c % GROUP, :],
                                           w2h[:, c % 2, :].bitcast(F32), ALU.subtract).then_inc(w2_split, 1)

                loops(pool, body)

            @block.tensor
            def _(pe):
                def turn(v, tiles, c, first=False):
                    before = splits(v, tiles)
                    if c == 0:
                        pe.wait_ge(x_loaded, 16 * v + 16)
                        if not first:
                            pe.wait_ge(gelu_done, 2 * STEPS * v - 2)
                    elif c in (None, 1):
                        if not first:
                            pe.wait_ge(gelu_done, 2 * STEPS * v)
                    else:
                        pe.wait_ge(xt_split, before + c - 1)
                    if c is None:
                        for n in range(KC):
                            mm = pe.transpose(hb[:, 0, n * P:(n + 1) * P], x_raw[:, 4, n * P:(n + 1) * P], k.ident[:, :])
                        mm.then_inc(xt5_full, 1)
                    else:
                        for t in range(4):
                            mm = pe.transpose(hb[:, 1 + c % 2, t * P:(t + 1) * P],
                                              x_raw[:, t, c * P:(c + 1) * P], k.ident[:, :])
                        mm.then_inc(xt_full, 1)

                def body(v, w, tiles, after):
                    def hidden(a):
                        width = RANK if a == 0 else P
                        if a == 0:
                            pe.wait_ge(xt_split, splits(v, tiles) + tiles)
                            pe.wait_ge(branch_split, 2 * v + 2)
                            wh, wl = wdh, wdl
                        else:
                            pe.wait_ge(w1_split, FC * v + a)
                            wh, wl = w1h[:, (a - 1) % 2, :, :], w1l[:, (a - 1) % 2, :, :]
                        for half in range(2):
                            n, rows = half_of(tiles, half)
                            pe.wait_ge(gelu_done, 2 * STEPS * v + max(2 * a + half - 2, 0))
                            out = hb[0:width, (2 * a + half) % 3, 0:n]
                            for c in range(KC):
                                pe.matmul(out, wh[:, c, :], xh[:, c, rows], start=(c == 0), stop=False)
                                pe.matmul(out, wh[:, c, :], xl[:, c, rows], start=False, stop=False)
                                mm = pe.matmul(out, wl[:, c, :], xh[:, c, rows], start=False, stop=(c == KC - 1))
                            mm.then_inc(h_full, 1)

                    def output(a, turns={}):
                        if a == 0:
                            pe.wait_ge(y_taken, v)
                            sh, sl, wh, wl = ah, al, wubh[:, :], wubl[:, :]
                        else:
                            pe.wait_ge(w2_split, FC * v + a)
                            i = (a - 1) % 2
                            sh, sl, wh, wl = gh[:, a % 2, :], gl[:, a % 2, :], w2h[:, i, :], w2l[:, i, :]
                        pe.wait_ge(g_split, STEPS * v + a + 1)
                        for t in range(tiles):
                            tile = slice(t * P, (t + 1) * P)
                            pe.matmul(y[:, t, :], sh[:, tile], wh, start=(a == 0), stop=False)
                            pe.matmul(y[:, t, :], sh[:, tile], wl, start=False, stop=False)
                            mm = pe.matmul(y[:, t, :], sl[:, tile], wh, start=False, stop=(a == STEPS - 1))
                            if t == tiles - 1:
                                mm.then_inc(y_done, 1)
                            for c in turns.get(t, []):
                                turn(v + 1, after[1], c)

                    hidden(0)
                    for a in range(1, STEPS):
                        hidden(a)
                        if a < STEPS - 1 or not after:
                            output(a - 1)
                    if not after:
                        output(STEPS - 1)
                        return
                    turn(v + 1, after[1], 0)
                    output(STEPS - 2, {1: [1], 3: [None] if after[1] == 5 else []})
                    output(STEPS - 1, {0: [2], 2: [3]})

                for c in range(KC):
                    turn(0, 4, c, first=True)
                loops(pe, body)

            @block.scalar
            def _(act):
                def take_x(v, tiles):
                    for c in order(tiles):
                        if c is None:
                            act.wait_ge(xt5_full, v - (B - 1))
                            act.activation(xh[:, :, 4 * P:], hb[:, 0, :].rearrange("p (c n) -> p c n", c=KC), ACT.Copy).then_inc(xt5_hi, 1)
                        else:
                            act.wait_ge(xt_full, KC * v + c + 1)
                            act.activation(xh[:, c, 0:4 * P], hb[:, 1 + c % 2, :], ACT.Copy).then_inc(xt_hi, 1)

                def body(v, w, tiles, after):
                    for a in range(STEPS):
                        if a > 0:
                            c = a - 1
                            wait_weights(act, v, c)
                            act.wait_ge(y_done, STEPS * v + (c if c >= 2 else 0))
                            act.activation(w2h[:, c % 2, :], w2_raw[:, c // GROUP % 2, c % GROUP, :],
                                           ACT.Copy).then_inc(w2_hi, 1)
                        act.wait_ge(g_split, STEPS * v + max(a - 1, 0))
                        dst = a_raw[:, :] if a == 0 else g_raw[:, a % 2, :]
                        width = RANK if a == 0 else P
                        bias = 0.0 if a == 0 else (b1[:, w * FC + a - 1:w * FC + a] if isinstance(w, int)
                                                   else b1[:, bass.ds(w * FC + (a - 1), 1)])
                        if a == 1:
                            act.wait_ge(small_loaded, 32)
                        for half in range(2):
                            n, rows = half_of(tiles, half)
                            wait_alone(act, h_full, 2 * (STEPS * v + a) + half + 1, k.passed)
                            act.activation(dst[:, rows], hb[0:width, (2 * a + half) % 3, 0:n], ACT.Gelu,
                                           bias=bias).then_inc(gelu_done, 1)
                    if after:
                        take_x(v + 1, after[1])
                    act.wait_ge(y_done, STEPS * (v + 1))
                    act.wait_ge(y_stored, 16 * v)
                    for t in range(tiles):
                        last = act.copy(y_sb[:, t, :], y[:, t, :])
                    last.then_inc(y_taken, 1)
                    act.wait_ge(y_taken, v + 1)
                    act.dma_start(region(k.expert_out, v, tiles), y_sb[:, 0:tiles, :]).then_inc(y_stored, 16)

                take_x(0, 4)
                loops(act, body)
                act.wait_ge(y_stored, 16 * (B + E))

            @block.vector
            def _(dve):
                for buf in (ah, al, wubh, wubl):
                    dve.memset(buf[32:64, :].bitcast(F32), 0.0).then_inc(consts, 1)
                    dve.memset(buf[64:128, :].bitcast(F32), 0.0).then_inc(consts, 1)
                dve.wait_ge(consts, 8)
                dve.memset(ah[32:33, :].bitcast(F32), 1.0).then_inc(consts, 1)
                dve.wait_ge(small_loaded, 32)
                dve.wait_ge(consts, 9)

                def split_branch(v, w):
                    dve.wait_ge(branch_loaded, 16 * v + 16)
                    wd = flat(wd_raw[:, bass.ds(w, 1), :]) if not isinstance(w, int) else wd_raw[:, w, :]
                    wd_h, wd_l = (x.rearrange("p c n -> p (c n)") for x in (wdh, wdl))
                    dve.tensor_copy(wd_h, wd).then_inc(branch_hi, 1)
                    dve.tensor_copy(wubh[0:RANK + 1, :], wub_raw[:, :]).then_inc(branch_hi, 1)
                    dve.wait_ge(branch_hi, 2 * v + 2)
                    dve.tensor_tensor(wd_l, wd, wd_h.bitcast(F32), ALU.subtract).then_inc(branch_split, 1)
                    dve.tensor_tensor(wubl[0:RANK + 1, :], wub_raw[:, :], wubh[0:RANK + 1, :].bitcast(F32),
                                      ALU.subtract).then_inc(branch_split, 1)

                def split_x(v, tiles):
                    for c in order(tiles):
                        if c is None:
                            dve.wait_ge(xt5_hi, v - (B - 1))
                            dve.tensor_tensor(xl[:, :, 4 * P:], hb[:, 0, :].rearrange("p (c n) -> p c n", c=KC),
                                              xh[:, :, 4 * P:].bitcast(F32),
                                              ALU.subtract).then_inc(xt_split, 1)
                        else:
                            dve.wait_ge(xt_hi, KC * v + c + 1)
                            dve.tensor_tensor(xl[:, c, 0:4 * P], hb[:, 1 + c % 2, :], xh[:, c, 0:4 * P].bitcast(F32),
                                              ALU.subtract).then_inc(xt_split, 1)

                def body(v, w, tiles, after):
                    for a in range(STEPS):
                        if a == 4 and after:
                            dve.wait_ge(y_done, STEPS * v + 1)
                            split_branch(v + 1, after[0])
                        if a < FC:
                            c = a
                            wait_weights(dve, v, c)
                            dve.wait_ge(h_full, 2 * (STEPS * v + (c if c >= 2 else 0)))
                            raw = w1_raw[:, c // GROUP % 2, c % GROUP, :]
                            hi, lo = (x[:, c % 2, :, :].rearrange("p c n -> p (c n)") for x in (w1h, w1l))
                            dve.tensor_copy(hi, raw).then_inc(w1_hi, 1)
                            dve.wait_ge(w1_hi, FC * v + c + 1)
                            dve.tensor_tensor(lo, raw, hi.bitcast(F32), ALU.subtract).then_inc(w1_split, 1)
                        n = tiles * P
                        dve.wait_ge(gelu_done, 2 * (STEPS * v + a + 1))
                        if a == 0:
                            raw, hi, lo = a_raw[:, 0:n], ah[0:RANK, 0:n], al[0:RANK, 0:n]
                        else:
                            raw, hi, lo = g_raw[:, a % 2, 0:n], gh[:, a % 2, 0:n], gl[:, a % 2, 0:n]
                            dve.wait_ge(y_done, STEPS * v + max(a - 1, 0))
                        dve.tensor_copy(hi, raw).then_inc(g_hi, 1)
                        dve.wait_ge(g_hi, STEPS * v + a + 1)
                        dve.tensor_tensor(lo, raw, hi.bitcast(F32), ALU.subtract).then_inc(g_split, 1)

                    if after:
                        split_x(v + 1, after[1])

                split_branch(0, 0)
                split_x(0, 4)
                loops(dve, body)


class Combine:

    def __init__(self, k, st, name, routing, source, norm, shared=None, before=0):
        self.k, self.routing, self.source, self.norm, self.shared, self.before = k, routing, source, norm, shared, before
        self.rows = k.sb(f"{name}_rows", [P, 2, TB, D], stack=st)
        self.index = k.sb(f"{name}_index", [P, 2, TB], U32, stack=st)
        if shared is not None:
            self.shared_rows = k.sb(f"{name}_shared_rows", [P, TB, D], stack=st)
        self.gathered = [k.sem(f"combine_gathered{i}") for i in range(2)]
        self.index_ready, self.shared_loaded, self.first, self.second = (
            k.sem("combine_index_ready"), k.sem("combine_shared_loaded"), k.sem("combine_first"), k.sem("combine_second"))

    def load_shared(self, eng, b):
        eng.wait_ge(self.norm.delta_ready, self.norm.count(b))
        eng.dma_start(self.shared_rows[:, :, :],
                      self.shared[bass.ds(b, 1), 0:S, :].rearrange("a (t p) d -> p (a t) d", p=P)
                      ).then_inc(self.shared_loaded, 16)

    def gather(self, pool, b):
        pool.wait_ge(self.norm.delta_ready, self.norm.count(b))
        pool.tensor_copy(self.index[:, :, :], self.routing.gather_row[:, :, bass.ds(b * TB, TB)]
                         ).then_inc(self.index_ready, 1)
        wait_alone(pool, self.index_ready, self.before + b + 1, self.k.passed)
        for c in range(2):
            for i in range(TB):
                pool.indirect_dma_start(
                    out=self.rows[:, c, i, :], out_offset=None, in_=self.source,
                    in_offset=bass.IndirectOffsetOnAxis(ap=self.index[:, c, i:i + 1], axis=0),
                ).then_inc(self.gathered[c], 16)

    def weight(self, c, b, i):
        return self.routing.weight[:, c, bass.ds(b * TB + i, 1)]

    def sum(self, dve, b):
        delta = self.norm.delta
        dve.wait_ge(self.gathered[0], 16 * TB * (self.before + b + 1))
        dve.wait_ge(self.norm.added, self.norm.count(b))
        for i in range(TB):
            dve.tensor_scalar(delta[:, i, :], self.rows[:, 0, i, :], self.weight(0, b, i), None,
                              ALU.mult).then_inc(self.first, 1)
        dve.wait_ge(self.gathered[1], 16 * TB * (self.before + b + 1))
        for i in range(TB):
            dve.wait_ge(self.first, TB * (self.before + b) + i + 1)
            last = dve.scalar_tensor_tensor(out=delta[:, i, :], in0=self.rows[:, 1, i, :],
                                            scalar=self.weight(1, b, i), in1=delta[:, i, :], op0=ALU.mult, op1=ALU.add)
            last.then_inc(self.norm.delta_ready if self.shared is None else self.second, 1)
        if self.shared is not None:
            dve.wait_ge(self.shared_loaded, 16 * (b + 1))
            for i in range(TB):
                dve.wait_ge(self.second, TB * b + i + 1)
                dve.scalar_tensor_tensor(out=delta[:, i, :], in0=self.shared_rows[:, i, :], scalar=0.2,
                                         in1=delta[:, i, :], op0=ALU.mult, op1=ALU.add
                                         ).then_inc(self.norm.delta_ready, 1)


def combine_and_attention1(k, routing, logits, h_rows):
    nc = k.nc

    def sem(n):
        return k.sem(f"a1_{n}")

    BANKS = 4
    full = [sem(f"full{i}") for i in range(BANKS)]
    free = [sem(f"free{i}") for i in range(BANKS)]
    max_done, negated, inv_done, prob_done, stored = (
        sem("max_done"), sem("negated"), sem("inv_done"), sem("prob_done"), sem("stored"))
    KINDS = ("hT", "scores", "probT", "ctx")

    with ExitStack() as st:
        norm1 = NormPass(k, st, "n1", (0, GB), (1, CA), (1, SA), sems="norm_a", before=B)
        norm2 = NormPass(k, st, "n2", (1, GA), (1, CB), (1, SB_), sems="norm_b")
        combine = Combine(k, st, "c0", routing, k.expert_out, norm1,
                          shared=k.expert_out[0:T, :].rearrange("(r q) d -> r q d", q=S))
        router = RouterPass(k, st, "r1", "wr", norm2, logits, before=B)
        h_t = k.sb("a1_h_t", [P, KC, S], stack=st)
        prob = k.sb("a1_prob", [P, KC, D], stack=st)
        prob_t = k.sb("a1_prob_t", [P, KC, D], stack=st)
        mx = k.sb("a1_max", [P, KC], stack=st)
        neg = k.sb("a1_neg_max", [P, KC], stack=st)
        total = k.sb("a1_total", [P, KC], stack=st)
        inv = k.sb("a1_inv", [P, KC], stack=st)
        ps = k.ps("a1_psum", [P, BANKS, D], st)
        h = norm1.h

        def turn(kind, b):
            return 4 * b + KINDS.index(kind)

        def wait_full(eng, kind, n, b):
            eng.wait_ge(full[n], turn(kind, b) + 1)

        def wait_free(pe, kind, n, b):
            pe.wait_ge(free[n], turn(kind, b))

        def wait_taken(pe, kind, b):
            for n in range(4):
                pe.wait_ge(free[n], turn(kind, b) + 1)

        with nc.Block() as block:
            @block.sync
            def _(sp):
                norm1.load(sp)
                norm2.load(sp)
                router.load(sp)
                combine.load_shared(sp, 0)

                def body(b, last):
                    if not last:
                        combine.load_shared(sp, b + 1)
                    for i in range(TB):
                        sp.wait_ge(norm2.h_ready, norm2.count(b, i + 1))
                        sp.dma_start(h_rows(b, i), norm2.h[:, i, :]).then_inc(stored, 16)

                batch_loop(sp, body)
                sp.wait_ge(stored, 16 * NT)

            @block.gpsimd
            def _(pool):
                combine.gather(pool, 0)
                norm1.gate(pool, 0)
                norm1.scale(pool, 0)

                def body(b, last):
                    if not last:
                        combine.gather(pool, b + 1)
                        norm1.gate(pool, b + 1)
                        norm1.scale(pool, b + 1)
                    norm2.scale(pool, b)

                batch_loop(pool, body)

            @block.tensor
            def _(pe):
                def turn_and_score(b):
                    pe.wait_ge(norm1.h_ready, norm1.count(b, TB))
                    for c in range(KC):
                        wait_free(pe, "hT", c, b)
                        for i in range(TB):
                            mm = pe.transpose(ps[:, c, i * P:(i + 1) * P], h[:, i, c * P:(c + 1) * P], k.ident[:, :])
                        mm.then_inc(full[c], 1)
                    for n in range(KC):
                        wait_free(pe, "scores", n, b)
                        for i in range(TB):
                            mm = pe.matmul(ps[:, n, :], h[:, i, n * P:(n + 1) * P], h[:, i, :],
                                           start=(i == 0), stop=(i == TB - 1))
                        mm.then_inc(full[n], 1)

                def body(b, last):
                    pe.wait_ge(prob_done, KC * b + KC)
                    for c in range(KC):
                        wait_free(pe, "probT", c, b)
                        for n in range(KC):
                            mm = pe.transpose(ps[:, c, n * P:(n + 1) * P], prob[:, n, c * P:(c + 1) * P], k.ident[:, :])
                        mm.then_inc(full[c], 1)
                    wait_taken(pe, "probT", b)
                    for i in range(TB):
                        for c in range(KC):
                            mm = pe.matmul(ps[:, i, :], h_t[:, c, i * P:(i + 1) * P], prob_t[:, c, :],
                                           start=(c == 0), stop=(c == KC - 1))
                        mm.then_inc(full[i], 1)
                    if not last:
                        turn_and_score(b + 1)
                    router.tensor(pe, b)

                turn_and_score(0)
                batch_loop(pe, body)

            @block.scalar
            def _(act):
                def take_turned(b):
                    for c in range(KC):
                        wait_full(act, "hT", c, b)
                        act.copy(h_t[:, c, :], ps[:, c, :]).then_inc(free[c], 1)

                norm1.root(act, 0)
                take_turned(0)

                def body(b, last):
                    act.wait_ge(negated, b + 1)
                    for n in range(KC):
                        act.activation(prob[:, n, :], ps[:, n, :], ACT.Exp, bias=neg[:, n:n + 1],
                                       accum_out=total[:, n:n + 1]).then_inc(free[n], 1)
                    for c in range(KC):
                        wait_full(act, "probT", c, b)
                        act.copy(prob_t[:, c, :], ps[:, c, :]).then_inc(free[c], 1)
                    if not last:
                        norm1.root(act, b + 1)
                        take_turned(b + 1)
                    norm2.root(act, b)
                    router.scalar(act, b)

                batch_loop(act, body)

            @block.vector
            def _(dve):
                def front(b):
                    combine.sum(dve, b)
                    norm1.add(dve, b)
                    norm1.statistics(dve, b)
                    norm1.center(dve, b)
                    norm1.shift(dve, b)

                dve.wait_ge(norm1.mod_loaded, 16 * 3 * B)
                dve.wait_ge(norm2.mod_loaded, 16 * 3 * B)
                front(0)

                def body(b, last):
                    for n in range(KC):
                        wait_full(dve, "scores", n, b)
                        dve.tensor_reduce(mx[:, n:n + 1], ps[:, n, :], AX.X, ALU.max).then_inc(max_done, 1)
                    dve.wait_ge(max_done, KC * b + KC)
                    dve.tensor_scalar(neg[:, :], mx[:, :], -1.0, None, ALU.mult).then_inc(negated, 1)
                    for n in range(KC):
                        dve.wait_ge(free[n], turn("scores", b) + 1)
                    dve.reciprocal(inv[:, :], total[:, :]).then_inc(inv_done, 1)
                    dve.wait_ge(inv_done, b + 1)
                    for n in range(KC):
                        dve.tensor_scalar(prob[:, n, :], prob[:, n, :], inv[:, n:n + 1], None,
                                          ALU.mult).then_inc(prob_done, 1)
                    if not last:
                        front(b + 1)
                    dve.wait_ge(norm2.added, norm2.count(b))
                    for i in range(TB):
                        wait_full(dve, "ctx", i, b)
                        dve.tensor_tensor(norm2.delta[:, i, :], ps[:, i, :], norm2.mod_of(0, b), ALU.mult
                                          ).then_inc(free[i], 1)
                    for i in range(TB):
                        dve.wait_ge(free[i], turn("ctx", b) + 1)
                    dve.sem_inc(norm2.delta_ready, TB)
                    dve.sem_inc(norm2.gated, TB)
                    norm2.add(dve, b)
                    norm2.statistics(dve, b)
                    router.wait_h_free(dve, b)
                    dve.wait_ge(stored, 16 * TB * b)
                    norm2.center(dve, b)
                    norm2.shift(dve, b)

                batch_loop(dve, body)


class Experts1Weights:

    FULL, REST = INNER // P, INNER % P

    def __init__(self, k, st):
        self.k = k
        self.loaded = k.sem("e1_w_loaded")
        self.gate_up = k.sb("e1_wgu", [P, E * KC * 2, INNER], stack=st)
        self.down = k.sb("e1_wd", [P, E * self.FULL, D], stack=st)
        self.down_rest = k.sb("e1_wd_rest", [self.REST, E, D], stack=st)

    def load(self, eng):
        for name, buf in (("wgu", self.gate_up), ("wd1", self.down), ("wd1_rest", self.down_rest)):
            eng.dma_start(buf[:, :, :], self.k.ins[name]).then_inc(self.loaded, 16)


def experts1(k, weights, tile_expert):
    nc = k.nc
    FULL, REST = weights.FULL, weights.REST
    NCH = FULL + 1

    def sem(n):
        return k.sem(f"e1_{n}")

    x_in, x_out = [sem(f"x_loaded{i}") for i in range(2)], [sem(f"y_stored{i}") for i in range(2)]
    xt_full, xt_taken, g_full, u_full, silu_done, h_ready = (
        sem("xt_full"), sem("xt_taken"), sem("g_full"), sem("u_full"), sem("silu_done"), sem("h_ready"))
    ht_full, ht_taken, y_full, y_taken = sem("ht_full"), sem("ht_taken"), sem("y_full"), sem("y_taken")
    with ExitStack() as st:
        def sb(n, shape, dtype=F32):
            return k.sb(f"e1_{n}", shape, dtype, stack=st)

        x = sb("x", [P, 2, D])
        xt = sb("xt", [P, 2, KC, P])
        g = sb("silu", [P, 2, INNER])
        h = sb("h", [P, 2, INNER])
        ht = sb("ht", [P, 2, NCH, P])
        y_sb = sb("y", [P, 2, D])
        pt = k.ps("e1_xt_psum", [P, KC, P], st)
        pgu = k.ps("e1_gu_psum", [P, 4, D], st)
        ph = k.ps("e1_ht_psum", [P, 4, P], st)
        py = k.ps("e1_y_psum", [P, D], st)

        def rows(buf, q, p):
            return buf.rearrange("(t p) d -> t p d", p=P)[bass.ds(2 * q + p, 1)].rearrange("a p d -> (a p) d")

        def after(q, p):
            return (q, 1) if p == 0 else (q + 1, 0)

        def before(q, p):
            return (q, 0) if p == 1 else (q - 1, 1)

        LAST = divmod(TILES1 - 1, 2)
        assert LAST[1] == 0

        def loop(eng, step):
            step(0, 0, True, False)
            with eng.Fori(0, LAST[0] - 1) as r:
                step(r, 1, False, False)
                step(r + 1, 0, False, False)
            step(LAST[0] - 1, 1, False, False)
            step(*LAST, False, True)

        with nc.Block() as block:
            @block.sync
            def _(sp):
                def load(q, p, first=False):
                    if not first:
                        sp.wait_ge(xt_full, 2 * q + p - 1)
                    sp.dma_start(x[:, p, :], rows(k.dispatch1, q, p)).then_inc(x_in[p], 16)

                load(0, 0, first=True)
                load(0, 1, first=True)
                with sp.Fori(1, LAST[0]) as q:
                    load(q, 0)
                    load(q, 1)
                load(*LAST)

            @block.gpsimd
            def _(pool):
                def store(q, p):
                    pool.wait_ge(y_taken, 2 * q + p + 1)
                    pool.dma_start(rows(k.expert_out1, q, p), y_sb[:, p, :]).then_inc(x_out[p], 16)

                with pool.Fori(0, LAST[0]) as q:
                    store(q, 0)
                    store(q, 1)
                store(*LAST)
                pool.wait_ge(x_out[0], 16 * (LAST[0] + 1))
                pool.wait_ge(x_out[1], 16 * LAST[0])

            @block.tensor
            def _(pe):
                pe.wait_ge(weights.loaded, 48)

                def expert(q, p):
                    return pe.value_load(tile_expert[0:1, bass.ds(2 * q + p, 1)], min_val=0, max_val=E - 1)

                def turn_x(q, p):
                    pe.wait_ge(x_in[p], 16 * (q + 1))
                    pe.wait_ge(xt_taken, 2 * q + p)
                    for c in range(KC):
                        mm = pe.transpose(pt[:, c, :], x[:, p, c * P:(c + 1) * P], k.ident[:, :])
                    mm.then_inc(xt_full, 1)

                def product(q, p, which, e, done):
                    for c in range(KC):
                        w = flat(weights.gate_up[:, bass.ds(e * (2 * KC) + (2 * c + which), 1), :])
                        mm = pe.matmul(pgu[:, 2 * p + which, 0:INNER], xt[:, p, c, :], w,
                                       start=(c == 0), stop=(c == KC - 1))
                    mm.then_inc(done, 1)

                def turn_h(q, p):
                    t = 2 * q + p
                    pe.wait_ge(h_ready, t + 1)
                    pe.wait_ge(ht_taken, t)
                    for c in range(NCH):
                        n = P if c < FULL else REST
                        mm = pe.transpose(ph[0:n, c, :], h[:, p, c * P:c * P + n], k.ident[:, :])
                    mm.then_inc(ht_full, 1)

                def down(q, p, e):
                    t = 2 * q + p
                    pe.wait_ge(ht_taken, t + 1)
                    pe.wait_ge(y_taken, t)
                    for c in range(NCH):
                        w = (flat(weights.down[:, bass.ds(e * FULL + c, 1), :]) if c < FULL
                             else flat(weights.down_rest[:, bass.ds(e, 1), :]))
                        n = P if c < FULL else REST
                        mm = pe.matmul(py[:, :], ht[0:n, p, c, :], w, start=(c == 0), stop=(c == NCH - 1))
                    mm.then_inc(y_full, 1)

                def step(q, p, first, last):
                    t, e = 2 * q + p, expert(q, p)
                    pe.wait_ge(xt_taken, t + 1)
                    if not first:
                        pe.wait_ge(h_ready, t - 1)
                    product(q, p, 0, e, g_full)
                    if not first:
                        turn_h(*before(q, p))
                    if not last:
                        turn_x(*after(q, p))
                    product(q, p, 1, e, u_full)
                    if not first:
                        down(*before(q, p), expert(*before(q, p)))

                turn_x(0, 0)
                loop(pe, step)
                turn_h(*LAST)
                down(*LAST, expert(*LAST))

            @block.scalar
            def _(act):
                def take_x(q, p, first=False):
                    act.wait_ge(xt_full, 2 * q + p + 1)
                    if not first:
                        act.wait_ge(u_full, 2 * q + p - 1)
                    act.copy(xt[:, p, :, :], pt[:, :, :]).then_inc(xt_taken, 1)

                def take_y(q, p):
                    act.wait_ge(y_full, 2 * q + p + 1)
                    act.wait_ge(x_out[p], 16 * q)
                    act.copy(y_sb[:, p, :], py[:, :]).then_inc(y_taken, 1)

                def step(q, p, first, last):
                    t = 2 * q + p
                    act.wait_ge(g_full, t + 1)
                    if not first:
                        act.wait_ge(h_ready, t - 1)
                    act.activation(g[:, p, :], pgu[:, 2 * p, 0:INNER], ACT.Silu).then_inc(silu_done, 1)
                    if not last:
                        take_x(*after(q, p))
                    if not first:
                        take_y(*before(q, p))

                take_x(0, 0, first=True)
                loop(act, step)
                take_y(*LAST)

            @block.vector
            def _(dve):
                def take_h(q, p):
                    t = 2 * q + p
                    dve.wait_ge(ht_full, t + 1)
                    dve.wait_ge(y_full, t)
                    dve.tensor_copy(ht[:, p, 0:FULL, :], ph[:, 0:FULL, :])
                    dve.tensor_copy(ht[0:REST, p, FULL, :], ph[0:REST, FULL, :]).then_inc(ht_taken, 1)

                def step(q, p, first, last):
                    t = 2 * q + p
                    if not first:
                        take_h(*before(q, p))
                    dve.wait_ge(silu_done, t + 1)
                    dve.wait_ge(u_full, t + 1)
                    if not first:
                        dve.wait_ge(ht_full, t - 1)
                    dve.tensor_tensor(h[:, p, :], g[:, p, :], pgu[:, 2 * p + 1, 0:INNER], ALU.mult).then_inc(h_ready, 1)

                loop(dve, step)
                take_h(*LAST)


def combine_to_output(k, routing):
    nc = k.nc
    x_ready, stored = k.sem("out_x_ready"), k.sem("out_stored")
    with ExitStack() as st:
        norm = NormPass(k, st, "n3", (1, GB), sems="norm_b", before=B)
        combine = Combine(k, st, "c1", routing, k.expert_out1, norm, before=B)
        with nc.Block() as block:
            @block.sync
            def _(sp):
                norm.load(sp)
                with sp.Fori(0, B) as b:
                    sp.wait_ge(norm.added, norm.count(b, TB))
                    sp.dma_start(k.out[bass.ds(b, 1)].rearrange("a (t p) d -> p (a t) d", p=P),
                                 k.x[:, bass.ds(b * TB, TB), :]).then_inc(stored, 16)
                sp.wait_ge(stored, 16 * B)

            @block.gpsimd
            def _(pool):
                combine.gather(pool, 0)

                def body(b, last):
                    if not last:
                        combine.gather(pool, b + 1)
                    norm.gate(pool, b)

                batch_loop(pool, body)

            @block.vector
            def _(dve):
                with dve.Fori(0, B) as b:
                    combine.sum(dve, b)
                    norm.add(dve, b)


def program(nc, ins, out, phases=99):
    with ExitStack() as stack:
        k = Core(nc, stack, ins, out)
        routing = Routing(k, "route", stack)
        tile_expert = k.sb("tile_expert", [P, TILES1], I32)
        logits = k.sb("logits", [P, NT, E])
        batches = k.dispatch[0:T, :].rearrange("(b s) d -> b s d", b=B)

        def one(ap, b, rows):
            return (ap[b:b + 1, rows, :] if isinstance(b, int) else ap[bass.ds(b, 1), rows, :]
                    ).rearrange("a q d -> (a q) d")

        def shared_rows(b, i):
            return one(batches, b, slice(i * P, (i + 1) * P))

        def h_rows1(b, i):
            return one(k.h_rows1.rearrange("(b s) d -> b s d", b=B), b, slice(i * P, (i + 1) * P))

        with ExitStack() as ctx_stack:
            ctx_t = k.sb("ctx_t", [P, B, KC, S], stack=ctx_stack)
            with ExitStack() as att_stack:
                att = Attention0(k, att_stack)
                start_and_modulation(k, att)
                if phases >= 1:
                    attention0(k, att, ctx_t)
            if phases >= 2:
                project_and_norm0(k, ctx_t, logits, shared_rows)
        if phases >= 2:
            route(k, "rt0", 0, logits, shared_rows, routing, k.dispatch)
        if phases >= 3:
            experts0(k)
        if phases >= 4:
            combine_and_attention1(k, routing, logits, h_rows1)
        with ExitStack() as weight_stack:
            weights = Experts1Weights(k, weight_stack)
            if phases >= 5:
                route(k, "rt1", 1, logits, h_rows1, routing, k.dispatch1, tile_expert, weights)
            if phases >= 6:
                experts1(k, weights, tile_expert)
        if phases >= 7:
            combine_to_output(k, routing)


def lay_out(inputs):
    import numpy as np

    g = {n: np.asarray(a) for n, a in inputs.items()}
    con = np.ascontiguousarray

    def chunks(w):
        return con(w.reshape(-1, P, w.shape[1]).transpose(1, 0, 2))

    lay = {"x": con(g["L0_attn_query"].reshape(T, D))}
    lay["c_t"] = con(np.stack([chunks(g["L0_c"].T), chunks(g["L1_c"].T)], 1))
    lay["wmod"] = con(np.stack([g["L0_wmod"], g["L1_wmod"]]).reshape(2, KC, P, 6, D)
                      .transpose(0, 3, 2, 1, 4).reshape(12, P, KC * D))
    w = g["L0_attn_Wqkv"].reshape(4, 4, 3, HN, D).transpose(2, 1, 0, 3, 4).reshape(3, D, D)
    lay["wqk"] = con(np.stack([chunks(w[0].T), chunks(w[1].T)], 1))
    lay["wv"] = chunks(w[2].T)
    lay["wproj"] = chunks(g["L0_attn_Wproj"].T)
    lay["bproj"] = con(g["L0_attn_bproj"].reshape(1, D))
    w1 = np.concatenate([g["L0_ffn_sw1"][None], g["L0_ffn_w1"]])
    lay["w1"] = con(w1.reshape(E + 1, KC, P, 4, 4, P).transpose(0, 3, 2, 4, 1, 5).reshape(E + 1, 4, P, 4 * KC * P))
    w2 = np.concatenate([g["L0_ffn_sw2"][None], g["L0_ffn_w2"]])
    lay["w2"] = con(w2.reshape(E + 1, 4, 4, P, D).transpose(0, 1, 3, 2, 4).reshape(E + 1, 4, P, 4 * D))
    wd = np.concatenate([g["L0_ffn_swd"][None], g["L0_ffn_wd"]])
    lay["wd"] = con(wd.reshape(E + 1, KC, P, RANK).transpose(2, 0, 1, 3).reshape(P, E + 1, KC * RANK))
    wu = np.concatenate([g["L0_ffn_swu"][None], g["L0_ffn_wu"]])
    b2 = np.concatenate([g["L0_ffn_sb2"][None], g["L0_ffn_b2"]])
    lay["wu_b2"] = con(np.concatenate([wu, b2[:, None, :]], 1))
    b1 = np.concatenate([g["L0_ffn_sb1"][None], g["L0_ffn_b1"]])
    lay["b1"] = con(b1.reshape(E + 1, FC, P).transpose(2, 0, 1).reshape(P, (E + 1) * FC))
    lay["wr"] = chunks(g["L1_ffn_Wr"])
    wgu = np.stack([g["L1_ffn_Wg"], g["L1_ffn_Wu"]], 2).reshape(E, KC, P, 2, INNER)
    lay["wgu"] = con(wgu.transpose(2, 0, 1, 3, 4).reshape(P, E * KC * 2, INNER))
    whole = INNER // P * P
    lay["wd1"] = con(g["L1_ffn_Wd"][:, :whole].reshape(E, INNER // P, P, D).transpose(2, 0, 1, 3)
                     .reshape(P, E * (INNER // P), D))
    lay["wd1_rest"] = con(g["L1_ffn_Wd"][:, whole:].transpose(1, 0, 2))
    lay["gate_w"] = chunks(g["L0_ffn_gate_w"])
    return lay


def kernel(**inputs):
    import concourse.bacc as bacc
    import numpy as np
    from concourse.bass_utils import run_bass_kernel_spmd

    nc = bacc.Bacc("TRN2", target_bir_lowering=False, num_devices=1)
    arrays = {f"in_{n}": a for n, a in lay_out(inputs).items()}
    ins = {n[3:]: nc.dram_tensor(n, a.shape, mybir.dt.from_np(a.dtype), kind="ExternalInput").ap()
           for n, a in arrays.items()}
    out = nc.dram_tensor("out_0", (B, S, D), F32, kind="ExternalOutput").ap()
    program(nc, ins, out)
    r = run_bass_kernel_spmd(nc, [arrays], core_ids=[0])
    return np.asarray(r.results[0]["out_0"])
```

```python
from contextlib import ExitStack

import concourse.bass as bass
from concourse import mybir

F32 = mybir.dt.float32
F32R = mybir.dt.float32r
I32 = mybir.dt.int32
U32 = mybir.dt.uint32
ALU = mybir.AluOpType
ACT = mybir.ActivationFunctionType
AX = mybir.AxisListType

P = 128
B, S, D = 4, 512, 512
T = B * S
NT = T // P
TB = S // P
KC = D // P
HEADS, HN = 16, 32
QUADS = 4
E = 8
F = 2048
FC = F // P
RANK = 32
CAP = 320
REGION = 2 * CAP
INNER = 352
TILES1 = 2 * T // P + E - 1
EPS = 1e-5
SA, CA, GA, SB_, CB, GB = range(6)


def flat(ap):
    return ap.rearrange("p a d -> p (a d)")


def tile_of(buf, index):
    if isinstance(index, int):
        return buf[:, index, :]
    return flat(buf[:, bass.ds(index, 1), :])


def batch_loop(eng, body):
    with eng.Fori(0, B - 1) as b:
        body(b, False)
    body(B - 1, True)


def wait_alone(eng, sem, value, passed):
    eng.wait_ge(sem, value)
    eng.sem_inc(passed, 1)


class Core:

    def __init__(self, nc, stack, ins, out):
        self.nc, self.stack, self.ins, self.out, self.sems = nc, stack, ins, out, {}
        self.x = self.sb("x_resid", [P, NT, D])
        self.ident = self.sb("ident", [P, P])
        self.passed = self.sem("waits_passed")
        self.eps = self.sb("eps", [P, 1])
        self.mod_rows = nc.dram_tensor("mod_rows", (2, 6, B, D), F32, kind="Internal").ap()
        self.h_rows0 = nc.dram_tensor("h_rows0", (T, D), F32, kind="Internal").ap()
        self.shared_out = nc.dram_tensor("shared_out", (T, D), F32, kind="Internal").ap()
        self.dispatch = nc.dram_tensor("dispatch0", (E * REGION, D), F32, kind="Internal").ap()
        self.expert_out = nc.dram_tensor("expert_out0", (E * REGION, D), F32, kind="Internal").ap()
        self.dispatch1 = nc.dram_tensor("dispatch1", (TILES1 * P, D), F32, kind="Internal").ap()
        self.h_rows1 = nc.dram_tensor("h_rows1", (T, D), F32, kind="Internal").ap()
        self.expert_out1 = nc.dram_tensor("expert_out1", (TILES1 * P, D), F32, kind="Internal").ap()

    def sb(self, name, shape, dtype=F32, stack=None):
        return (stack or self.stack).enter_context(self.nc.sbuf_tensor(name, shape, dtype))

    def ps(self, name, shape, stack):
        return stack.enter_context(self.nc.psum_tensor(name, shape, F32))

    def sem(self, name):
        if name not in self.sems:
            self.sems[name] = self.stack.enter_context(self.nc.semaphore(name))
        return self.sems[name]

    def mod_tile(self, layer, which, batch):
        row = self.mod_rows[layer, which]
        row = row[batch:batch + 1, :] if isinstance(batch, int) else row[bass.ds(batch, 1), :]
        return row.broadcast_to([P, D])


class Modulation:

    def __init__(self, k, st, layer):
        self.k, self.layer = k, layer
        self.w = k.sb(f"wmod_sb{layer}", [P, 6, KC * D], stack=st)
        self.c_t = k.sb(f"c_t{layer}", [P, KC, B], stack=st)
        self.silu = k.sb(f"c_t_silu{layer}", [P, KC, B], stack=st)
        self.rows = k.sb(f"mod_rows_sb{layer}", [P, 2, D], stack=st)
        self.sign = k.sb(f"gate_sign{layer}", [P, 2, D], stack=st)
        self.psum = k.ps(f"mod_psum{layer}", [P, 2, D], st)
        self.c_loaded, self.silu_done, self.multiplied, self.half_step, self.rows_done, self.stored = (
            k.sem(f"mod_{s}") for s in ("c_loaded", "silu_done", "multiplied", "half_step", "rows_done", "stored"))
        self.w_loaded = [k.sem(f"mod_w_loaded{i}") for i in range(2)]

    def place(self, buf, n):
        return buf[32 * (n % 4):32 * (n % 4) + B, n // 4, :]

    def load_c(self, eng):
        eng.dma_start(self.c_t[:, :, :], self.k.ins["c_t"][:, self.layer]).then_inc(self.c_loaded, 16)

    def load_w(self, eng):
        for n in range(6):
            eng.dma_start(self.w[:, n, :], self.k.ins["wmod"][6 * self.layer + n]).then_inc(self.w_loaded[n // 4], 16)

    def activate(self, act):
        act.wait_ge(self.c_loaded, 16 * (self.layer + 1))
        act.activation(self.silu[:, :, :], self.c_t[:, :, :], ACT.Silu).then_inc(self.silu_done, 1)

    def multiply(self, pe):
        pe.wait_ge(self.silu_done, self.layer + 1)
        for group in (range(4), range(4, 6)):
            pe.wait_ge(self.w_loaded[group[0] // 4], 16 * len(group) * (self.layer + 1))
            for c in range(KC):
                for n in group:
                    mm = pe.matmul(self.place(self.psum, n), self.silu[:, c, :], self.w[:, n, c * D:(c + 1) * D],
                                   start=(c == 0), stop=(c == KC - 1))
            mm.then_inc(self.multiplied, 1)

    def finish(self, dve):
        halves = 6 * self.layer
        for n in range(6):
            src, dst, sign = self.place(self.psum, n), self.place(self.rows, n), self.place(self.sign, n)
            dve.wait_ge(self.multiplied, 2 * self.layer + n // 4 + 1)
            if n in (CA, CB):
                dve.tensor_scalar(dst, src, 1.0, None, ALU.add).then_inc(self.rows_done, 1)
            elif n in (SA, SB_):
                dve.tensor_copy(dst, src).then_inc(self.rows_done, 1)
            else:
                dve.tensor_scalar(sign, src, 0.0, 2.0, ALU.is_ge, ALU.mult).then_inc(self.half_step, 1)
                dve.wait_ge(self.half_step, halves + 1)
                dve.tensor_scalar(sign, sign, -1.0, None, ALU.add).then_inc(self.half_step, 1)
                dve.wait_ge(self.half_step, halves + 2)
                dve.tensor_tensor(dst, src, sign, ALU.mult).then_inc(self.half_step, 1)
                halves += 3
                dve.wait_ge(self.half_step, halves)
                dve.scalar_tensor_tensor(out=dst, in0=dst, scalar=0.25, in1=sign, op0=ALU.max,
                                         op1=ALU.mult).then_inc(self.rows_done, 1)

    def store(self, eng):
        for n in range(6):
            eng.wait_ge(self.rows_done, 6 * self.layer + n + 1)
            eng.dma_start(self.k.mod_rows[self.layer, n], self.place(self.rows, n)).then_inc(self.stored, 16)
        eng.wait_ge(self.stored, 16 * 6 * (self.layer + 1))


def start(k, att):
    nc, ins = k.nc, k.ins
    x_loaded, att_w_loaded = k.sem("x_loaded"), k.sem("att_w_loaded")
    stats_done, var_done, sd_done, rstd_done = k.sem("stats_done"), k.sem("var_done"), k.sem("sd_done"), k.sem("rstd_done")
    cleared = k.sem("cleared")
    with ExitStack() as st:
        mods = Modulation(k, st, 0)
        stats = k.sb("ln1_stats", [P, NT, 6], stack=st)
        sd = k.sb("ln1_sd", [P, NT], stack=st)
        with nc.Block() as block:
            @block.sync
            def _(sp):
                mods.load_c(sp)
                for t in range(0, NT, TB):
                    sp.dma_start(k.x[:, t:t + TB, :],
                                 ins["x"][t * P:(t + TB) * P, :].rearrange("(t p) d -> p t d", p=P)
                                 ).then_inc(x_loaded, 16)
                mods.load_w(sp)
                sp.dma_start(att.wqk[:, :, :, :], ins["wqk"]).then_inc(att_w_loaded, 16)
                sp.dma_start(att.wv[:, :, :], ins["wv"]).then_inc(att_w_loaded, 16)
                mods.store(sp)
                sp.wait_ge(att_w_loaded, 32)

            @block.scalar
            def _(act):
                mods.activate(act)
                act.wait_ge(var_done, NT)
                act.activation(sd[:, :], att.mean_var[:, :, 1], ACT.Sqrt, bias=k.eps[:, 0:1]).then_inc(sd_done, 1)

            @block.gpsimd
            def _(pool):
                pool.memset(k.ident[:, :], 0.0).then_inc(cleared, 1)
                pool.wait_ge(cleared, 1)
                pool.affine_select(out=k.ident[:, :], in_=k.ident[:, :], compare_op=ALU.not_equal, fill=1.0,
                                   base=0, pattern=[[-1, P]], channel_multiplier=1).then_inc(cleared, 1)
                pool.wait_ge(cleared, 2)
                pool.memset(att.ones[:, :], 1.0).then_inc(cleared, 1)
                pool.wait_ge(cleared, 3)
                pool.memset(att.zeros[:, :], 0.0).then_inc(cleared, 1)
                pool.wait_ge(cleared, 4)
                pool.memset(att.ks[96:128, :, :, :].bitcast(F32), 0.0).then_inc(cleared, 1)
                pool.wait_ge(cleared, 5)
                pool.memset(att.qs[96:128, :, :, :].bitcast(F32), 0.0).then_inc(cleared, 1)
                pool.wait_ge(cleared, 6)
                pool.memset(att.ks[96:97, :, :, :].bitcast(F32), 1.0)

            @block.tensor
            def _(pe):
                mods.multiply(pe)

            @block.vector
            def _(dve):
                dve.memset(k.eps[:, :], EPS)
                dve.wait_ge(x_loaded, 16 * B)
                for t in range(NT):
                    dve.bn_stats(stats[:, t, :], k.x[:, t, :]).then_inc(stats_done, 1)
                for t in range(NT):
                    dve.wait_ge(stats_done, t + 1)
                    dve.bn_aggr(att.mean_var[:, t, :], stats[:, t, :]).then_inc(var_done, 1)
                dve.wait_ge(sd_done, 1)
                dve.reciprocal(att.rstd[:, :], sd[:, :]).then_inc(rstd_done, 1)
                dve.wait_ge(rstd_done, 1)
                dve.scalar_tensor_tensor(out=att.shift[:, :], in0=att.mean_var[:, :, 0], scalar=-1.0,
                                         in1=att.rstd[:, :], op0=ALU.mult, op1=ALU.mult)
                mods.finish(dve)


class Attention0:

    def __init__(self, k, st):
        self.wqk = k.sb("wqk_sb", [P, 2, KC, D], stack=st)
        self.wv = k.sb("wv_sb", [P, KC, D], stack=st)
        self.mean_var = k.sb("ln1_mean_var", [P, NT, 2], stack=st)
        self.rstd = k.sb("ln1_rstd", [P, NT], stack=st)
        self.shift = k.sb("ln1_shift", [P, NT], stack=st)
        self.qs = k.sb("a0_q_stack", [P, 2, 4, S], F32R, stack=st)
        self.ks = k.sb("a0_k_stack", [P, 2, 4, S], F32R, stack=st)
        self.ones = k.sb("a0_ones", [P, HN], stack=st)
        self.zeros = k.sb("zero_rows", [P, 4 * D], stack=st)


def attention0(k, att, ctx_t):
    nc, ins = k.nc, k.ins
    NORM = float(HN) ** -0.5
    mod_loaded = k.sem("a0_mod_loaded")
    n_centered, n_scaled, h_ready = k.sem("a0_centered"), k.sem("a0_scaled"), k.sem("a0_h_ready")
    transposed = k.sem("a0_h_transposed")
    gen_full = [k.sem(f"a0_gen_full{i}") for i in range(2)]
    gen_free = [k.sem(f"a0_gen_free{i}") for i in range(2)]
    hi_done = k.sem("a0_hi_done")
    scores_full, max_done = k.sem("a0_scores_full"), k.sem("a0_max_done")
    row_full, row_taken = k.sem("a0_max_row_full"), k.sem("a0_max_row_taken")
    st_full, p_ready = k.sem("a0_st_full"), k.sem("a0_p_ready")
    pv_done, ctx_taken, recip_done, ctx_done = (
        k.sem("a0_pv_done"), k.sem("a0_ctx_taken"), k.sem("a0_recip_done"), k.sem("a0_ctx_done"))
    zero_stored = k.sem("zero_stored")

    uses = [("hT", c) for c in range(KC)] + [("q", 0), ("k", 0)] + [("v", t) for t in range(TB)]
    for j in range(QUADS):
        if j + 1 < QUADS:
            uses += [("q", j + 1), ("k", j + 1)]
    G = {u: n for n, u in enumerate(uses)}
    GH = len(uses) // 2
    assert len(uses) % 2 == 0

    with ExitStack() as st:
        mod = k.sb("a0_mod", [P, 2, D], stack=st)
        h = k.sb("a0_h", [P, TB, D], stack=st)
        h_t = k.sb("a0_h_t", [P, KC, S], stack=st)
        v = k.sb("a0_v", [P, TB, D], stack=st)
        qs, ks, ones = att.qs, att.ks, att.ones
        mx = k.sb("a0_max", [P, 16], stack=st)
        prob = k.sb("a0_prob", [P, 8, S], stack=st)
        rec = k.sb("a0_rec", [P, S], stack=st)
        ctx_raw = k.sb("a0_ctx_raw", [P, S], stack=st)
        den_raw = k.sb("a0_den_raw", [P, S], stack=st)
        gen = k.ps("a0_gen", [P, 2, S], st)
        sc = k.ps("a0_scores", [P, 2, S], st)
        scT = k.ps("a0_scores_t", [P, 2, S], st)
        ctx = k.ps("a0_ctx", [P, S], st)
        den = k.ps("a0_den", [P, S], st)

        def wait_full(eng, b, use):
            eng.wait_ge(gen_full[G[use] % 2], b * GH + G[use] // 2 + 1)

        def wait_freed(pe, b, use):
            pe.wait_ge(gen_free[G[use] % 2], b * GH + G[use] // 2)

        def wait_taken(eng, b, use):
            eng.wait_ge(gen_free[G[use] % 2], b * GH + G[use] // 2 + 1)

        with nc.Block() as block:
            @block.sync
            def _(sp):
                def load_mods(b):
                    sp.dma_start(mod[:, 0, :], k.mod_tile(0, CA, b)).then_inc(mod_loaded, 16)
                    sp.dma_start(mod[:, 1, :], k.mod_tile(0, SA, b)).then_inc(mod_loaded, 16)

                load_mods(0)
                zero_stores = 0
                for buf in (k.dispatch, k.dispatch1):
                    for r in range(0, buf.shape[0], 4 * P):
                        n = min(4, (buf.shape[0] - r) // P)
                        sp.dma_start(buf[r:r + n * P, :].rearrange("(p a) d -> p (a d)", p=P),
                                     att.zeros[:, 0:n * D]).then_inc(zero_stored, 16)
                        zero_stores += 1
                with sp.Fori(1, B) as b:
                    sp.wait_ge(h_ready, TB * b)
                    load_mods(b)
                sp.wait_ge(zero_stored, 16 * zero_stores)

            @block.gpsimd
            def _(pool):
                with pool.Fori(0, B) as b:
                    pool.wait_ge(mod_loaded, 32 * b + 32)
                    for i in range(TB):
                        pool.wait_ge(n_centered, TB * b + i + 1)
                        pool.tensor_tensor(h[:, i, :], h[:, i, :], mod[:, 0, :], ALU.mult).then_inc(n_scaled, 1)
                    for i in range(TB):
                        pool.wait_ge(n_scaled, TB * b + i + 1)
                        pool.tensor_tensor(h[:, i, :], h[:, i, :], mod[:, 1, :], ALU.add).then_inc(h_ready, 1)

            @block.tensor
            def _(pe):
                with pe.Fori(0, B) as b:
                    def project(which, j, chunks):
                        n, g = (0 if which == "q" else 1), G[(which, j)]
                        if 0 in chunks:
                            wait_freed(pe, b, (which, j))
                        for c in chunks:
                            mm = pe.matmul(gen[:, g % 2, :], att.wqk[:, n, c, j * P:(j + 1) * P], h_t[:, c, :],
                                           start=(c == 0), stop=(c == KC - 1))
                        if KC - 1 in chunks:
                            mm.then_inc(gen_full[g % 2], 1)

                    pe.wait_ge(h_ready, TB * b + TB)
                    for c in range(KC):
                        wait_freed(pe, b, ("hT", c))
                        for i in range(TB):
                            mm = pe.transpose(gen[:, G[("hT", c)] % 2, i * P:(i + 1) * P],
                                              h[:, i, c * P:(c + 1) * P], k.ident[:, :])
                        mm.then_inc(gen_full[G[("hT", c)] % 2], 1)
                    wait_taken(pe, b, ("hT", KC - 2))
                    wait_taken(pe, b, ("hT", KC - 1))
                    project("q", 0, range(KC))
                    project("k", 0, range(KC))
                    for t in range(TB):
                        g = G[("v", t)]
                        wait_freed(pe, b, ("v", t))
                        for c in range(KC):
                            mm = pe.matmul(gen[:, g % 2, :], h_t[:, c, t * P:(t + 1) * P], att.wv[:, c, :],
                                           start=(c == 0), stop=(c == KC - 1))
                        mm.then_inc(gen_full[g % 2], 1)
                    for j in range(QUADS):
                        par = j % 2
                        wait_taken(pe, b, ("q", j))
                        wait_taken(pe, b, ("k", j))
                        for a in range(4):
                            for t in range(TB):
                                s = 16 * j + 4 * a + t
                                pe.wait_ge(max_done, 64 * b + max(s - 1, 0))
                                if a == 0 and t < 2:
                                    pe.wait_ge(row_taken, 16 * b + 4 * j)
                                pe.matmul(sc[:, s % 2, :], qs[0:96, par, a, t * P:(t + 1) * P], ks[0:96, par, a, :],
                                          start=True, stop=True).then_inc(scores_full, 1)
                                if t % 2 and j + 1 < QUADS:
                                    project("q" if a < 2 else "k", j + 1, [2 * (a % 2) + t // 2])
                        for a in range(4):
                            pe.wait_ge(max_done, 64 * b + 16 * (j + 1))
                            pe.wait_ge(row_taken, 16 * b + 4 * j + max(a - 1, 0))
                            for t in range(TB):
                                mm = pe.transpose(sc[0:1, a % 2, t * P:(t + 1) * P],
                                                  mx[:, 4 * a + t:4 * a + t + 1], k.ident[:, :])
                            mm.then_inc(row_full, 1)

                        def score_t(t, a):
                            s = 16 * j + 4 * t + a
                            if t == 0:
                                pe.wait_ge(row_taken, 16 * b + 4 * j + a + 1)
                            pe.wait_ge(p_ready, 64 * b + max(s - 1, 0))
                            pe.matmul(scT[:, s % 2, :], ks[:, par, a, t * P:(t + 1) * P], qs[:, par, a, :],
                                      start=True, stop=True).then_inc(st_full, 1)

                        def weigh(t, to):
                            if to is ctx:
                                pe.wait_ge(p_ready, 64 * b + 16 * j + 4 * t + 4)
                                if t == 0:
                                    pe.wait_ge(ctx_taken, 8 * b + 2 * j)
                            for a in range(4):
                                w = v[:, t, j * P + HN * a:j * P + HN * (a + 1)] if to is ctx else ones[:, :]
                                mm = pe.matmul(to[HN * a:HN * (a + 1), :], w, prob[:, 4 * (t % 2) + a, :],
                                               start=(t == 0), stop=(t == TB - 1))
                            mm.then_inc(pv_done, 1)

                        for t in range(TB + 1):
                            for a, to in ((0, ctx), (2, den)):
                                if t < TB:
                                    score_t(t, a)
                                    score_t(t, a + 1)
                                if t > 0:
                                    weigh(t - 1, to)

            @block.scalar
            def _(act):
                def center(b):
                    wait_alone(act, transposed, b, k.passed)
                    for i in range(TB):
                        act.activation(h[:, i, :], tile_of(k.x, b * TB + i), ACT.Identity,
                                       scale=att.rstd[:, bass.ds(b * TB + i, 1)],
                                       bias=att.shift[:, bass.ds(b * TB + i, 1)]).then_inc(n_centered, 1)

                def body(b, last):
                    for c in (1, 3):
                        wait_full(act, b, ("hT", c))
                        act.copy(h_t[:, c, :], gen[:, G[("hT", c)] % 2, :]).then_inc(gen_free[G[("hT", c)] % 2], 1)
                    def split_hi(which, j):
                        stack = qs if which == "q" else ks
                        wait_full(act, b, (which, j))
                        act.wait_ge(st_full, 64 * b + 16 * max(j - 1, 0))
                        for a in range(4):
                            act.activation(stack[0:HN, j % 2, a, :],
                                           gen[HN * a:HN * (a + 1), G[(which, j)] % 2, :],
                                           ACT.Copy).then_inc(hi_done, 1)

                    split_hi("q", 0)
                    split_hi("k", 0)
                    act.wait_ge(pv_done, 32 * b)
                    for t in (1, 3):
                        wait_full(act, b, ("v", t))
                        act.copy(v[:, t, :], gen[:, G[("v", t)] % 2, :]).then_inc(gen_free[G[("v", t)] % 2], 1)

                    for j in range(QUADS):
                        if j + 1 < QUADS:
                            split_hi("q", j + 1)
                        if j == 1 and not last:
                            center(b + 1)
                        for a in range(4):
                            act.wait_ge(row_full, 16 * b + 4 * j + a + 1)
                            act.activation(qs[96:97, j % 2, a, :], sc[0:1, a % 2, :], ACT.Copy,
                                           scale=-1.0).then_inc(row_taken, 1)
                        for t in range(TB):
                            for a in range(4):
                                s = 16 * j + 4 * t + a
                                act.wait_ge(st_full, 64 * b + s + 1)
                                act.wait_ge(pv_done, 32 * b + 2 * max(4 * j + t - 1, 0))
                                act.activation(prob[:, 4 * (t % 2) + a, :], scT[:, s % 2, :], ACT.Exp,
                                               scale=NORM).then_inc(p_ready, 1)
                            if t == 0 and j + 1 < QUADS:
                                split_hi("k", j + 1)
                        act.wait_ge(pv_done, 32 * b + 8 * j + 8)
                        act.wait_ge(ctx_done, 4 * b + j)
                        act.copy(den_raw[:, :], den[:, :]).then_inc(ctx_taken, 1)
                        act.copy(ctx_raw[:, :], ctx[:, :]).then_inc(ctx_taken, 1)

                center(0)
                batch_loop(act, body)

            @block.vector
            def _(dve):
                with dve.Fori(0, B) as b:
                    for c in (0, 2):
                        wait_full(dve, b, ("hT", c))
                        dve.tensor_copy(h_t[:, c, :], gen[:, G[("hT", c)] % 2, :]
                                        ).then_inc(gen_free[G[("hT", c)] % 2], 1)
                    wait_full(dve, b, ("hT", 3))
                    dve.nop().then_inc(transposed, 1)
                    def split_lo(which, j):
                        stack, lo, dup = (qs, HN, 2 * HN) if which == "q" else (ks, 2 * HN, HN)
                        g = G[(which, j)]
                        dve.wait_ge(st_full, 64 * b + 16 * max(j - 1, 0))
                        for a in range(4):
                            dve.wait_ge(hi_done, 32 * b + 8 * j + 4 * (which == "k") + a + 1)
                            dve.tensor_copy(stack[dup:dup + HN, j % 2, a, :], stack[0:HN, j % 2, a, :].bitcast(F32))
                            last = dve.tensor_tensor(stack[lo:lo + HN, j % 2, a, :],
                                                     gen[HN * a:HN * (a + 1), g % 2, :],
                                                     stack[0:HN, j % 2, a, :].bitcast(F32), ALU.subtract)
                        last.then_inc(gen_free[g % 2], 1)

                    def normalize(j):
                        dve.wait_ge(ctx_taken, 8 * b + 2 * j + 2)
                        dve.reciprocal(rec[:, :], den_raw[:, :]).then_inc(recip_done, 1)
                        dve.wait_ge(recip_done, 4 * b + j + 1)
                        dve.tensor_tensor(flat(ctx_t[:, j, bass.ds(b, 1), :]), ctx_raw[:, :], rec[:, :],
                                          ALU.mult).then_inc(ctx_done, 1)

                    split_lo("q", 0)
                    split_lo("k", 0)
                    dve.wait_ge(pv_done, 32 * b)
                    for t in (0, 2):
                        wait_full(dve, b, ("v", t))
                        dve.tensor_copy(v[:, t, :], gen[:, G[("v", t)] % 2, :]).then_inc(gen_free[G[("v", t)] % 2], 1)

                    for j in range(QUADS):
                        for s in range(16):
                            dve.wait_ge(scores_full, 64 * b + 16 * j + s + 1)
                            dve.tensor_reduce(mx[:, s:s + 1], sc[:, s % 2, :], AX.X, ALU.max).then_inc(max_done, 1)
                        if j + 1 < QUADS:
                            split_lo("q", j + 1)
                            split_lo("k", j + 1)
                        if j > 0:
                            normalize(j - 1)
                    normalize(QUADS - 1)


class NormPass:

    def __init__(self, k, st, name, *which, sems, before=0):
        self.k, self.which, self.before = k, which, before
        self.gate_loaded, self.mod_loaded = k.sem(f"{sems}_gate_loaded"), k.sem(f"{sems}_mod_loaded")
        self.mod = k.sb(f"{name}_mod", [P, 3, D], stack=st)
        self.delta = k.sb(f"{name}_delta", [P, TB, D], stack=st)
        self.delta_ready, self.gated, self.added = (k.sem(f"{sems}_{s}") for s in ("delta_ready", "gated", "added"))
        self.h = k.sb(f"{name}_h", [P, TB, D], stack=st)
        self.stats = k.sb(f"{name}_stats", [P, TB, 6], stack=st)
        self.mean_var = k.sb(f"{name}_mean_var", [P, TB, 2], stack=st)
        self.sd = k.sb(f"{name}_sd", [P, TB], stack=st)
        self.rstd = k.sb(f"{name}_rstd", [P, TB], stack=st)
        self.stats_done, self.var_done, self.sd_done, self.rstd_done, self.centered, self.scaled, self.h_ready = (
            k.sem(f"{sems}_{s}") for s in ("stats_done", "var_done", "sd_done", "rstd_done", "centered", "scaled", "h_ready"))

    def count(self, b, tiles=0):
        return TB * (self.before + b) + tiles

    def load_gate(self, eng, b):
        eng.wait_ge(self.gated, self.count(b))
        eng.dma_start(self.mod[:, 0, :], self.k.mod_tile(*self.which[0], b)).then_inc(self.gate_loaded, 16)

    def load_mod(self, eng, b):
        eng.wait_ge(self.h_ready, self.count(b))
        for n in (1, 2):
            eng.dma_start(self.mod[:, n, :], self.k.mod_tile(*self.which[n], b)).then_inc(self.mod_loaded, 16)

    def wait_gate(self, eng, b):
        eng.wait_ge(self.gate_loaded, 16 * (self.before + b + 1))

    def wait_mod(self, eng, b):
        eng.wait_ge(self.mod_loaded, 32 * (self.before + b + 1))

    def gate(self, pool, b):
        self.wait_gate(pool, b)
        for i in range(TB):
            pool.wait_ge(self.delta_ready, self.count(b, i + 1))
            pool.tensor_tensor(self.delta[:, i, :], self.delta[:, i, :], self.mod[:, 0, :],
                               ALU.mult).then_inc(self.gated, 1)

    def add(self, dve, b):
        for i in range(TB):
            x = tile_of(self.k.x, b * TB + i)
            dve.wait_ge(self.gated, self.count(b, i + 1))
            dve.tensor_tensor(x, x, self.delta[:, i, :], ALU.add).then_inc(self.added, 1)

    def statistics(self, dve, b):
        wait_alone(dve, self.added, self.count(b, TB), self.k.passed)
        for i in range(TB):
            dve.bn_stats(self.stats[:, i, :], tile_of(self.k.x, b * TB + i)).then_inc(self.stats_done, 1)
        wait_alone(dve, self.stats_done, self.count(b, TB), self.k.passed)
        for i in range(TB):
            dve.bn_aggr(self.mean_var[:, i, :], self.stats[:, i, :]).then_inc(self.var_done, 1)

    def root(self, act, b):
        act.wait_ge(self.var_done, self.count(b, TB))
        act.activation(self.sd[:, :], self.mean_var[:, :, 1], ACT.Sqrt, bias=self.k.eps[:, 0:1]).then_inc(self.sd_done, 1)

    def center(self, dve, b):
        dve.wait_ge(self.sd_done, self.before + b + 1)
        dve.reciprocal(self.rstd[:, :], self.sd[:, :]).then_inc(self.rstd_done, 1)
        dve.wait_ge(self.rstd_done, self.before + b + 1)
        for i in range(TB):
            dve.tensor_scalar(self.h[:, i, :], tile_of(self.k.x, b * TB + i), self.mean_var[:, i, 0:1],
                              self.rstd[:, i:i + 1], ALU.subtract, ALU.mult).then_inc(self.centered, 1)

    def scale(self, pool, b):
        self.wait_mod(pool, b)
        for i in range(TB):
            pool.wait_ge(self.centered, self.count(b, i + 1))
            pool.tensor_tensor(self.h[:, i, :], self.h[:, i, :], self.mod[:, 1, :], ALU.mult).then_inc(self.scaled, 1)

    def shift(self, dve, b):
        self.wait_mod(dve, b)
        for i in range(TB):
            dve.wait_ge(self.scaled, self.count(b, i + 1))
            dve.tensor_tensor(self.h[:, i, :], self.h[:, i, :], self.mod[:, 2, :], ALU.add).then_inc(self.h_ready, 1)


class RouterPass:

    def __init__(self, k, st, name, w_name, norm, logits, before=0):
        self.k, self.norm, self.logits, self.w_name, self.before = k, norm, logits, w_name, before
        self.w_loaded = k.sem(f"{name}_w_loaded")
        self.w = k.sb(f"{name}_w", [P, KC, E], stack=st)
        self.h_t = k.sb(f"{name}_h_t", [P, 2, KC, P], stack=st)
        self.t_psum = k.ps(f"{name}_t_psum", [P, 2, KC, P], st)
        self.l_psum = k.ps(f"{name}_l_psum", [P, TB, E], st)
        self.t_full, self.t_taken, self.tile_routed, self.logits_taken = (
            k.sem("router_t_full"), k.sem("router_t_taken"), k.sem("router_tile_routed"), k.sem("router_logits_taken"))

    def count(self, b, tiles=0):
        return TB * (self.before + b) + tiles

    def load(self, eng):
        eng.dma_start(self.w[:, :, :], self.k.ins[self.w_name]).then_inc(self.w_loaded, 16)

    def tensor(self, pe, b):
        pe.wait_ge(self.w_loaded, 16)

        def logits_of(i):
            pe.wait_ge(self.t_taken, self.count(b, i + 1))
            for c in range(KC):
                mm = pe.matmul(self.l_psum[:, i, :], self.h_t[:, i % 2, c, :], self.w[:, c, :],
                               start=(c == 0), stop=(c == KC - 1))
            mm.then_inc(self.tile_routed, 1)

        for i in range(TB):
            pe.wait_ge(self.norm.h_ready, self.norm.count(b, i + 1))
            pe.wait_ge(self.t_taken, self.count(b, max(i - 1, 0)))
            for c in range(KC):
                mm = pe.transpose(self.t_psum[:, i % 2, c, :], self.norm.h[:, i, c * P:(c + 1) * P], self.k.ident[:, :])
            mm.then_inc(self.t_full, 1)
            if i == 0:
                pe.wait_ge(self.logits_taken, self.before + b)
            else:
                logits_of(i - 1)
        logits_of(TB - 1)

    def scalar(self, act, b):
        for i in range(TB):
            act.wait_ge(self.t_full, self.count(b, i + 1))
            act.wait_ge(self.tile_routed, self.count(b, max(i - 1, 0)))
            act.copy(self.h_t[:, i % 2, :, :], self.t_psum[:, i % 2, :, :]).then_inc(self.t_taken, 1)
        act.wait_ge(self.tile_routed, self.count(b, TB))
        act.copy(self.logits[:, bass.ds(b * TB, TB), :], self.l_psum[:, :, :]).then_inc(self.logits_taken, 1)

    def wait_h_free(self, dve, b):
        dve.wait_ge(self.t_full, self.count(b))


def project_and_norm0(k, ctx_t, logits, h_rows):
    nc, ins = k.nc, k.ins
    w_loaded, ctx_ready, proj_full, stored = (
        k.sem("p_w_loaded"), k.sem("p_ctx_ready"), k.sem("p_proj_full"), k.sem("p_h_stored"))
    with ExitStack() as st:
        w = k.sb("wproj_sb", [P, KC, D], stack=st)
        bias = k.sb("bproj_tile", [P, D], stack=st)
        cj = k.sb("ctx_batch", [P, KC, S], stack=st)
        pp = k.ps("proj_psum", [P, TB, D], st)
        norm = NormPass(k, st, "n0", (0, GA), (0, CB), (0, SB_), sems="norm_a")
        router = RouterPass(k, st, "r0", "gate_w", norm, logits)

        with nc.Block() as block:
            @block.sync
            def _(sp):
                sp.dma_start(w[:, :, :], ins["wproj"]).then_inc(w_loaded, 16)
                sp.dma_start(bias[:, :], ins["bproj"].broadcast_to([P, D])).then_inc(w_loaded, 16)
                norm.load_gate(sp, 0)
                norm.load_mod(sp, 0)
                router.load(sp)

                def body(b, last):
                    if not last:
                        norm.load_gate(sp, b + 1)
                    for i in range(TB):
                        sp.wait_ge(norm.h_ready, norm.count(b, i + 1))
                        sp.dma_start(h_rows(b, i), norm.h[:, i, :]).then_inc(stored, 16)
                    if not last:
                        norm.load_mod(sp, b + 1)

                batch_loop(sp, body)
                sp.wait_ge(stored, 16 * NT)

            @block.gpsimd
            def _(pool):
                with pool.Fori(0, B) as b:
                    norm.gate(pool, b)
                    norm.scale(pool, b)

            @block.tensor
            def _(pe):
                def project(b, first):
                    pe.wait_ge(ctx_ready, b + 1)
                    for i in range(TB):
                        if not first:
                            pe.wait_ge(norm.delta_ready, norm.count(b - 1, i + 1))
                        for c in range(KC):
                            mm = pe.matmul(pp[:, i, :], cj[:, c, i * P:(i + 1) * P], w[:, c, :],
                                           start=(c == 0), stop=(c == KC - 1))
                        mm.then_inc(proj_full, 1)

                def body(b, last):
                    if not last:
                        project(b + 1, False)
                    router.tensor(pe, b)

                pe.wait_ge(w_loaded, 32)
                project(0, True)
                batch_loop(pe, body)

            @block.scalar
            def _(act):
                act.copy(cj[:, :, :], ctx_t[:, 0, :, :]).then_inc(ctx_ready, 1)

                def body(b, last):
                    if not last:
                        act.wait_ge(proj_full, TB * b + TB)
                        act.copy(cj[:, :, :], ctx_t[:, bass.ds(b + 1, 1), :, :].rearrange("p a c s -> p (a c) s")
                                 ).then_inc(ctx_ready, 1)
                    norm.root(act, b)
                    router.scalar(act, b)

                batch_loop(act, body)

            @block.vector
            def _(dve):
                dve.wait_ge(w_loaded, 32)
                with dve.Fori(0, B) as b:
                    for i in range(TB):
                        dve.wait_ge(proj_full, TB * b + i + 1)
                        dve.tensor_tensor(norm.delta[:, i, :], pp[:, i, :], bias[:, :], ALU.add
                                          ).then_inc(norm.delta_ready, 1)
                    norm.add(dve, b)
                    norm.statistics(dve, b)
                    router.wait_h_free(dve, b)
                    dve.wait_ge(stored, 16 * TB * b)
                    norm.center(dve, b)
                    norm.shift(dve, b)


class Routing:

    def __init__(self, k, name, stack):
        self.weight = k.sb(f"{name}_weight", [P, 2, NT], stack=stack)
        self.steps = 0
        self.filled = k.sb(f"{name}_filled", [P, E], I32, stack=stack)
        self.scatter_row = k.sb(f"{name}_scatter_row", [P, 2, NT], U32, stack=stack)
        self.gather_row = k.sb(f"{name}_gather_row", [P, 2, NT], U32, stack=stack)


class Scatter:

    RING = 4

    def __init__(self, k, st, layer, h_rows, routing, dispatch):
        self.layer, self.h_rows, self.routing, self.dispatch = layer, h_rows, routing, dispatch
        self.h = k.sb(f"scatter_ring{layer}", [P, self.RING, D], stack=st)
        self.loaded = [k.sem(f"scatter_loaded{i}") for i in range(self.RING)]
        self.scattered = [k.sem(f"scatter_done{i}") for i in range(self.RING)]

    def uses(self, t):
        return NT // self.RING * self.layer + t // self.RING

    def load(self, eng, t):
        if t >= self.RING:
            eng.wait_ge(self.scattered[t % self.RING], 16 * 2 * self.uses(t))
        eng.dma_start(self.h[:, t % self.RING, :], self.h_rows(t // TB, t % TB)).then_inc(self.loaded[t % self.RING], 16)

    def scatter(self, pool, t):
        pool.wait_ge(self.loaded[t % self.RING], 16 * (self.uses(t) + 1))
        for c in range(2):
            pool.indirect_dma_start(
                out=self.dispatch,
                out_offset=bass.IndirectOffsetOnAxis(ap=self.routing.scatter_row[:, c, t:t + 1], axis=0),
                in_=self.h[:, t % self.RING, :], in_offset=None, bounds_check=self.dispatch.shape[0] - 1,
                oob_is_err=False,
            ).then_inc(self.scattered[t % self.RING], 16)

    def wait_done(self, eng):
        for s in self.scattered:
            eng.wait_ge(s, 16 * 2 * self.uses(NT))


def route(k, name, layer, logits, routing, make_scatter=None, tile_expert=None, weights=None):
    nc = k.nc
    exp_in, exp_out, onehot_done, counted = (
        k.sem("route_exp_in"), k.sem("route_exp_out"), k.sem("route_onehot_done"), k.sem("route_counted"))
    step_done, rows_done = k.sem("route_step"), k.sem("route_rows_done")
    iota_done, consts = k.sem(f"{name}_iota_done"), k.sem(f"{name}_consts")
    HUGE = float(1 << 20)
    NK = 2 * E * NT
    with ExitStack() as st:
        def sb(n, shape, dtype=F32):
            return k.sb(f"{name}_{n}", shape, dtype, stack=st)

        mods = Modulation(k, st, 1) if layer == 0 else None
        scatter = make_scatter(st) if layer == 1 else None
        before = sb("before", [P, P])
        ones = sb("ones", [P, P])
        running = sb("running", [P, 2 * E, NT])
        iotas = sb("iotas", [P, 2 * E + TILES1], I32)
        iotas_f = sb("iotas_f", [P, 2 * E + TILES1])
        stat = sb("stat", [P, 4, NT])
        best = sb("best", [P, NT, 8])
        index = sb("index", [P, NT, 8], U32)
        index_f = sb("index_f", [P, NT, 8])
        onehot = sb("onehot", [P, 2, E, NT])
        total = sb("total", [P, 2, E, NT])
        incl = sb("incl", [P, 2, E, NT])
        place = sb("place", [P, 2, E, NT])
        prod = sb("prod", [P, 2, E, NT])
        pos = sb("pos", [P, 2, NT])
        base = sb("base", [P, 2, E])
        row = sb("row", [P, 2, NT])
        keep = sb("keep", [P, 2, NT])
        counts = sb("counts", [P, 4, E])
        counts_i = sb("counts_i", [P, E], I32)
        cmp = sb("cmp", [P, TILES1, E])
        te = sb("te", [P, TILES1])
        cp = k.ps(f"{name}_count_psum", [P, 2, NK], st)

        def over_e(ap):
            return ap.rearrange("p (t a) -> p t a", a=1).broadcast_to([P, NT, E])

        def ket(ap):
            return ap.rearrange("p k e t -> p (k e) t")

        with nc.Block() as block:
            @block.sync
            def _(sp):
                if layer == 0:
                    mods.load_c(sp)
                    mods.load_w(sp)
                    mods.store(sp)
                else:
                    for t in range(NT):
                        scatter.load(sp, t)

            @block.gpsimd
            def _(pool):
                pool.iota(iotas[:, 0:E], [[1, E]], base=0, channel_multiplier=0).then_inc(iota_done, 1)
                pool.wait_ge(iota_done, 1)
                pool.iota(iotas[:, E:2 * E], [[REGION, E]], base=0, channel_multiplier=0).then_inc(iota_done, 1)
                pool.wait_ge(iota_done, 2)
                pool.iota(iotas[:, 2 * E:], [[P, TILES1]], base=0, channel_multiplier=0).then_inc(iota_done, 1)
                pool.memset(ones[:, :], 1.0).then_inc(consts, 1)
                pool.memset(before[:, :], 1.0).then_inc(consts, 1)
                pool.memset(running[:, :, :], 1.0).then_inc(consts, 1)
                pool.wait_ge(consts, 3)
                pool.memset(running[:, :, 0:1], 0.0).then_inc(consts, 1)
                pool.affine_select(out=before[:, :], in_=before[:, :], compare_op=ALU.is_gt, fill=0.0,
                                   base=0, pattern=[[1, P]], channel_multiplier=-1).then_inc(consts, 1)
                if layer == 1:
                    pool.wait_ge(rows_done, 1)
                    for t in range(NT):
                        scatter.scatter(pool, t)
                    scatter.wait_done(pool)

            @block.scalar
            def _(act):
                if weights:
                    weights.load_gate_up(act)
                act.wait_ge(exp_in, layer + 1)
                act.activation(logits[:, :, :], logits[:, :, :], ACT.Exp).then_inc(exp_out, 1)
                if layer == 0:
                    mods.activate(act)

            @block.tensor
            def _(pe):
                pe.wait_ge(consts, 5)
                pe.wait_ge(onehot_done, 2 * (layer + 1))
                pe.matmul(cp[:, 0, :], before[:, :], onehot.rearrange("p k e t -> p (k e t)"), start=True, stop=True)
                pe.matmul(cp[:, 1, :], ones[:, :], onehot.rearrange("p k e t -> p (k e t)"), start=True,
                          stop=True).then_inc(counted, 1)
                if layer == 0:
                    mods.multiply(pe)

            @block.vector
            def _(dve):
                def step(ins):
                    routing.steps += 1
                    ins.then_inc(step_done, 1)
                    dve.wait_ge(step_done, routing.steps)

                dve.wait_ge(iota_done, 3)
                step(dve.tensor_copy(iotas_f[:, :], iotas[:, :]))
                top, total_p, inv, both = (stat[:, n, :] for n in range(4))
                step(dve.tensor_reduce(top, logits[:, :, :], AX.X, ALU.max))
                dve.tensor_tensor(logits[:, :, :], logits[:, :, :], over_e(top), ALU.subtract).then_inc(exp_in, 1)
                dve.wait_ge(exp_out, layer + 1)
                step(dve.tensor_reduce(total_p, logits[:, :, :], AX.X, ALU.add))
                step(dve.reciprocal(inv, total_p))
                step(dve.tensor_tensor(logits[:, :, :], logits[:, :, :], over_e(inv), ALU.mult))
                for t in range(NT):
                    last = dve.max(best[:, t, :], logits[:, t, :])
                step(last)
                for t in range(NT):
                    last = dve.max_index(index[:, t, :], best[:, t, :], logits[:, t, :])
                step(last)
                step(dve.tensor_copy(index_f[:, :, :], index[:, :, :]))
                for c in range(2):
                    ids = iotas_f[:, 0:E].rearrange("p (a e) -> p a e", a=1).broadcast_to([P, NT, E])
                    dve.tensor_tensor(onehot[:, c, :, :].rearrange("p e t -> p t e"), ids,
                                      over_e(index_f[:, :, c]), ALU.is_equal).then_inc(onehot_done, 1)
                dve.wait_ge(counted, layer + 1)
                dve.wait_ge(consts, 5)
                step(dve.tensor_copy(total.rearrange("p k e t -> p (k e t)"), cp[:, 1, :]))
                step(dve.tensor_tensor_scan(incl.rearrange("p k e t -> p (k e t)"),
                                            running.rearrange("p a t -> p (a t)"),
                                            total.rearrange("p k e t -> p (k e t)"), 0.0, ALU.mult, ALU.add))
                step(dve.tensor_tensor(ket(place), ket(incl), ket(total), ALU.subtract))
                step(dve.tensor_tensor(place.rearrange("p k e t -> p (k e t)"),
                                       place.rearrange("p k e t -> p (k e t)"), cp[:, 0, :], ALU.add))
                step(dve.tensor_tensor(ket(prod), ket(onehot), ket(place), ALU.mult))
                for c in range(2):
                    step(dve.tensor_reduce(pos[:, c, :], prod[:, c, :, :].rearrange("p e t -> p t e"), AX.X, ALU.add))
                n_first, n_second = incl[:, 0, :, NT - 1], incl[:, 1, :, NT - 1]
                if layer == 0:
                    step(dve.tensor_copy(base[:, 0, :], iotas_f[:, E:2 * E]))
                    step(dve.tensor_scalar(counts[:, 0, :], n_first, float(CAP), None, ALU.min))
                    step(dve.tensor_tensor(base[:, 1, :], base[:, 0, :], counts[:, 0, :], ALU.add))
                    step(dve.tensor_scalar(counts[:, 1, :], n_second, float(CAP), None, ALU.min))
                    step(dve.tensor_tensor(routing.filled[:, :], counts[:, 0, :], counts[:, 1, :], ALU.add))
                else:
                    step(dve.tensor_tensor(counts[:, 0, :], n_first, n_second, ALU.add))
                    step(dve.tensor_scalar(counts_i[:, :], counts[:, 0, :], float(P - 1), None, ALU.add))
                    step(dve.tensor_scalar(counts_i[:, :], counts_i[:, :], P.bit_length() - 1, None,
                                           ALU.logical_shift_right))
                    step(dve.tensor_copy(counts[:, 1, :], counts_i[:, :]))
                    step(dve.tensor_tensor_scan(counts[:, 2, :], ones[:, 0:E], counts[:, 1, :], 0.0, ALU.mult, ALU.add))
                    step(dve.tensor_tensor(counts[:, 3, :], counts[:, 2, :], counts[:, 1, :], ALU.subtract))
                    step(dve.tensor_scalar(base[:, 0, :], counts[:, 3, :], float(P), None, ALU.mult))
                    step(dve.tensor_tensor(base[:, 1, :], base[:, 0, :], n_first, ALU.add))
                    tiles = iotas_f[:, 2 * E:].rearrange("p (t a) -> p t a", a=1).broadcast_to([P, TILES1, E])
                    starts = base[:, 0, :].rearrange("p (a e) -> p a e", a=1).broadcast_to([P, TILES1, E])
                    step(dve.tensor_tensor(cmp[:, :, :], tiles, starts, ALU.is_ge))
                    step(dve.tensor_reduce(te[:, :], cmp[:, :, :], AX.X, ALU.add))
                    step(dve.tensor_scalar(tile_expert[:, :], te[:, :], -1.0, None, ALU.add))
                step(dve.tensor_tensor(ket(prod), ket(onehot),
                                       base.rearrange("p k (e a) -> p (k e) a", a=1).broadcast_to([P, 2 * E, NT]),
                                       ALU.mult))
                for c in range(2):
                    step(dve.tensor_reduce(row[:, c, :], prod[:, c, :, :].rearrange("p e t -> p t e"), AX.X, ALU.add))
                step(dve.tensor_tensor(row[:, :, :], row[:, :, :], pos[:, :, :], ALU.add))
                w = routing.weight
                if layer == 0:
                    step(dve.tensor_scalar(keep[:, :, :], pos[:, :, :], float(CAP), None, ALU.is_lt))
                    for c in range(2):
                        step(dve.tensor_tensor(w[:, c, :], best[:, :, c], keep[:, c, :], ALU.mult))
                    step(dve.tensor_tensor(pos[:, :, :], row[:, :, :], keep[:, :, :], ALU.mult))
                    step(dve.tensor_copy(routing.gather_row[:, :, :], pos[:, :, :]))
                    step(dve.tensor_scalar(keep[:, :, :], keep[:, :, :], -HUGE, HUGE, ALU.mult, ALU.add))
                    step(dve.tensor_tensor(row[:, :, :], row[:, :, :], keep[:, :, :], ALU.add))
                else:
                    step(dve.tensor_tensor(both, best[:, :, 0], best[:, :, 1], ALU.add))
                    step(dve.reciprocal(inv, both))
                    for c in range(2):
                        step(dve.tensor_tensor(w[:, c, :], best[:, :, c], inv, ALU.mult))
                    step(dve.tensor_copy(routing.gather_row[:, :, :], row[:, :, :]))
                last = dve.tensor_copy(routing.scatter_row[:, :, :], row[:, :, :])
                if layer == 1:
                    last.then_inc(rows_done, 1)
                else:
                    mods.finish(dve)


def experts0(k, routing, make_scatter):
    nc, ins = k.nc, k.ins
    STEPS = FC + 1
    GROUP = 4
    GROUPS = FC // GROUP
    HALF = REGION // 2

    def sem(n):
        return k.sem(f"e0_{n}")

    small_loaded, x_loaded, branch_loaded = sem("small_loaded"), sem("x_loaded"), sem("branch_loaded")
    w_loaded = [sem(f"w_loaded{i}") for i in range(2)]
    xt_full, xt5_full, xt_hi, xt5_hi, xt_split = (
        sem("xt_full"), sem("xt5_full"), sem("xt_hi"), sem("xt5_hi"), sem("xt_split"))
    branch_hi, branch_split, w1_hi, w1_split, w2_hi, w2_split = (
        sem("branch_hi"), sem("branch_split"), sem("w1_hi"), sem("w1_split"), sem("w2_hi"), sem("w2_split"))
    h_full, gelu_done, g_hi, g_split = sem("h_full"), sem("gelu_done"), sem("g_hi"), sem("g_split")
    y_done, y_taken, y_stored, consts = sem("y_done"), sem("y_taken"), sem("y_stored"), sem("consts")

    with ExitStack() as st:
        def sb(n, shape, dtype=F32):
            return k.sb(f"e0_{n}", shape, dtype, stack=st)

        scatter = make_scatter(st)
        assert NT == FC
        x_raw = sb("x_raw", [P, 5, D])
        xh, xl = sb("x_hi", [P, KC, REGION], F32R), sb("x_lo", [P, KC, REGION], F32R)
        w1_raw, w2_raw = sb("w1_raw", [P, 2, GROUP, KC * P]), sb("w2_raw", [P, 2, GROUP, D])
        w1h, w1l = sb("w1_hi", [P, 2, KC, P], F32R), sb("w1_lo", [P, 2, KC, P], F32R)
        w2h, w2l = sb("w2_hi", [P, 2, D], F32R), sb("w2_lo", [P, 2, D], F32R)
        g_raw = sb("g_raw", [P, 2, REGION])
        gh, gl = sb("g_hi", [P, 2, REGION], F32R), sb("g_lo", [P, 2, REGION], F32R)
        a_raw = sb("branch_g_raw", [RANK, REGION])
        ah, al = sb("branch_g_hi", [P, REGION], F32R), sb("branch_g_lo", [P, REGION], F32R)
        wub_raw = sb("wu_b2_raw", [RANK + 1, D])
        wubh, wubl = sb("wu_b2_hi", [P, D], F32R), sb("wu_b2_lo", [P, D], F32R)
        wd_raw = sb("wd_raw", [P, E + 1, KC * RANK])
        wdh, wdl = sb("wd_hi", [P, KC, RANK], F32R), sb("wd_lo", [P, KC, RANK], F32R)
        b1 = sb("b1_sb", [P, (E + 1) * FC])
        y_sb = sb("y_sb", [P, 5, D])
        y = k.ps("e0_y", [P, 5, D], st)
        hb = k.ps("e0_h", [P, 3, S], st)

        def region(rows, v, tiles):
            shared, experts = rows
            if tiles == 4:
                return shared.rearrange("(r t p) d -> r p t d", r=B, p=P)[bass.ds(v, 1)].rearrange("a p t d -> (a p) t d")
            return experts.rearrange("(r t p) d -> r p t d", r=E, p=P)[bass.ds(v - B, 1)].rearrange("a p t d -> (a p) t d")

        def splits(v, tiles):
            return 4 * v if tiles == 4 else 5 * v - B

        def of_expert(ap, w):
            if isinstance(w, int):
                return ap[w]
            return ap[bass.ds(w, 1)].rearrange("a p n -> (a p) n")

        def loops(eng, body):
            body(0, 0, 4, (0, 4))
            with eng.Fori(1, B - 1) as v:
                body(v, 0, 4, (0, 4))
            body(B - 1, 0, 4, (1, 5))
            with eng.Fori(B, B + E - 1) as v:
                body(v, v - (B - 1), 5, (v - (B - 2), 5))
            body(B + E - 1, E, 5, None)

        def half_of(tiles, half):
            n = tiles * P // 2
            return n, slice(half * n, (half + 1) * n)

        def by_filling(eng, v, tiles, steps):
            if tiles == 4:
                return steps(4)
            filled = eng.value_load(routing.filled[0:1, bass.ds(v - B, 1)], min_val=0, max_val=REGION)
            with eng.If(filled > 4 * P):
                steps(5)
            with eng.Else():
                steps(4)

        def order(tiles):
            return (0, 1, 2, 3) if tiles == 4 else (0, 1, None, 2, 3)

        with nc.Block() as block:
            @block.sync
            def _(sp):
                sp.dma_start(wd_raw[:, :, :], ins["wd"]).then_inc(small_loaded, 16)
                sp.dma_start(b1[:, :], ins["b1"]).then_inc(small_loaded, 16)

                def load_x(v, w, tiles):
                    sp.dma_start(x_raw[:, 0:tiles, :], region((k.h_rows0, k.dispatch), v, tiles)).then_inc(x_loaded, 16)
                    sp.dma_start(wub_raw[:, :], of_expert(ins["wu_b2"], w)).then_inc(branch_loaded, 16)

                def body(v, w, tiles, after):
                    for g in range(GROUPS):
                        done = FC * v + (GROUP * (g - 1) if g >= 2 else 0)
                        sp.wait_ge(w1_split, done)
                        sp.wait_ge(w2_split, done)
                        for raw, name in ((w1_raw, "w1"), (w2_raw, "w2")):
                            sp.dma_start(raw[:, g % 2, :, :].rearrange("p c n -> p (c n)"),
                                         of_expert(ins[name][:, g], w)).then_inc(w_loaded[g % 2], 16)
                        if g == 1 and after:
                            sp.wait_ge(xt_split, splits(v, tiles) + tiles)
                            sp.wait_ge(branch_split, 2 * v + 2)
                            if tiles == 4 and after[1] == 5:
                                scatter.wait_done(sp)
                            load_x(v + 1, *after)
                        if isinstance(v, int) and v == 0:
                            for t in range(GROUP * g, GROUP * (g + 1)):
                                scatter.load(sp, t)

                load_x(0, 0, 4)
                loops(sp, body)

            def wait_weights(eng, v, c):
                g = c // GROUP
                eng.wait_ge(w_loaded[g % 2], 32 * (GROUPS // 2 * v + g // 2 + 1))

            @block.gpsimd
            def _(pool):
                def body(v, w, tiles, after):
                    for c in range(FC):
                        if isinstance(v, int) and v == 0:
                            scatter.scatter(pool, c)
                        pool.wait_ge(w2_hi, FC * v + c + 1)
                        pool.tensor_tensor(w2l[:, c % 2, :], w2_raw[:, c // GROUP % 2, c % GROUP, :],
                                           w2h[:, c % 2, :].bitcast(F32), ALU.subtract).then_inc(w2_split, 1)

                loops(pool, body)

            @block.tensor
            def _(pe):
                def turn(v, tiles, c, first=False):
                    before = splits(v, tiles)
                    if c == 0:
                        pe.wait_ge(x_loaded, 16 * v + 16)
                        if not first:
                            pe.wait_ge(gelu_done, 2 * STEPS * v - 2)
                    elif c in (None, 1):
                        if not first:
                            pe.wait_ge(gelu_done, 2 * STEPS * v)
                    else:
                        pe.wait_ge(xt_split, before + c - 1)
                    if c is None:
                        for n in range(KC):
                            mm = pe.transpose(hb[:, 0, n * P:(n + 1) * P], x_raw[:, 4, n * P:(n + 1) * P], k.ident[:, :])
                        mm.then_inc(xt5_full, 1)
                    else:
                        for t in range(4):
                            mm = pe.transpose(hb[:, 1 + c % 2, t * P:(t + 1) * P],
                                              x_raw[:, t, c * P:(c + 1) * P], k.ident[:, :])
                        mm.then_inc(xt_full, 1)

                def body(v, w, tiles, after):
                    def hidden(a, used):
                        width = RANK if a == 0 else P
                        if a == 0:
                            pe.wait_ge(xt_split, splits(v, tiles) + tiles)
                            pe.wait_ge(branch_split, 2 * v + 2)
                            wh, wl = wdh, wdl
                        else:
                            pe.wait_ge(w1_split, FC * v + a)
                            wh, wl = w1h[:, (a - 1) % 2, :, :], w1l[:, (a - 1) % 2, :, :]
                        for half in range(2):
                            n, rows = half_of(used, half)
                            pe.wait_ge(gelu_done, 2 * STEPS * v + max(2 * a + half - 2, 0))
                            out = hb[0:width, (2 * a + half) % 3, 0:n]
                            for c in range(KC):
                                pe.matmul(out, wh[:, c, :], xh[:, c, rows], start=(c == 0), stop=False)
                                pe.matmul(out, wh[:, c, :], xl[:, c, rows], start=False, stop=False)
                                mm = pe.matmul(out, wl[:, c, :], xh[:, c, rows], start=False, stop=(c == KC - 1))
                            mm.then_inc(h_full, 1)

                    def output(a, used, turns={}):
                        if a == 0:
                            pe.wait_ge(y_taken, v)
                            sh, sl, wh, wl = ah, al, wubh[:, :], wubl[:, :]
                        else:
                            pe.wait_ge(w2_split, FC * v + a)
                            i = (a - 1) % 2
                            sh, sl, wh, wl = gh[:, a % 2, :], gl[:, a % 2, :], w2h[:, i, :], w2l[:, i, :]
                        pe.wait_ge(g_split, STEPS * v + a + 1)
                        span = tiles if a == 0 else used
                        for t in range(span):
                            tile = slice(t * P, (t + 1) * P)
                            pe.matmul(y[:, t, :], sh[:, tile], wh, start=(a == 0), stop=False)
                            pe.matmul(y[:, t, :], sh[:, tile], wl, start=False, stop=False)
                            mm = pe.matmul(y[:, t, :], sl[:, tile], wh, start=False,
                                           stop=(a == STEPS - 1 or t >= used))
                            if t == span - 1:
                                mm.then_inc(y_done, 1)
                            for c in turns.get(t, []):
                                turn(v + 1, after[1], c)

                    def steps(used):
                        for a in range(1, STEPS):
                            hidden(a, used)
                            if a < STEPS - 1 or not after:
                                output(a - 1, used)
                        if not after:
                            output(STEPS - 1, used)
                            return
                        turn(v + 1, after[1], 0)
                        output(STEPS - 2, used, {1: [1], 3: [None] if after[1] == 5 else []})
                        output(STEPS - 1, used, {0: [2], 2: [3]})

                    hidden(0, tiles)
                    by_filling(pe, v, tiles, steps)

                for c in range(KC):
                    turn(0, 4, c, first=True)
                loops(pe, body)

            @block.scalar
            def _(act):
                def take_x(v, tiles):
                    for c in order(tiles):
                        if c is None:
                            act.wait_ge(xt5_full, v - (B - 1))
                            act.activation(xh[:, :, 4 * P:], hb[:, 0, :].rearrange("p (c n) -> p c n", c=KC), ACT.Copy).then_inc(xt5_hi, 1)
                        else:
                            act.wait_ge(xt_full, KC * v + c + 1)
                            act.activation(xh[:, c, 0:4 * P], hb[:, 1 + c % 2, :], ACT.Copy).then_inc(xt_hi, 1)

                def body(v, w, tiles, after):
                    def step(a, used):
                        if a > 0:
                            c = a - 1
                            wait_weights(act, v, c)
                            act.wait_ge(y_done, STEPS * v + (c if c >= 2 else 0))
                            act.activation(w2h[:, c % 2, :], w2_raw[:, c // GROUP % 2, c % GROUP, :],
                                           ACT.Copy).then_inc(w2_hi, 1)
                        act.wait_ge(g_split, STEPS * v + max(a - 1, 0))
                        dst = a_raw[:, :] if a == 0 else g_raw[:, a % 2, :]
                        width = RANK if a == 0 else P
                        bias = 0.0 if a == 0 else (b1[:, w * FC + a - 1:w * FC + a] if isinstance(w, int)
                                                   else b1[:, bass.ds(w * FC + (a - 1), 1)])
                        if a == 1:
                            act.wait_ge(small_loaded, 32)
                        for half in range(2):
                            n, rows = half_of(used, half)
                            wait_alone(act, h_full, 2 * (STEPS * v + a) + half + 1, k.passed)
                            act.activation(dst[:, rows], hb[0:width, (2 * a + half) % 3, 0:n], ACT.Gelu,
                                           bias=bias).then_inc(gelu_done, 1)

                    def steps(used):
                        for a in range(1, STEPS):
                            step(a, used)

                    step(0, tiles)
                    by_filling(act, v, tiles, steps)
                    if after:
                        take_x(v + 1, after[1])
                    act.wait_ge(y_done, STEPS * (v + 1))
                    act.wait_ge(y_stored, 16 * v)
                    for t in range(tiles):
                        last = act.copy(y_sb[:, t, :], y[:, t, :])
                    last.then_inc(y_taken, 1)
                    act.wait_ge(y_taken, v + 1)
                    act.dma_start(region((k.shared_out, k.expert_out), v, tiles), y_sb[:, 0:tiles, :]).then_inc(y_stored, 16)

                take_x(0, 4)
                loops(act, body)
                act.wait_ge(y_stored, 16 * (B + E))

            @block.vector
            def _(dve):
                for buf in (ah, al, wubh, wubl):
                    dve.memset(buf[32:64, :].bitcast(F32), 0.0).then_inc(consts, 1)
                    dve.memset(buf[64:128, :].bitcast(F32), 0.0).then_inc(consts, 1)
                dve.memset(g_raw[:, :, 4 * P:], 0.0).then_inc(consts, 1)
                dve.wait_ge(consts, 9)
                dve.memset(ah[32:33, :].bitcast(F32), 1.0).then_inc(consts, 1)
                dve.wait_ge(small_loaded, 32)
                dve.wait_ge(consts, 10)

                def split_branch(v, w):
                    dve.wait_ge(branch_loaded, 16 * v + 16)
                    wd = flat(wd_raw[:, bass.ds(w, 1), :]) if not isinstance(w, int) else wd_raw[:, w, :]
                    wd_h, wd_l = (x.rearrange("p c n -> p (c n)") for x in (wdh, wdl))
                    dve.tensor_copy(wd_h, wd).then_inc(branch_hi, 1)
                    dve.tensor_copy(wubh[0:RANK + 1, :], wub_raw[:, :]).then_inc(branch_hi, 1)
                    dve.wait_ge(branch_hi, 2 * v + 2)
                    dve.tensor_tensor(wd_l, wd, wd_h.bitcast(F32), ALU.subtract).then_inc(branch_split, 1)
                    dve.tensor_tensor(wubl[0:RANK + 1, :], wub_raw[:, :], wubh[0:RANK + 1, :].bitcast(F32),
                                      ALU.subtract).then_inc(branch_split, 1)

                def split_x(v, tiles):
                    for c in order(tiles):
                        if c is None:
                            dve.wait_ge(xt5_hi, v - (B - 1))
                            dve.tensor_tensor(xl[:, :, 4 * P:], hb[:, 0, :].rearrange("p (c n) -> p c n", c=KC),
                                              xh[:, :, 4 * P:].bitcast(F32),
                                              ALU.subtract).then_inc(xt_split, 1)
                        else:
                            dve.wait_ge(xt_hi, KC * v + c + 1)
                            dve.tensor_tensor(xl[:, c, 0:4 * P], hb[:, 1 + c % 2, :], xh[:, c, 0:4 * P].bitcast(F32),
                                              ALU.subtract).then_inc(xt_split, 1)

                def body(v, w, tiles, after):
                    for a in range(STEPS):
                        if a == 4 and after:
                            dve.wait_ge(y_done, STEPS * v + 1)
                            split_branch(v + 1, after[0])
                        if a < FC:
                            c = a
                            wait_weights(dve, v, c)
                            dve.wait_ge(h_full, 2 * (STEPS * v + (c if c >= 2 else 0)))
                            raw = w1_raw[:, c // GROUP % 2, c % GROUP, :]
                            hi, lo = (x[:, c % 2, :, :].rearrange("p c n -> p (c n)") for x in (w1h, w1l))
                            dve.tensor_copy(hi, raw).then_inc(w1_hi, 1)
                            dve.wait_ge(w1_hi, FC * v + c + 1)
                            dve.tensor_tensor(lo, raw, hi.bitcast(F32), ALU.subtract).then_inc(w1_split, 1)
                        n = tiles * P
                        dve.wait_ge(gelu_done, 2 * (STEPS * v + a + 1))
                        if a == 0:
                            raw, hi, lo = a_raw[:, 0:n], ah[0:RANK, 0:n], al[0:RANK, 0:n]
                        else:
                            raw, hi, lo = g_raw[:, a % 2, 0:n], gh[:, a % 2, 0:n], gl[:, a % 2, 0:n]
                            dve.wait_ge(y_done, STEPS * v + max(a - 1, 0))
                        dve.tensor_copy(hi, raw).then_inc(g_hi, 1)
                        dve.wait_ge(g_hi, STEPS * v + a + 1)
                        dve.tensor_tensor(lo, raw, hi.bitcast(F32), ALU.subtract).then_inc(g_split, 1)

                    if after:
                        split_x(v + 1, after[1])

                split_branch(0, 0)
                split_x(0, 4)
                loops(dve, body)


class Combine:

    def __init__(self, k, st, name, routing, source, norm, shared):
        self.k, self.routing, self.source, self.norm, self.shared = k, routing, source, norm, shared
        self.rows = k.sb(f"{name}_rows", [P, 2, TB, D], stack=st)
        self.index = k.sb(f"{name}_index", [P, 2, TB], U32, stack=st)
        self.shared_rows = k.sb(f"{name}_shared_rows", [P, TB, D], stack=st)
        self.gathered = [k.sem(f"combine_gathered{i}") for i in range(2)]
        self.index_ready, self.shared_loaded, self.first, self.second = (
            k.sem("combine_index_ready"), k.sem("combine_shared_loaded"), k.sem("combine_first"), k.sem("combine_second"))

    def load_shared(self, eng, b):
        eng.wait_ge(self.norm.delta_ready, self.norm.count(b))
        eng.dma_start(self.shared_rows[:, :, :],
                      self.shared[bass.ds(b, 1), 0:S, :].rearrange("a (t p) d -> p (a t) d", p=P)
                      ).then_inc(self.shared_loaded, 16)

    def gather(self, pool, b):
        pool.wait_ge(self.norm.delta_ready, self.norm.count(b))
        pool.tensor_copy(self.index[:, :, :], self.routing.gather_row[:, :, bass.ds(b * TB, TB)]
                         ).then_inc(self.index_ready, 1)
        wait_alone(pool, self.index_ready, b + 1, self.k.passed)
        for c in range(2):
            for i in range(TB):
                pool.indirect_dma_start(
                    out=self.rows[:, c, i, :], out_offset=None, in_=self.source,
                    in_offset=bass.IndirectOffsetOnAxis(ap=self.index[:, c, i:i + 1], axis=0),
                ).then_inc(self.gathered[c], 16)

    def weight(self, c, b, i):
        return self.routing.weight[:, c, bass.ds(b * TB + i, 1)]

    def first_products(self, act, b):
        act.wait_ge(self.norm.added, self.norm.count(b))
        wait_alone(act, self.gathered[0], 16 * TB * (b + 1), self.k.passed)
        for i in range(TB):
            act.activation(self.norm.delta[:, i, :], self.rows[:, 0, i, :], ACT.Copy,
                           scale=self.weight(0, b, i)).then_inc(self.first, 1)

    def sum(self, dve, b):
        delta = self.norm.delta
        dve.wait_ge(self.gathered[1], 16 * TB * (b + 1))
        for i in range(TB):
            dve.wait_ge(self.first, TB * b + i + 1)
            dve.scalar_tensor_tensor(out=delta[:, i, :], in0=self.rows[:, 1, i, :], scalar=self.weight(1, b, i),
                                     in1=delta[:, i, :], op0=ALU.mult, op1=ALU.add).then_inc(self.second, 1)
        dve.wait_ge(self.shared_loaded, 16 * (b + 1))
        for i in range(TB):
            dve.wait_ge(self.second, TB * b + i + 1)
            dve.scalar_tensor_tensor(out=delta[:, i, :], in0=self.shared_rows[:, i, :], scalar=0.2,
                                     in1=delta[:, i, :], op0=ALU.mult, op1=ALU.add
                                     ).then_inc(self.norm.delta_ready, 1)


def combine_and_attention1(k, routing, logits, h_rows, weights):
    nc = k.nc

    def sem(n):
        return k.sem(f"a1_{n}")

    BANKS = 4
    full = [sem(f"full{i}") for i in range(BANKS)]
    free = [sem(f"free{i}") for i in range(BANKS)]
    max_done, negated, inv_done, prob_done, stored = (
        sem("max_done"), sem("negated"), sem("inv_done"), sem("prob_done"), sem("stored"))
    KINDS = ("hT", "scores", "probT", "ctx")

    with ExitStack() as st:
        norm1 = NormPass(k, st, "n1", (0, GB), (1, CA), (1, SA), sems="norm_a", before=B)
        norm2 = NormPass(k, st, "n2", (1, GA), (1, CB), (1, SB_), sems="norm_b")
        combine = Combine(k, st, "c0", routing, k.expert_out, norm1,
                          shared=k.shared_out.rearrange("(r q) d -> r q d", q=S))
        router = RouterPass(k, st, "r1", "wr", norm2, logits, before=B)
        h_t = k.sb("a1_h_t", [P, KC, S], stack=st)
        prob = k.sb("a1_prob", [P, KC, D], stack=st)
        prob_t = k.sb("a1_prob_t", [P, KC, D], stack=st)
        mx = k.sb("a1_max", [P, KC], stack=st)
        neg = k.sb("a1_neg_max", [P, KC], stack=st)
        total = k.sb("a1_total", [P, KC], stack=st)
        inv = k.sb("a1_inv", [P, KC], stack=st)
        ps = k.ps("a1_psum", [P, BANKS, D], st)
        h = norm1.h

        def turn(kind, b):
            return 4 * b + KINDS.index(kind)

        def wait_full(eng, kind, n, b):
            eng.wait_ge(full[n], turn(kind, b) + 1)

        def wait_free(pe, kind, n, b):
            pe.wait_ge(free[n], turn(kind, b))

        def wait_taken(pe, kind, b):
            for n in range(4):
                pe.wait_ge(free[n], turn(kind, b) + 1)

        with nc.Block() as block:
            @block.sync
            def _(sp):
                combine.load_shared(sp, 0)
                for norm in (norm1, norm2):
                    norm.load_gate(sp, 0)
                    norm.load_mod(sp, 0)
                router.load(sp)
                sp.wait_ge(norm1.h_ready, norm1.count(0, TB))
                weights.load_down(sp)

                def body(b, last):
                    if not last:
                        norm1.load_gate(sp, b + 1)
                        norm1.load_mod(sp, b + 1)
                        combine.load_shared(sp, b + 1)
                        norm2.load_gate(sp, b + 1)
                    for i in range(TB):
                        sp.wait_ge(norm2.h_ready, norm2.count(b, i + 1))
                        sp.dma_start(h_rows(b, i), norm2.h[:, i, :]).then_inc(stored, 16)
                    if not last:
                        norm2.load_mod(sp, b + 1)

                batch_loop(sp, body)
                sp.wait_ge(stored, 16 * NT)

            @block.gpsimd
            def _(pool):
                combine.gather(pool, 0)
                norm1.gate(pool, 0)
                norm1.scale(pool, 0)

                def body(b, last):
                    if not last:
                        combine.gather(pool, b + 1)
                        norm1.gate(pool, b + 1)
                        norm1.scale(pool, b + 1)
                    norm2.scale(pool, b)

                batch_loop(pool, body)

            @block.tensor
            def _(pe):
                def turn_and_score(b):
                    pe.wait_ge(norm1.h_ready, norm1.count(b, TB))
                    for c in range(KC):
                        wait_free(pe, "hT", c, b)
                        for i in range(TB):
                            mm = pe.transpose(ps[:, c, i * P:(i + 1) * P], h[:, i, c * P:(c + 1) * P], k.ident[:, :])
                        mm.then_inc(full[c], 1)
                    for n in range(KC):
                        wait_free(pe, "scores", n, b)
                        for i in range(TB):
                            mm = pe.matmul(ps[:, n, :], h[:, i, n * P:(n + 1) * P], h[:, i, :],
                                           start=(i == 0), stop=(i == TB - 1))
                        mm.then_inc(full[n], 1)

                def body(b, last):
                    pe.wait_ge(prob_done, KC * b + KC)
                    for c in range(KC):
                        wait_free(pe, "probT", c, b)
                        for n in range(KC):
                            mm = pe.transpose(ps[:, c, n * P:(n + 1) * P], prob[:, n, c * P:(c + 1) * P], k.ident[:, :])
                        mm.then_inc(full[c], 1)
                    wait_taken(pe, "probT", b)
                    for i in range(TB):
                        for c in range(KC):
                            mm = pe.matmul(ps[:, i, :], h_t[:, c, i * P:(i + 1) * P], prob_t[:, c, :],
                                           start=(c == 0), stop=(c == KC - 1))
                        mm.then_inc(full[i], 1)
                    if not last:
                        turn_and_score(b + 1)
                    router.tensor(pe, b)

                turn_and_score(0)
                batch_loop(pe, body)

            @block.scalar
            def _(act):
                def take_turned(b):
                    for c in range(KC):
                        wait_full(act, "hT", c, b)
                        act.copy(h_t[:, c, :], ps[:, c, :]).then_inc(free[c], 1)

                combine.first_products(act, 0)
                norm1.root(act, 0)
                take_turned(0)

                def body(b, last):
                    act.wait_ge(negated, b + 1)
                    for n in range(KC):
                        act.activation(prob[:, n, :], ps[:, n, :], ACT.Exp, bias=neg[:, n:n + 1],
                                       accum_out=total[:, n:n + 1]).then_inc(free[n], 1)
                    for c in range(KC):
                        wait_full(act, "probT", c, b)
                        act.copy(prob_t[:, c, :], ps[:, c, :]).then_inc(free[c], 1)
                    if not last:
                        combine.first_products(act, b + 1)
                        norm1.root(act, b + 1)
                        take_turned(b + 1)
                    norm2.root(act, b)
                    router.scalar(act, b)

                batch_loop(act, body)

            @block.vector
            def _(dve):
                def front(b):
                    combine.sum(dve, b)
                    norm1.add(dve, b)
                    norm1.statistics(dve, b)
                    norm1.center(dve, b)
                    norm1.shift(dve, b)

                front(0)

                def body(b, last):
                    for n in range(KC):
                        wait_full(dve, "scores", n, b)
                        dve.tensor_reduce(mx[:, n:n + 1], ps[:, n, :], AX.X, ALU.max).then_inc(max_done, 1)
                    dve.wait_ge(max_done, KC * b + KC)
                    dve.tensor_scalar(neg[:, :], mx[:, :], -1.0, None, ALU.mult).then_inc(negated, 1)
                    for n in range(KC):
                        dve.wait_ge(free[n], turn("scores", b) + 1)
                    dve.reciprocal(inv[:, :], total[:, :]).then_inc(inv_done, 1)
                    dve.wait_ge(inv_done, b + 1)
                    for n in range(KC):
                        dve.tensor_scalar(prob[:, n, :], prob[:, n, :], inv[:, n:n + 1], None,
                                          ALU.mult).then_inc(prob_done, 1)
                    if not last:
                        front(b + 1)
                    dve.wait_ge(norm2.added, norm2.count(b))
                    norm2.wait_gate(dve, b)
                    for i in range(TB):
                        wait_full(dve, "ctx", i, b)
                        dve.tensor_tensor(norm2.delta[:, i, :], ps[:, i, :], norm2.mod[:, 0, :], ALU.mult
                                          ).then_inc(free[i], 1)
                    for i in range(TB):
                        dve.wait_ge(free[i], turn("ctx", b) + 1)
                    dve.sem_inc(norm2.delta_ready, TB)
                    dve.sem_inc(norm2.gated, TB)
                    norm2.add(dve, b)
                    norm2.statistics(dve, b)
                    router.wait_h_free(dve, b)
                    dve.wait_ge(stored, 16 * TB * b)
                    norm2.center(dve, b)
                    norm2.shift(dve, b)

                batch_loop(dve, body)


class Experts1Weights:

    FULL, REST = INNER // P, INNER % P

    def __init__(self, k, st):
        self.k = k
        self.gate_up_loaded, self.down_loaded = k.sem("e1_gate_up_loaded"), k.sem("e1_down_loaded")
        self.down = k.sb("e1_wd", [P, E * self.FULL, D], stack=st)
        self.down_rest = k.sb("e1_wd_rest", [self.REST, E, D], stack=st)

    def load_down(self, eng):
        for name, buf in (("wd1", self.down), ("wd1_rest", self.down_rest)):
            eng.dma_start(buf[:, :, :], self.k.ins[name]).then_inc(self.down_loaded, 16)

    def place_gate_up(self, st):
        self.gate_up = self.k.sb("e1_wgu", [P, E * KC * 2, INNER], stack=st)

    def load_gate_up(self, eng):
        eng.dma_start(self.gate_up[:, :, :], self.k.ins["wgu"]).then_inc(self.gate_up_loaded, 16)


def experts1(k, weights, tile_expert):
    nc = k.nc
    FULL, REST = weights.FULL, weights.REST
    NCH = FULL + 1

    def sem(n):
        return k.sem(f"e1_{n}")

    x_in, x_out = [sem(f"x_loaded{i}") for i in range(2)], [sem(f"y_stored{i}") for i in range(2)]
    xt_full, xt_taken, g_full, u_full, silu_done, h_ready = (
        sem("xt_full"), sem("xt_taken"), sem("g_full"), sem("u_full"), sem("silu_done"), sem("h_ready"))
    ht_full, ht_taken, y_full, y_taken = sem("ht_full"), sem("ht_taken"), sem("y_full"), sem("y_taken")
    with ExitStack() as st:
        def sb(n, shape, dtype=F32):
            return k.sb(f"e1_{n}", shape, dtype, stack=st)

        x = sb("x", [P, 2, D])
        xt = sb("xt", [P, 2, KC, P])
        g = sb("silu", [P, 2, INNER])
        h = sb("h", [P, 2, INNER])
        ht = sb("ht", [P, 2, NCH, P])
        y_sb = sb("y", [P, 2, D])
        pt = k.ps("e1_xt_psum", [P, KC, P], st)
        pgu = k.ps("e1_gu_psum", [P, 4, D], st)
        ph = k.ps("e1_ht_psum", [P, 4, P], st)
        py = k.ps("e1_y_psum", [P, D], st)

        def rows(buf, q, p):
            return buf.rearrange("(t p) d -> t p d", p=P)[bass.ds(2 * q + p, 1)].rearrange("a p d -> (a p) d")

        def after(q, p):
            return (q, 1) if p == 0 else (q + 1, 0)

        def before(q, p):
            return (q, 0) if p == 1 else (q - 1, 1)

        LAST = divmod(TILES1 - 1, 2)
        assert LAST[1] == 0

        def loop(eng, step):
            step(0, 0, True, False)
            with eng.Fori(0, LAST[0] - 1) as r:
                step(r, 1, False, False)
                step(r + 1, 0, False, False)
            step(LAST[0] - 1, 1, False, False)
            step(*LAST, False, True)

        with nc.Block() as block:
            @block.sync
            def _(sp):
                def load(q, p, first=False):
                    if not first:
                        sp.wait_ge(xt_full, 2 * q + p - 1)
                    sp.dma_start(x[:, p, :], rows(k.dispatch1, q, p)).then_inc(x_in[p], 16)

                load(0, 0, first=True)
                load(0, 1, first=True)
                with sp.Fori(1, LAST[0]) as q:
                    load(q, 0)
                    load(q, 1)
                load(*LAST)

            @block.gpsimd
            def _(pool):
                def store(q, p):
                    pool.wait_ge(y_taken, 2 * q + p + 1)
                    pool.dma_start(rows(k.expert_out1, q, p), y_sb[:, p, :]).then_inc(x_out[p], 16)

                with pool.Fori(0, LAST[0]) as q:
                    store(q, 0)
                    store(q, 1)
                store(*LAST)
                pool.wait_ge(x_out[0], 16 * (LAST[0] + 1))
                pool.wait_ge(x_out[1], 16 * LAST[0])

            @block.tensor
            def _(pe):
                pe.wait_ge(weights.gate_up_loaded, 16)
                pe.wait_ge(weights.down_loaded, 32)

                def expert(q, p):
                    return pe.value_load(tile_expert[0:1, bass.ds(2 * q + p, 1)], min_val=0, max_val=E - 1)

                def turn_x(q, p):
                    pe.wait_ge(x_in[p], 16 * (q + 1))
                    pe.wait_ge(xt_taken, 2 * q + p)
                    for c in range(KC):
                        mm = pe.transpose(pt[:, c, :], x[:, p, c * P:(c + 1) * P], k.ident[:, :])
                    mm.then_inc(xt_full, 1)

                def product(q, p, which, e, done):
                    for c in range(KC):
                        w = flat(weights.gate_up[:, bass.ds(e * (2 * KC) + (2 * c + which), 1), :])
                        mm = pe.matmul(pgu[:, 2 * p + which, 0:INNER], xt[:, p, c, :], w,
                                       start=(c == 0), stop=(c == KC - 1))
                    mm.then_inc(done, 1)

                def turn_h(q, p):
                    t = 2 * q + p
                    pe.wait_ge(h_ready, t + 1)
                    pe.wait_ge(ht_taken, t)
                    for c in range(NCH):
                        n = P if c < FULL else REST
                        mm = pe.transpose(ph[0:n, c, :], h[:, p, c * P:c * P + n], k.ident[:, :])
                    mm.then_inc(ht_full, 1)

                def down(q, p, e):
                    t = 2 * q + p
                    pe.wait_ge(ht_taken, t + 1)
                    pe.wait_ge(y_taken, t)
                    for c in range(NCH):
                        w = (flat(weights.down[:, bass.ds(e * FULL + c, 1), :]) if c < FULL
                             else flat(weights.down_rest[:, bass.ds(e, 1), :]))
                        n = P if c < FULL else REST
                        mm = pe.matmul(py[:, :], ht[0:n, p, c, :], w, start=(c == 0), stop=(c == NCH - 1))
                    mm.then_inc(y_full, 1)

                def step(q, p, first, last):
                    t, e = 2 * q + p, expert(q, p)
                    pe.wait_ge(xt_taken, t + 1)
                    if not first:
                        pe.wait_ge(h_ready, t - 1)
                    product(q, p, 0, e, g_full)
                    if not first:
                        turn_h(*before(q, p))
                    if not last:
                        turn_x(*after(q, p))
                    product(q, p, 1, e, u_full)
                    if not first:
                        down(*before(q, p), expert(*before(q, p)))

                turn_x(0, 0)
                loop(pe, step)
                turn_h(*LAST)
                down(*LAST, expert(*LAST))

            @block.scalar
            def _(act):
                def take_x(q, p, first=False):
                    act.wait_ge(xt_full, 2 * q + p + 1)
                    if not first:
                        act.wait_ge(u_full, 2 * q + p - 1)
                    act.copy(xt[:, p, :, :], pt[:, :, :]).then_inc(xt_taken, 1)

                def take_y(q, p):
                    act.wait_ge(y_full, 2 * q + p + 1)
                    act.wait_ge(x_out[p], 16 * q)
                    act.copy(y_sb[:, p, :], py[:, :]).then_inc(y_taken, 1)

                def step(q, p, first, last):
                    t = 2 * q + p
                    act.wait_ge(g_full, t + 1)
                    if not first:
                        act.wait_ge(h_ready, t - 1)
                    act.activation(g[:, p, :], pgu[:, 2 * p, 0:INNER], ACT.Silu).then_inc(silu_done, 1)
                    if not last:
                        take_x(*after(q, p))
                    if not first:
                        take_y(*before(q, p))

                take_x(0, 0, first=True)
                loop(act, step)
                take_y(*LAST)

            @block.vector
            def _(dve):
                def take_h(q, p):
                    t = 2 * q + p
                    dve.wait_ge(ht_full, t + 1)
                    dve.wait_ge(y_full, t)
                    dve.tensor_copy(ht[:, p, 0:FULL, :], ph[:, 0:FULL, :])
                    dve.tensor_copy(ht[0:REST, p, FULL, :], ph[0:REST, FULL, :]).then_inc(ht_taken, 1)

                def step(q, p, first, last):
                    t = 2 * q + p
                    if not first:
                        take_h(*before(q, p))
                    dve.wait_ge(silu_done, t + 1)
                    dve.wait_ge(u_full, t + 1)
                    if not first:
                        dve.wait_ge(ht_full, t - 1)
                    dve.tensor_tensor(h[:, p, :], g[:, p, :], pgu[:, 2 * p + 1, 0:INNER], ALU.mult).then_inc(h_ready, 1)

                loop(dve, step)
                take_h(*LAST)


def combine_to_output(k, routing):
    nc = k.nc
    gathered = [k.sem(f"combine_gathered{i}") for i in range(B)]
    first, second, gated, added = (
        k.sem("combine_first"), k.sem("combine_second"), k.sem("norm_b_gated"), k.sem("norm_b_added"))
    gates_loaded, stored = k.sem("out_gates_loaded"), k.sem("out_stored")
    with ExitStack() as st:
        gates = k.sb("out_gates", [P, B, D], stack=st)
        rows = k.sb("out_rows", [P, B, 2, TB, D], stack=st)
        delta = k.sb("out_delta", [P, 2, TB, D], stack=st)

        def weight(c, t):
            return routing.weight[:, c, t:t + 1]

        with nc.Block() as block:
            @block.sync
            def _(sp):
                for b in range(B):
                    sp.dma_start(gates[:, b, :], k.mod_tile(1, GB, b)).then_inc(gates_loaded, 16)
                for b in range(B):
                    sp.wait_ge(added, NT + TB * (b + 1))
                    sp.dma_start(k.out[b].rearrange("(t p) d -> p t d", p=P),
                                 k.x[:, b * TB:(b + 1) * TB, :]).then_inc(stored, 16)
                sp.wait_ge(stored, 16 * B)

            @block.gpsimd
            def _(pool):
                for b in range(B):
                    for c in range(2):
                        for i in range(TB):
                            t = b * TB + i
                            pool.indirect_dma_start(
                                out=rows[:, b, c, i, :], out_offset=None, in_=k.expert_out1,
                                in_offset=bass.IndirectOffsetOnAxis(ap=routing.gather_row[:, c, t:t + 1], axis=0),
                            ).then_inc(gathered[b], 16)

            @block.scalar
            def _(act):
                for b in range(B):
                    act.wait_ge(gathered[b], 16 * ((NT if b < 2 else 0) + 2 * TB))
                    if b >= 2:
                        act.wait_ge(added, NT + TB * (b - 1))
                    for i in range(TB):
                        act.activation(delta[:, b % 2, i, :], rows[:, b, 0, i, :], ACT.Copy,
                                       scale=weight(0, b * TB + i)).then_inc(first, 1)

            @block.vector
            def _(dve):
                dve.wait_ge(gates_loaded, 16 * B)
                for b in range(B):
                    d = delta[:, b % 2]
                    for i in range(TB):
                        t = b * TB + i
                        dve.wait_ge(first, NT + t + 1)
                        dve.scalar_tensor_tensor(out=d[:, i, :], in0=rows[:, b, 1, i, :], scalar=weight(1, t),
                                                 in1=d[:, i, :], op0=ALU.mult, op1=ALU.add).then_inc(second, 1)
                    for i in range(TB):
                        dve.wait_ge(second, NT + b * TB + i + 1)
                        dve.tensor_tensor(d[:, i, :], d[:, i, :], gates[:, b, :], ALU.mult).then_inc(gated, 1)
                    for i in range(TB):
                        t = b * TB + i
                        dve.wait_ge(gated, NT + t + 1)
                        dve.tensor_tensor(k.x[:, t, :], k.x[:, t, :], d[:, i, :], ALU.add).then_inc(added, 1)


def program(nc, ins, out, phases=99):
    with ExitStack() as stack:
        k = Core(nc, stack, ins, out)
        routing = Routing(k, "route", stack)
        tile_expert = k.sb("tile_expert", [P, TILES1], I32)
        logits = k.sb("logits", [P, NT, E])

        def scatter(layer, dispatch):
            return lambda st: Scatter(k, st, layer, h_rows1 if layer else h_rows0, routing, dispatch)

        def one(ap, b, rows):
            return (ap[b:b + 1, rows, :] if isinstance(b, int) else ap[bass.ds(b, 1), rows, :]
                    ).rearrange("a q d -> (a q) d")

        def h_rows0(b, i):
            return one(k.h_rows0.rearrange("(b s) d -> b s d", b=B), b, slice(i * P, (i + 1) * P))

        def h_rows1(b, i):
            return one(k.h_rows1.rearrange("(b s) d -> b s d", b=B), b, slice(i * P, (i + 1) * P))

        with ExitStack() as ctx_stack:
            ctx_t = k.sb("ctx_t", [P, B, KC, S], stack=ctx_stack)
            with ExitStack() as att_stack:
                att = Attention0(k, att_stack)
                start(k, att)
                if phases >= 1:
                    attention0(k, att, ctx_t)
            if phases >= 2:
                project_and_norm0(k, ctx_t, logits, h_rows0)
        if phases >= 2:
            route(k, "rt0", 0, logits, routing)
        if phases >= 3:
            experts0(k, routing, scatter(0, k.dispatch))
        with ExitStack() as weight_stack:
            weights = Experts1Weights(k, weight_stack)
            if phases >= 4:
                combine_and_attention1(k, routing, logits, h_rows1, weights)
            weights.place_gate_up(weight_stack)
            if phases >= 5:
                route(k, "rt1", 1, logits, routing, scatter(1, k.dispatch1), tile_expert, weights)
            if phases >= 6:
                experts1(k, weights, tile_expert)
        if phases >= 7:
            combine_to_output(k, routing)


def lay_out(inputs):
    import numpy as np

    g = {n: np.asarray(a) for n, a in inputs.items()}
    con = np.ascontiguousarray

    def chunks(w):
        return con(w.reshape(-1, P, w.shape[1]).transpose(1, 0, 2))

    lay = {"x": con(g["L0_attn_query"].reshape(T, D))}
    lay["c_t"] = con(np.stack([chunks(g["L0_c"].T), chunks(g["L1_c"].T)], 1))
    lay["wmod"] = con(np.stack([g["L0_wmod"], g["L1_wmod"]]).reshape(2, KC, P, 6, D)
                      .transpose(0, 3, 2, 1, 4).reshape(12, P, KC * D))
    w = g["L0_attn_Wqkv"].reshape(4, 4, 3, HN, D).transpose(2, 1, 0, 3, 4).reshape(3, D, D)
    lay["wqk"] = con(np.stack([chunks(w[0].T), chunks(w[1].T)], 1))
    lay["wv"] = chunks(w[2].T)
    lay["wproj"] = chunks(g["L0_attn_Wproj"].T)
    lay["bproj"] = con(g["L0_attn_bproj"].reshape(1, D))
    w1 = np.concatenate([g["L0_ffn_sw1"][None], g["L0_ffn_w1"]])
    lay["w1"] = con(w1.reshape(E + 1, KC, P, 4, 4, P).transpose(0, 3, 2, 4, 1, 5).reshape(E + 1, 4, P, 4 * KC * P))
    w2 = np.concatenate([g["L0_ffn_sw2"][None], g["L0_ffn_w2"]])
    lay["w2"] = con(w2.reshape(E + 1, 4, 4, P, D).transpose(0, 1, 3, 2, 4).reshape(E + 1, 4, P, 4 * D))
    wd = np.concatenate([g["L0_ffn_swd"][None], g["L0_ffn_wd"]])
    lay["wd"] = con(wd.reshape(E + 1, KC, P, RANK).transpose(2, 0, 1, 3).reshape(P, E + 1, KC * RANK))
    wu = np.concatenate([g["L0_ffn_swu"][None], g["L0_ffn_wu"]])
    b2 = np.concatenate([g["L0_ffn_sb2"][None], g["L0_ffn_b2"]])
    lay["wu_b2"] = con(np.concatenate([wu, b2[:, None, :]], 1))
    b1 = np.concatenate([g["L0_ffn_sb1"][None], g["L0_ffn_b1"]])
    lay["b1"] = con(b1.reshape(E + 1, FC, P).transpose(2, 0, 1).reshape(P, (E + 1) * FC))
    lay["wr"] = chunks(g["L1_ffn_Wr"])
    wgu = np.stack([g["L1_ffn_Wg"], g["L1_ffn_Wu"]], 2).reshape(E, KC, P, 2, INNER)
    lay["wgu"] = con(wgu.transpose(2, 0, 1, 3, 4).reshape(P, E * KC * 2, INNER))
    whole = INNER // P * P
    lay["wd1"] = con(g["L1_ffn_Wd"][:, :whole].reshape(E, INNER // P, P, D).transpose(2, 0, 1, 3)
                     .reshape(P, E * (INNER // P), D))
    lay["wd1_rest"] = con(g["L1_ffn_Wd"][:, whole:].transpose(1, 0, 2))
    lay["gate_w"] = chunks(g["L0_ffn_gate_w"])
    return lay


def kernel(**inputs):
    import concourse.bacc as bacc
    import numpy as np
    from concourse.bass_utils import run_bass_kernel_spmd

    nc = bacc.Bacc("TRN2", target_bir_lowering=False, num_devices=1)
    arrays = {f"in_{n}": a for n, a in lay_out(inputs).items()}
    ins = {n[3:]: nc.dram_tensor(n, a.shape, mybir.dt.from_np(a.dtype), kind="ExternalInput").ap()
           for n, a in arrays.items()}
    out = nc.dram_tensor("out_0", (B, S, D), F32, kind="ExternalOutput").ap()
    program(nc, ins, out)
    r = run_bass_kernel_spmd(nc, [arrays], core_ids=[0])
    return np.asarray(r.results[0]["out_0"])
```
